# Optimizing a Trainium2 kernel written in Bass

```python
import numpy as np
import jax
import jax.numpy as jnp

def _softmax(x, axis=-1):
    return jax.nn.softmax(x, axis=axis)

def _gelu(x):
    return jax.nn.gelu(x, approximate=True)

def _silu(x):
    return jax.nn.silu(x)

def _sigmoid(x):
    return jax.nn.sigmoid(x)

def _layernorm(x, axis=-1, eps=1e-05):
    m = jnp.mean(x, axis=axis, keepdims=True)
    v = jnp.var(x, axis=axis, keepdims=True)
    return (x - m) / jnp.sqrt(v + eps)

def _scatter_add(tgt, idx, src, axis=0):
    return tgt.at[idx].add(src)

def _segment_sum(src, seg, n):
    return jax.ops.segment_sum(src, seg, n)
kernel_name = 'mk_gnn_preln_d2_gnn_r16_c100aa'

def setup_inputs(seed: int=0):
    np.random.seed(seed)
    _w = jnp.asarray

    def _rec_inputs():
        import jax
        import jax.numpy as jnp
        _gk = jax.random.key(seed)
        x = -0.000202 + 1 * jax.random.normal(jax.random.fold_in(_gk, 1), (6250, 128), jnp.float32)
        src = jax.random.randint(jax.random.fold_in(_gk, 2), (200000,), 0, 6250, jnp.int32)
        dst = jax.random.randint(jax.random.fold_in(_gk, 3), (200000,), 0, 6250, jnp.int32)
        _o = jnp.argsort(dst, stable=True)
        src = src[_o]
        dst = dst[_o]
        return (x, src, dst)
    x, src, dst = _rec_inputs()

    def _L0_gnn_setup():
        import jax, jax.numpy as jnp
        import numpy as np
        N_NODES = 3125
        N_EDGES = 50000
        D_IN = 128
        D_OUT = 128
        key = jax.random.key(seed)
        ks = jax.random.split(key, 6)
        x = jax.random.normal(ks[0], (N_NODES, D_IN), dtype=jnp.float32)
        edge_index = jax.random.randint(ks[1], (2, N_EDGES), 0, N_NODES, dtype=jnp.int32)
        s1 = 1.0 / np.sqrt(2 * D_IN)
        s2 = 1.0 / np.sqrt(D_IN)
        W1 = jax.random.normal(ks[2], (2 * D_IN, D_IN), dtype=jnp.float32) * s1
        b1 = jnp.zeros((D_IN,), dtype=jnp.float32)
        W2 = jax.random.normal(ks[3], (D_IN, 1), dtype=jnp.float32) * s2
        b2 = jnp.zeros((1,), dtype=jnp.float32)
        Wl = jax.random.normal(ks[4], (D_IN, D_OUT), dtype=jnp.float32) * s2
        bl = jnp.zeros((D_OUT,), dtype=jnp.float32)
        return {'x': x, 'edge_index': edge_index, 'W1': W1, 'b1': b1, 'W2': W2, 'b2': b2, 'Wl': Wl, 'bl': bl}
    _L0_gnn_all = _L0_gnn_setup()
    _L0_gnn_in = {k: v for k, v in _L0_gnn_all.items() if k in ('W1', 'b1', 'W2', 'b2', 'Wl', 'bl')}
    del _L0_gnn_all

    def _L1_gnn_setup():
        import jax, jax.numpy as jnp
        import numpy as np
        N_NODES = 3125
        N_EDGES = 37500
        D_IN = 128
        D_HID = 128
        NUM_LAYERS = 4

        def _graph_conv(x, src, dst, W, b, R, num_nodes):
            agg = jax.ops.segment_max(x[src], dst, num_segments=num_nodes)
            agg = jnp.where(jnp.isneginf(agg), 0.0, agg)
            return agg @ W + b + x @ R
        key = jax.random.key(seed)
        ks = jax.random.split(key, 8)
        x = jax.random.normal(ks[0], (N_NODES, D_IN), dtype=jnp.float32)
        edge_index = jax.random.randint(ks[1], (2, N_EDGES), 0, N_NODES, dtype=jnp.int32)
        s = 0.05
        W1 = jax.random.normal(ks[2], (D_IN, D_HID), dtype=jnp.float32) * s
        b1 = jnp.zeros((D_HID,), dtype=jnp.float32)
        R1 = jax.random.normal(ks[3], (D_IN, D_HID), dtype=jnp.float32) * s
        W2 = jax.random.normal(ks[4], (D_HID, D_HID), dtype=jnp.float32) * s
        b2 = jnp.zeros((D_HID,), dtype=jnp.float32)
        R2 = jax.random.normal(ks[5], (D_HID, D_HID), dtype=jnp.float32) * s
        return {'x': x, 'edge_index': edge_index, 'W1': W1, 'b1': b1, 'R1': R1, 'W2': W2, 'b2': b2, 'R2': R2}
    _L1_gnn_all = _L1_gnn_setup()
    _L1_gnn_in = {k: v for k, v in _L1_gnn_all.items() if k in ('W1', 'b1', 'R1', 'W2', 'b2', 'R2')}
    del _L1_gnn_all
    return {'x': x, 'src': src, 'dst': dst, 'L0_gnn_W1': _L0_gnn_in['W1'], 'L0_gnn_b1': _L0_gnn_in['b1'], 'L0_gnn_W2': _L0_gnn_in['W2'], 'L0_gnn_b2': _L0_gnn_in['b2'], 'L0_gnn_Wl': _L0_gnn_in['Wl'], 'L0_gnn_bl': _L0_gnn_in['bl'], 'L1_gnn_W1': _L1_gnn_in['W1'], 'L1_gnn_b1': _L1_gnn_in['b1'], 'L1_gnn_R1': _L1_gnn_in['R1'], 'L1_gnn_W2': _L1_gnn_in['W2'], 'L1_gnn_b2': _L1_gnn_in['b2'], 'L1_gnn_R2': _L1_gnn_in['R2']}

def reference(x, src, dst, L0_gnn_W1, L0_gnn_b1, L0_gnn_W2, L0_gnn_b2, L0_gnn_Wl, L0_gnn_bl, L1_gnn_W1, L1_gnn_b1, L1_gnn_R1, L1_gnn_W2, L1_gnn_b2, L1_gnn_R2):
    import jax
    import jax.numpy as jnp

    def _L0_gnn_ref(x, edge_index, W1, b1, W2, b2, Wl, bl):
        import jax, jax.numpy as jnp
        import numpy as np
        N_NODES = 3125
        N_EDGES = 50000
        D_IN = 128
        D_OUT = 128
        row, col = (edge_index[0], edge_index[1])
        n, d = x.shape
        xc = x[row]
        xn = x[col]
        h = jax.nn.relu(xc @ W1[:d] + xn @ W1[d:] + b1)
        mask = jax.nn.sigmoid(h @ W2 + b2)[:, 0]
        seg_sum = jax.ops.segment_sum(mask, row, num_segments=n)
        w = mask / (seg_sum[row] + 1e-09)
        agg = jax.ops.segment_sum(w[:, None] * xn, row, num_segments=n)
        deg = jax.ops.segment_sum(jnp.ones_like(mask), row, num_segments=n)
        out_emb = jnp.where((deg > 0)[:, None], 0.5 * x + 0.5 * agg, x)
        return jax.nn.relu(out_emb @ Wl + bl)

    def _L1_gnn_ref(x, edge_index, W1, b1, R1, W2, b2, R2):
        import jax, jax.numpy as jnp
        import numpy as np
        N_NODES = 3125
        N_EDGES = 37500
        D_IN = 128
        D_HID = 128
        NUM_LAYERS = 4

        def _graph_conv(x, src, dst, W, b, R, num_nodes):
            agg = jax.ops.segment_max(x[src], dst, num_segments=num_nodes)
            agg = jnp.where(jnp.isneginf(agg), 0.0, agg)
            return agg @ W + b + x @ R
        src, dst = (edge_index[0], edge_index[1])
        n = x.shape[0]
        h = jax.nn.relu(_graph_conv(x, src, dst, W1, b1, R1, n))
        for _ in range(NUM_LAYERS - 1):
            h = jax.nn.relu(_graph_conv(h, src, dst, W2, b2, R2, n))
        return h
    edge_index = jnp.stack([src, dst])
    h = jnp.maximum(_layernorm(x, axis=-1), 0.0)
    x = x + _L0_gnn_ref(h, edge_index, L0_gnn_W1, L0_gnn_b1, L0_gnn_W2, L0_gnn_b2, L0_gnn_Wl, L0_gnn_bl)
    h = jnp.maximum(_layernorm(x, axis=-1), 0.0)
    x = x + _L1_gnn_ref(h, edge_index, L1_gnn_W1, L1_gnn_b1, L1_gnn_R1, L1_gnn_W2, L1_gnn_b2, L1_gnn_R2)
    return x

_drawn_inputs = setup_inputs


def setup_inputs(seed=0):
    import zlib

    import numpy as np

    out = dict(_drawn_inputs(seed))
    spreads = {'L0_gnn_b1': (0.0, 0.8),
     'L0_gnn_bl': (0.0, 0.1),
     'L1_gnn_b1': (0.0, 0.571),
     'L1_gnn_b2': (0.0, 0.1)}
    factors = {'L0_gnn_W1': 8.0, 'L0_gnn_W2': 8.0}
    for name, (base, spread) in spreads.items():
        noise = np.random.default_rng([zlib.crc32(name.encode()), seed]).standard_normal(out[name].shape)
        drawn = base * np.exp(spread * noise) if base else spread * noise
        out[name] = jnp.asarray(drawn.astype(out[name].dtype))
    for name, factor in factors.items():
        out[name] = (out[name] * factor).astype(out[name].dtype)
    return out
```

```python
import numpy as np
from contextlib import ExitStack
import concourse.bass as bass
from concourse import mybir
from concourse.alu_op_type import AluOpType as ALU

F32 = mybir.dt.float32
BF16 = mybir.dt.bfloat16
I32 = mybir.dt.int32
ACT = mybir.ActivationFunctionType
AX = mybir.AxisListType

P = 128
NODES = 6250
EDGES = 200000
D = 128
TILES = -(-NODES // P)
NODES_PAD = TILES * P
LAST_ROWS = NODES - (TILES - 1) * P
PAD_NODE = NODES_PAD - 1
SUB = 8
CHUNKS = 2 * SUB * -(-EDGES // (P * 2 * SUB))
EDGES_PAD = P * CHUNKS
SUBS = CHUNKS // SUB
FULL_PARTS = EDGES // CHUNKS
REST = EDGES - FULL_PARTS * CHUNKS
assert FULL_PARTS == P - 1 and REST > 0 and PAD_NODE >= NODES
GROUP = 4
BODY = 16
GROUPS = BODY // GROUP
BLOCK = 64
LTILES = TILES + 1
SLOTS_MAX = EDGES + GROUP + EDGES // P + (GROUP + 1) * TILES + 2 * BLOCK
ZERO_ROW = NODES_PAD
TABLE_ROWS = NODES_PAD + P
W0 = 2 * D + 4
A0 = D + 4
DEG_CAP = 1023
KEY_STEP = 8192
HEAD, TAIL = 4, 3
PASS = HEAD + TAIL
PASSES = TILES // PASS
assert PASSES * PASS == TILES


class Count:

    def __init__(self, eng, sem):
        self.eng, self.sem, self.base, self.n = eng, sem, 0, 0

    def did(self, instruction):
        instruction.then_inc(self.sem, 1)
        self.n += 1

    def wait(self):
        self.eng.wait_ge(self.sem, self.base + self.n)

    def enter(self, i, per_pass):
        self.before = self.base + self.n
        self.base, self.n, self.per_pass = self.before + i * per_pass, 0, per_pass

    def leave(self, passes):
        assert self.n == self.per_pass, (self.n, self.per_pass)
        self.base, self.n = self.before + passes * self.per_pass, 0


def turn(eng, turns):
    eng.sem_inc(turns, 1)


def bc(ap, shape):
    return ap.to_broadcast(shape)


def gnn(nc, x_in, src_in, dst_in, w1_in, b1_in, w2_in, b2_in, wl_in, bl_in,
        gw1_in, gb1_in, gr1_in, gw2_in, gb2_in, gr2_in, out):
    def dram(name, shape, dt=F32):
        return nc.dram_tensor(name, shape, dt).ap()

    table0 = dram("table0", [TABLE_ROWS, W0])
    own0 = dram("own0", [NODES_PAD, 3 * D])
    table1 = dram("table1", [TABLE_ROWS, D])
    own1 = dram("own1", [NODES_PAD, D])
    nbrs = [dram(f"nbrs{k}", [EDGES_PAD, 1], I32) for k in range(2)]
    meta = [dram(f"meta{k}", [NODES_PAD, 4], I32) for k in range(2)]
    slots = [dram(f"slots{k}", [P, SLOTS_MAX], I32) for k in range(2)]
    slot_tile = [dram(f"slot_tile{k}", [1, SLOTS_MAX // GROUP], I32) for k in range(2)]

    with ExitStack() as whole:
        def tensors(ctx, tag=""):
            def sb(name, shape, dt=F32):
                return ctx.enter_context(nc.sbuf_tensor(name + tag, shape, dt))

            def ps(name, shape, dt=F32):
                return ctx.enter_context(nc.psum_tensor(name + tag, shape, dt))

            def sem(name):
                return ctx.enter_context(nc.semaphore(name + tag))
            return sb, ps, sem

        sb, ps, sem = tensors(whole)
        turns = sem("turns")
        iota_col = sb("iota_col", [P, 1])
        iota_row = sb("iota_row", [P, P])
        ident = sb("ident", [P, P])
        ident_b = sb("ident_b", [P, P], BF16)
        below = sb("below", [P, P])
        above = sb("above", [P, P])
        ones = sb("ones", [P, P])
        tile_ids = sb("tile_ids", [1, LTILES, BLOCK // GROUP], I32)
        degree = [sb(f"degree{k}", [P, TILES]) for k in range(2)]
        start = [sb(f"start{k}", [P, TILES]) for k in range(2)]
        row_info = [sb(f"row_info{k}", [P, LTILES, 4], I32) for k in range(2)]
        tile_info = [sb(f"tile_info{k}", [1, 4 * LTILES + 4], I32) for k in range(2)]
        G_OFF, N_BLOCKS, B_OFF, BODIES = 0, LTILES, 2 * LTILES, 3 * LTILES

        keys = ExitStack()
        ksb, _, _ = tensors(keys)
        ends_i = [ksb(f"ends_i{k}", [P, CHUNKS + SUB], I32) for k in range(2)]
        lo = [ksb(f"lo{k}", [P, CHUNKS + SUB]) for k in range(2)]
        hi = [ksb(f"hi{k}", [P, CHUNKS + SUB]) for k in range(2)]
        lo_b = [ksb(f"lo_b{k}", [P, CHUNKS + SUB], BF16) for k in range(2)]
        hi_b = [ksb(f"hi_b{k}", [P, CHUNKS + SUB], BF16) for k in range(2)]

        with ExitStack() as ctx:
            sb, ps, sem = tensors(ctx)
            iota_i = sb("iota_i", [P, P], I32)
            iota_ci = sb("iota_ci", [P, 1], I32)
            digit_i = sb("digit_i", [P, CHUNKS + SUB], I32)
            zeros_b = sb("zeros_b", [P, P], BF16)
            one_lo = [[sb(f"h_lo{k}{p}", [P, SUB, P], BF16) for p in range(2)] for k in range(2)]
            one_hi = [[sb(f"h_hi{k}{p}", [P, SUB, TILES], BF16) for p in range(2)] for k in range(2)]
            total = [sb(f"total{k}", [P, TILES]) for k in range(2)]
            upto = [sb(f"upto{k}", [P, TILES]) for k in range(2)]
            hist = [ps(f"hist{k}", [P, TILES]) for k in range(2)]
            within = [ps(f"within{k}", [P, TILES]) for k in range(2)]
            totals = [ps(f"totals{k}", [P, TILES]) for k in range(2)]
            pads_set = sem("pads_set")
            iota_made = sem("iota_made")
            ends_loaded = [sem(f"ends_loaded{k}") for k in range(2)]
            nbrs_copied = sem("nbrs_copied")
            v_did = sem("h_v_did")
            digits_made = sem("digits_made")
            ones_made = [sem(f"h_ones_made{k}") for k in range(2)]
            hist_did = [sem(f"hist_did{k}") for k in range(2)]
            hist_out = sem("hist_out")
            prefix_did = sem("prefix_did")
            block = ctx.enter_context(nc.Block())

            @block.sync
            def _(sp):
                sp.wait_ge(pads_set, 2)
                for k, ends in enumerate((src_in, dst_in)):
                    sp.dma_start(ends_i[k][0:FULL_PARTS, 0:CHUNKS],
                                 ends[0:FULL_PARTS * CHUNKS].rearrange("(p c) -> p c", c=CHUNKS)
                                 ).then_inc(ends_loaded[k], 16)
                    sp.dma_start(ends_i[k][FULL_PARTS:P, 0:REST],
                                 ends[FULL_PARTS * CHUNKS:EDGES].rearrange("(p c) -> p c", p=1)
                                 ).then_inc(ends_loaded[k], 16)
                sp.wait_ge(ends_loaded[0], 32)
                sp.dma_start(nbrs[1].rearrange("(p c) o -> p (c o)", p=P),
                             ends_i[0][:, 0:CHUNKS]).then_inc(nbrs_copied, 16)
                sp.wait_ge(nbrs_copied, 16)

            @block.gpsimd
            def _(pool):
                pool.iota(iota_i[:, :], [[1, P]], base=0, channel_multiplier=0).then_inc(iota_made, 1)
                pool.iota(iota_ci[:, :], [[1, 1]], base=0, channel_multiplier=1).then_inc(iota_made, 1)
                pool.iota(tile_ids[:, :, :], [[1, LTILES], [0, BLOCK // GROUP]], base=0,
                          channel_multiplier=0).then_inc(iota_made, 1)

            @block.vector
            def _(dve):
                own = Count(dve, v_did)
                for k in range(2):
                    dve.memset(ends_i[k][:, :], PAD_NODE).then_inc(pads_set, 1)
                dve.wait_ge(iota_made, 3)
                own.did(dve.tensor_copy(iota_row[:, :], iota_i[:, :]))
                own.did(dve.tensor_copy(iota_col[:, :], iota_ci[:, :]))
                own.did(dve.memset(ones[:, :], 1.0))
                own.did(dve.memset(zeros_b[:, :], 0.0))
                own.wait()
                own.did(dve.tensor_scalar(ident[:, :], iota_row[:, :], iota_col[:, :], None, ALU.is_equal))
                own.did(dve.tensor_scalar(ident_b[:, :], iota_row[:, :], iota_col[:, :], None, ALU.is_equal))
                own.did(dve.tensor_scalar(below[:, :], iota_row[:, :], iota_col[:, :], None, ALU.is_lt))
                own.did(dve.tensor_scalar(above[:, :], iota_row[:, :], iota_col[:, :], None, ALU.is_gt))
                for k in range(2):
                    dve.wait_ge(ends_loaded[k], 32)
                    own.wait()
                    own.did(dve.tensor_scalar(digit_i[:, :], ends_i[k][:, :], P - 1, None, ALU.bitwise_and))
                    own.wait()
                    own.did(dve.tensor_copy(lo[k][:, :], digit_i[:, :]))
                    own.did(dve.tensor_copy(lo_b[k][:, :], digit_i[:, :]))
                    own.wait()
                    own.did(dve.tensor_scalar(digit_i[:, :], ends_i[k][:, :], 7, None,
                                              ALU.arith_shift_right))
                    own.wait()
                    own.did(dve.tensor_copy(hi[k][:, :], digit_i[:, :]))
                    own.did(dve.tensor_scalar(hi_b[k][:, :], digit_i[:, :], float(P), None, ALU.mult))
                own.wait()
                dve.sem_inc(digits_made, 1)
                with dve.Fori(0, SUBS // 2) as i:
                    for p in range(2):
                        for k in range(2):
                            dve.wait_ge(hist_did[k], i * 2 + p + 1)
                            dve.tensor_tensor(
                                one_lo[k][p][:, :, :],
                                bc(lo[k][:, bass.ds((i * 2 + p) * SUB, SUB)].unsqueeze(2), [P, SUB, P]),
                                bc(iota_row[:, :].unsqueeze(1), [P, SUB, P]), ALU.is_equal)
                            dve.tensor_tensor(
                                one_hi[k][p][:, :, :],
                                bc(hi[k][:, bass.ds((i * 2 + p) * SUB, SUB)].unsqueeze(2), [P, SUB, TILES]),
                                bc(iota_row[:, 0:TILES].unsqueeze(1), [P, SUB, TILES]),
                                ALU.is_equal).then_inc(ones_made[k], 1)
                for k in range(2):
                    dve.wait_ge(hist_did[k], SUBS + 3)
                    own.did(dve.tensor_copy(degree[k][:, :], hist[k][:, :]))
                    own.wait()
                    dve.sem_inc(hist_out, 1)
                    dve.wait_ge(prefix_did, 2 * k + 2)
                    own.did(dve.tensor_copy(total[k][:, :], totals[k][:, :]))
                    own.wait()
                    own.did(dve.tensor_tensor_scan(upto[k][:, :], bc(ones[:, 0:1], [P, TILES]), total[k][:, :],
                                                   0.0, ALU.mult, ALU.add))
                    own.wait()
                    own.did(dve.tensor_tensor(upto[k][:, :], upto[k][:, :], total[k][:, :], ALU.subtract))
                    own.wait()
                    own.did(dve.tensor_tensor(start[k][:, :], upto[k][:, :], within[k][:, :], ALU.add))
                own.wait()

            @block.tensor
            def _(pe):
                pe.wait_ge(digits_made, 1)
                for k in range(2):
                    pe.matmul(hist[k][:, :], zeros_b[:, :], zeros_b[:, 0:TILES], start=True,
                              stop=False).then_inc(hist_did[k], 1)
                    pe.matmul(hist[k][:, :], zeros_b[:, :], zeros_b[:, 0:TILES], start=False,
                              stop=False).then_inc(hist_did[k], 1)
                with pe.Fori(0, SUBS // 2) as i:
                    for p in range(2):
                        for k in range(2):
                            pe.wait_ge(ones_made[k], i * 2 + p + 1)
                            for c in range(SUB):
                                last = pe.matmul(hist[k][:, :], one_lo[k][p][:, c, :], one_hi[k][p][:, c, :],
                                                 start=False, stop=False)
                            last.then_inc(hist_did[k], 1)
                for k in range(2):
                    pe.matmul(hist[k][:, :], zeros_b[:, :], zeros_b[:, 0:TILES], start=False,
                              stop=True).then_inc(hist_did[k], 1)
                for k in range(2):
                    pe.wait_ge(hist_out, k + 1)
                    pe.matmul(within[k][:, :], above[:, :], degree[k][:, :], start=True,
                              stop=True).then_inc(prefix_did, 1)
                    pe.matmul(totals[k][:, :], ones[:, :], degree[k][:, :], start=True,
                              stop=True).then_inc(prefix_did, 1)

        def sort(k):
            with ExitStack() as ctx:
                sb, ps, sem = tensors(ctx, f"_{k}")
                one_lo = [sb(f"s_lo{p}", [P, SUB, P], BF16) for p in range(2)]
                one_hi = [sb(f"s_hi{p}", [P, SUB, TILES], BF16) for p in range(2)]
                one_lo_t = [sb(f"s_lo_t{p}", [P, SUB, P]) for p in range(2)]
                equal = sb("s_equal", [P, SUB, P], BF16)
                before = [sb(f"s_before{p}", [P, SUB]) for p in range(2)]
                next_sb = [sb(f"s_next{c}", [P, TILES]) for c in range(SUB)]
                picked = sb("s_picked", [P, SUB, TILES])
                base = sb("s_base", [P, SUB])
                place = [sb(f"s_place{p}", [P, SUB], I32) for p in range(2)]
                other = [sb(f"s_other{p}", [P, SUB], I32) for p in range(2)]
                key_row = ps("s_key_row", [P, SUB, P])
                lo_row = ps("s_lo_row", [P, SUB, P])
                next_free = ps("s_next_free", [P, TILES])
                looked = [ps(f"s_looked{p}", [P, SUB, TILES]) for p in range(2)]
                v_did = sem("s_v_did")
                rows_made = sem("s_rows_made")
                rows_used = sem("s_rows_used")
                ones_made = sem("s_ones_made")
                next_updated = sem("s_next_updated")
                next_copied = sem("s_next_copied")
                looked_up = sem("s_looked_up")
                looked_free = sem("s_looked_free")
                place_made = sem("s_place_made")
                scattered = [sem(f"s_scattered{p}") for p in range(2)]
                block = ctx.enter_context(nc.Block())

                @block.tensor
                def _(pe):
                    def rows(b):
                        for c in range(SUB):
                            col = bass.ds(b * SUB + c, 1)
                            lo_of, hi_of = bc(lo_b[k][:, col], [P, P]), bc(hi_b[k][:, col], [P, P])
                            pe.matmul(lo_row[:, c, :], lo_of, ident_b[:, :], start=True, stop=True)
                            pe.matmul(key_row[:, c, :], lo_of, ident_b[:, :], start=True, stop=False)
                            last = pe.matmul(key_row[:, c, :], hi_of, ident_b[:, :], start=False, stop=True)
                        last.then_inc(rows_made, 1)

                    pe.matmul(next_free[:, :], ident[:, :], start[k][:, :], start=True,
                              stop=True).then_inc(next_updated, 1)
                    rows(0)
                    with pe.Fori(0, SUBS // 2) as i:
                        for p in range(2):
                            b = i * 2 + p
                            pe.wait_ge(rows_used, b + 1)
                            rows(b + 1)
                            pe.wait_ge(ones_made, b + 1)
                            pe.wait_ge(looked_free, b + 1)
                            for c in range(SUB):
                                pe.wait_ge(next_copied, b * SUB + c + 1)
                                last = pe.matmul(looked[p][:, c, :], one_lo_t[p][:, c, :], next_sb[c][:, :],
                                                 start=True, stop=True)
                                if c == SUB - 1:
                                    last.then_inc(looked_up, 1)
                                pe.matmul(next_free[:, :], one_lo[p][:, c, :], one_hi[p][:, c, :],
                                          start=False, stop=True, skip_group_check=True).then_inc(next_updated, 1)

                @block.scalar
                def _(act):
                    with act.Fori(0, SUBS) as b:
                        for c in range(SUB):
                            act.wait_ge(next_updated, b * SUB + c + 1)
                            act.copy(next_sb[c][:, :], next_free[:, :]).then_inc(next_copied, 1)

                @block.vector
                def _(dve):
                    own = Count(dve, v_did)

                    def build(b, p):
                        col = bass.ds(b * SUB, SUB)
                        dve.tensor_tensor(one_lo[p][:, :, :], bc(lo[k][:, col].unsqueeze(2), [P, SUB, P]),
                                          bc(iota_row[:, :].unsqueeze(1), [P, SUB, P]), ALU.is_equal)
                        dve.tensor_tensor(one_hi[p][:, :, :], bc(hi[k][:, col].unsqueeze(2), [P, SUB, TILES]),
                                          bc(iota_row[:, 0:TILES].unsqueeze(1), [P, SUB, TILES]), ALU.is_equal)
                        dve.wait_ge(rows_made, b + 1)
                        dve.tensor_scalar(one_lo_t[p][:, :, :], lo_row[:, :, :], iota_col[:, :], None,
                                          ALU.is_equal).then_inc(ones_made, 1)
                        for c in range(SUB):
                            last = dve.scalar_tensor_tensor(
                                equal[:, c, :], key_row[:, c, :], key_f[:, bass.ds(b * SUB + c, 1)], below[:, :],
                                ALU.is_equal, ALU.mult, accum_out=before[p][:, c:c + 1])
                        last.then_inc(rows_used, 1)

                    def finish(b, i, p):
                        dve.wait_ge(looked_up, b + 1)
                        own.wait()
                        own.did(dve.tensor_tensor(picked[:, :, :], looked[p][:, :, :], one_hi[p][:, :, :],
                                                  ALU.mult))
                        own.wait()
                        dve.sem_inc(looked_free, 1)
                        own.did(dve.tensor_reduce(base[:, :], picked[:, :, :], AX.X, ALU.add))
                        own.wait()
                        dve.wait_ge(scattered[p], i * (SUB * 16))
                        dve.wait_ge(rows_used, b + 1)
                        own.did(dve.tensor_tensor(place[p][:, :], base[:, :], before[p][:, :], ALU.add))
                        own.did(dve.tensor_copy(other[p][:, :], ends_i[1 - k][:, bass.ds(b * SUB, SUB)]))
                        own.wait()
                        dve.sem_inc(place_made, 1)

                    key_f = sb_key
                    own.did(dve.scalar_tensor_tensor(key_f[:, :], hi[k][:, :], float(P), lo[k][:, :],
                                                     ALU.mult, ALU.add))
                    own.wait()
                    dve.sem_inc(looked_free, 2)
                    build(0, 0)
                    with dve.Fori(0, SUBS // 2) as i:
                        own.enter(i, 8)
                        for p in range(2):
                            b = i * 2 + p
                            dve.wait_ge(next_updated, b * SUB + 1)
                            build(b + 1, 1 - p)
                            finish(b, i, p)
                        own.leave(SUBS // 2)

                @block.gpsimd
                def _(pool):
                    with pool.Fori(0, SUBS // 2) as i:
                        for p in range(2):
                            pool.wait_ge(place_made, i * 2 + p + 1)
                            turn(pool, turns)
                            for c in range(SUB):
                                pool.indirect_dma_start(
                                    nbrs[k], bass.IndirectOffsetOnAxis(place[p][:, c:c + 1], 0),
                                    other[p][:, c:c + 1], None).then_inc(scattered[p], 16)
                    for p in range(2):
                        pool.wait_ge(scattered[p], SUBS // 2 * SUB * 16)

        sb_key = ksb("s_key_f", [P, CHUNKS + SUB])
        sort(0)
        keys.close()

        def rstd_steps(dve, own, stats, mean, spread, rstd):
            own.wait()
            own.did(dve.tensor_tensor(mean[:, :], stats[:, :, 1], stats[:, :, 4], ALU.add))
            own.did(dve.tensor_tensor(spread[:, :], stats[:, :, 1], stats[:, :, 4], ALU.subtract))
            own.did(dve.tensor_tensor(rstd[:, :], stats[:, :, 2], stats[:, :, 5], ALU.add))
            own.wait()
            own.did(dve.tensor_scalar(mean[:, :], mean[:, :], 0.5, None, ALU.mult))
            own.did(dve.tensor_tensor(spread[:, :], spread[:, :], spread[:, :], ALU.mult))
            own.did(dve.tensor_scalar(rstd[:, :], rstd[:, :], 1.0 / D, 1e-5, ALU.mult, ALU.add))
            own.wait()
            own.did(dve.scalar_tensor_tensor(rstd[:, :], spread[:, :], 0.25, rstd[:, :], ALU.mult, ALU.add))
            own.wait()

        def halves(t):
            return ((0, t, HEAD), (1, t + HEAD, TAIL))

        with ExitStack() as ctx:
            sb, ps, sem = tensors(ctx)
            x = sb("f_x", [P, TILES, D])
            h = sb("f_h", [P, TILES, D])
            ab = sb("f_ab", [P, TILES, 2 * D])
            w1 = sb("f_w1", [P, 2 * D])
            b1 = sb("f_b1", [1, 2 * D])
            stats = sb("f_stats", [P, TILES, 6])
            mean = sb("f_mean", [P, TILES])
            spread = sb("f_spread", [P, TILES])
            rstd = sb("f_rstd", [P, TILES])
            one_cols = sb("f_one_cols", [P, TILES, W0 - 2 * D])
            zero_rows = sb("f_zero_rows", [P, W0])
            h_stage = [sb(f"f_h_stage{q}", [P, HEAD, D]) for q in range(2)]
            h_t = [sb(f"f_h_t{q}", [P, HEAD, D]) for q in range(2)]
            turned = [ps(f"f_turned{q}", [P, HEAD, D]) for q in range(2)]
            product = [ps(f"f_product{q}", [P, HEAD, 2 * D]) for q in range(2)]
            x_clear = sem("f_x_clear")
            x_loaded = sem("f_x_loaded")
            w_loaded = sem("f_w_loaded")
            v_did = sem("f_v_did")
            var_made = sem("f_var_made")
            std_made = sem("f_std_made")
            centred = sem("f_centred")
            h_made = sem("f_h_made")
            h_staged = [sem(f"f_h_staged{q}") for q in range(2)]
            h_turned = [sem(f"f_h_turned{q}") for q in range(2)]
            h_copied = [sem(f"f_h_copied{q}") for q in range(2)]
            ab_made = [sem(f"f_ab_made{q}") for q in range(2)]
            ab_copied = [sem(f"f_ab_copied{q}") for q in range(2)]
            pads_made = sem("f_pads_made")
            stored = sem("f_stored")
            block = ctx.enter_context(nc.Block())

            def by_node(ap):
                return ap[0:NODES_PAD, :].rearrange("(t p) f -> p t f", p=P)

            @block.sync
            def _(sp):
                sp.dma_start(w1[:, 0:D], w1_in[0:D, :]).then_inc(w_loaded, 16)
                sp.dma_start(w1[:, D:2 * D], w1_in[D:2 * D, :]).then_inc(w_loaded, 16)
                sp.dma_start(x[:, 0:TILES - 1, :],
                             x_in[0:(TILES - 1) * P, :].rearrange("(t p) f -> p t f", p=P)
                             ).then_inc(x_loaded, 16)
                sp.wait_ge(x_clear, 2)
                sp.dma_start(x[0:LAST_ROWS, TILES - 1, :], x_in[(TILES - 1) * P:NODES, :]).then_inc(x_loaded, 16)
                sp.dma_start(b1[0:1, 0:D], b1_in.rearrange("(o n) -> o n", o=1)).then_inc(w_loaded, 16)
                sp.wait_ge(x_loaded, 32)
                sp.dma_start(by_node(own0)[:, :, 2 * D:3 * D], x[:, :, :]).then_inc(stored, 16)
                sp.wait_ge(pads_made, 2)
                sp.dma_start(by_node(table0)[:, :, 2 * D:W0], one_cols[:, :, :]).then_inc(stored, 16)
                sp.dma_start(table0[NODES_PAD:TABLE_ROWS, :], zero_rows[:, :]).then_inc(stored, 16)
                sp.dma_start(table1[NODES_PAD:TABLE_ROWS, :], zero_rows[:, 0:D]).then_inc(stored, 16)
                sp.wait_ge(h_made, 1)
                sp.dma_start(by_node(own0)[:, :, D:2 * D], h[:, :, :]).then_inc(stored, 16)
                sp.dma_start(by_node(table0)[:, :, D:2 * D], h[:, :, :]).then_inc(stored, 16)
                for q in range(2):
                    sp.wait_ge(ab_copied[q], PASSES)
                sp.dma_start(by_node(own0)[:, :, 0:D], ab[:, :, 0:D]).then_inc(stored, 16)
                sp.dma_start(by_node(table0)[:, :, 0:D], ab[:, :, D:2 * D]).then_inc(stored, 16)
                sp.wait_ge(stored, 8 * 16)

            @block.scalar
            def _(act):
                act.wait_ge(var_made, 1)
                act.sqrt(rstd[:, :], rstd[:, :]).then_inc(std_made, 1)
                act.wait_ge(centred, 1)
                act.activation(h[:, :, :], h[:, :, :], ACT.Relu).then_inc(h_made, 1)
                with act.Fori(0, PASSES) as i:
                    for q, _, n in halves(0):
                        act.wait_ge(h_turned[q], i + 1)
                        act.wait_ge(ab_made[q], i)
                        act.copy(h_t[q][:, 0:n, :], turned[q][:, 0:n, :]).then_inc(h_copied[q], 1)

            @block.gpsimd
            def _(pool):
                pool.wait_ge(h_made, 1)
                with pool.Fori(0, PASSES) as i:
                    for q, t, n in halves(i * PASS):
                        pool.wait_ge(h_turned[q], i)
                        pool.tensor_copy(h_stage[q][:, 0:n, :], h[:, bass.ds(t, n), :]).then_inc(h_staged[q], 1)

            @block.tensor
            def _(pe):
                pe.wait_ge(w_loaded, 48)
                with pe.Fori(0, PASSES) as i:
                    for q, t, n in halves(i * PASS):
                        pe.wait_ge(h_staged[q], i + 1)
                        pe.wait_ge(h_copied[q], i)
                        for c in range(n):
                            last = pe.transpose(turned[q][:, c, :], h_stage[q][:, c, :], ident[:, :])
                        last.then_inc(h_turned[q], 1)
                    for q, t, n in halves(i * PASS):
                        pe.wait_ge(h_copied[q], i + 1)
                        pe.wait_ge(ab_copied[q], i)
                        for c in range(n):
                            pe.matmul(product[q][:, c, :], h_t[q][:, c, :], w1[:, :], start=True, stop=False)
                            last = pe.matmul(product[q][:, c, :], ones[0:1, :], b1[0:1, :], start=False,
                                             stop=True)
                        last.then_inc(ab_made[q], 1)

            @block.vector
            def _(dve):
                own = Count(dve, v_did)
                dve.memset(x[:, TILES - 1, :], 0.0).then_inc(x_clear, 1)
                dve.memset(b1[:, :], 0.0).then_inc(x_clear, 1)
                own.did(dve.memset(one_cols[:, :, :], 0.0))
                own.wait()
                dve.memset(one_cols[:, :, 0:1], 1.0).then_inc(pads_made, 1)
                dve.memset(zero_rows[:, :], 0.0).then_inc(pads_made, 1)
                dve.wait_ge(x_loaded, 32)
                with dve.Fori(0, TILES) as t:
                    own.enter(t, 1)
                    own.did(dve.bn_stats(stats[:, bass.ds(t, 1), :].squeeze(1), x[:, bass.ds(t, 1), :].squeeze(1)))
                    own.leave(TILES)
                rstd_steps(dve, own, stats, mean, spread, rstd)
                dve.sem_inc(var_made, 1)
                dve.wait_ge(std_made, 1)
                own.did(dve.reciprocal(rstd[:, :], rstd[:, :]))
                own.did(dve.tensor_tensor(h[:, :, :], x[:, :, :], bc(mean[:, :].unsqueeze(2), [P, TILES, D]),
                                          ALU.subtract))
                own.wait()
                dve.tensor_tensor(h[:, :, :], h[:, :, :], bc(rstd[:, :].unsqueeze(2), [P, TILES, D]),
                                  ALU.mult).then_inc(centred, 1)
                with dve.Fori(0, PASSES) as i:
                    for q, t, n in halves(i * PASS):
                        dve.wait_ge(ab_made[q], i + 1)
                        dve.tensor_copy(ab[:, bass.ds(t, n), :], product[q][:, 0:n, :]).then_inc(ab_copied[q], 1)

        with ExitStack() as ctx:
            sb, ps, sem = tensors(ctx)
            node_i = sb("r_node_i", [P, TILES], I32)
            node = sb("r_node", [P, TILES])
            real = sb("r_real", [P, TILES])
            key = [sb(f"r_key{k}", [P, TILES]) for k in range(2)]
            minus_key = sb("r_minus_key", [P, TILES])
            key_row = [sb(f"r_key_row{k}", [P, NODES_PAD]) for k in range(2)]
            compared = [sb(f"r_compared{k}", [P, NODES_PAD], BF16) for k in range(2)]
            higher = [sb(f"r_higher{k}", [P, TILES]) for k in range(2)]
            rank = [sb(f"r_rank{k}", [P, TILES], I32) for k in range(2)]
            record = [sb(f"r_record{k}", [P, TILES, 4], I32) for k in range(2)]
            key_stage = [sb(f"r_key_stage{q}", [P, HEAD]) for q in range(2)]
            spread_out = [ps(f"r_spread_out{q}", [P, HEAD, P]) for q in range(2)]
            keys_staged = [sem(f"r_keys_staged{q}") for q in range(2)]
            node_made = sem("r_node_made")
            v_did = sem("r_v_did")
            keys_made = sem("r_keys_made")
            rows_made = [sem(f"r_rows_made{q}") for q in range(2)]
            rows_copied = [sem(f"r_rows_copied{q}") for q in range(2)]
            signs_summed = sem("r_signs_summed")
            ranked = sem("r_ranked")
            recorded = [sem(f"r_recorded{k}") for k in range(2)]
            info_loaded = sem("r_info_loaded")
            block = ctx.enter_context(nc.Block())

            @block.gpsimd
            def _(pool):
                pool.iota(node_i[:, :], [[P, TILES]], base=0, channel_multiplier=1).then_inc(node_made, 1)
                pool.wait_ge(keys_made, 2)
                for k in range(2):
                    with pool.Fori(0, PASSES) as i:
                        for q, t, n in halves(i * PASS):
                            pool.wait_ge(rows_made[q], k * PASSES + i)
                            pool.tensor_copy(key_stage[q][:, 0:n],
                                             key[k][:, bass.ds(t, n)]).then_inc(keys_staged[q], 1)
                for k in range(2):
                    pool.wait_ge(ranked, k + 1)
                    for t in range(TILES):
                        pool.indirect_dma_start(meta[k], bass.IndirectOffsetOnAxis(rank[k][:, t:t + 1], 0),
                                                record[k][:, t, :], None).then_inc(recorded[k], 16)

            @block.sync
            def _(sp):
                for k in range(2):
                    sp.wait_ge(recorded[k], TILES * 16)
                    sp.dma_start(row_info[k][:, 0:TILES, :],
                                 meta[k].rearrange("(t p) c -> p t c", p=P)).then_inc(info_loaded, 16)
                sp.wait_ge(info_loaded, 32)

            @block.tensor
            def _(pe):
                for k in range(2):
                    with pe.Fori(0, PASSES) as i:
                        for q, t, n in halves(i * PASS):
                            pe.wait_ge(keys_staged[q], k * PASSES + i + 1)
                            pe.wait_ge(rows_copied[q], k * PASSES + i)
                            for c in range(n):
                                last = pe.matmul(spread_out[q][:, c, :],
                                                 bc(key_stage[q][:, c:c + 1], [P, P]), ident[:, :],
                                                 start=True, stop=True)
                            last.then_inc(rows_made[q], 1)

            @block.scalar
            def _(act):
                for k in range(2):
                    with act.Fori(0, PASSES) as i:
                        for q, t, n in halves(i * PASS):
                            act.wait_ge(rows_made[q], k * PASSES + i + 1)
                            act.copy(key_row[k][:, bass.ds(t * P, n * P)],
                                     spread_out[q][:, 0:n, :].rearrange("p c m -> p (c m)")
                                     ).then_inc(rows_copied[q], 1)
                for q in range(2):
                    act.wait_ge(rows_copied[q], 2 * PASSES)
                with act.Fori(0, TILES) as t:
                    act.wait_ge(signs_summed, t)
                    act.activation(compared[0][:, :], key_row[0][:, :], ACT.Sign,
                                   bias=minus_key[:, bass.ds(t, 1)],
                                   accum_out=higher[0][:, bass.ds(t, 1)]).then_inc(signs_summed, 1)

            @block.vector
            def _(dve):
                own = Count(dve, v_did)
                dve.wait_ge(node_made, 1)
                own.did(dve.tensor_copy(node[:, :], node_i[:, :]))
                own.wait()
                own.did(dve.tensor_scalar(real[:, :], node[:, :], float(NODES), None, ALU.is_lt))
                own.wait()
                for k in range(2):
                    own.did(dve.memset(row_info[k][:, :, :], 0))
                    own.did(dve.memset(record[k][:, :, :], 0))
                    own.did(dve.tensor_tensor(degree[k][:, :], degree[k][:, :], real[:, :], ALU.mult))
                    own.wait()
                    own.did(dve.tensor_scalar(key[k][:, :], degree[k][:, :], float(DEG_CAP), float(KEY_STEP),
                                              ALU.min, ALU.mult))
                    own.did(dve.tensor_copy(record[k][:, :, 0], start[k][:, :]))
                    own.did(dve.tensor_copy(record[k][:, :, 1], degree[k][:, :]))
                    own.did(dve.tensor_copy(record[k][:, :, 2], node_i[:, :]))
                    own.wait()
                    own.did(dve.tensor_tensor(key[k][:, :], key[k][:, :], node[:, :], ALU.add))
                    own.wait()
                own.did(dve.tensor_scalar(minus_key[:, :], key[0][:, :], -1.0, None, ALU.mult))
                own.wait()
                dve.sem_inc(keys_made, 2)
                for q in range(2):
                    dve.wait_ge(rows_copied[q], 2 * PASSES)
                with dve.Fori(0, TILES) as t:
                    own.enter(t, 1)
                    own.wait()
                    own.did(dve.tensor_scalar(compared[1][:, :], key_row[1][:, :], key[1][:, bass.ds(t, 1)], 0.0,
                                              ALU.is_gt, ALU.add, accum_out=higher[1][:, bass.ds(t, 1)]))
                    own.leave(TILES)
                dve.wait_ge(signs_summed, TILES)
                own.wait()
                own.did(dve.tensor_scalar(rank[0][:, :], higher[0][:, :], float(NODES_PAD - 1), 0.5,
                                          ALU.add, ALU.mult))
                own.did(dve.tensor_copy(rank[1][:, :], higher[1][:, :]))
                own.wait()
                dve.sem_inc(ranked, 2)

        with ExitStack() as ctx:
            sb, ps, sem = tensors(ctx)
            deg = [sb(f"t_deg{k}", [P, LTILES]) for k in range(2)]
            most = sb("t_most", [LTILES, 1])
            counts_i = sb("t_counts_i", [LTILES, 2], I32)
            counts = [sb(f"t_counts{k}", [LTILES, 2]) for k in range(2)]
            deg_t = ps("t_deg_t", [LTILES, P])
            sums = ps("t_sums", [1, 4 * LTILES + 4])
            v_did = sem("t_v_did")
            deg_made = sem("t_deg_made")
            deg_turned = sem("t_deg_turned")
            counts_made = sem("t_counts_made")
            sums_made = sem("t_sums_made")
            block = ctx.enter_context(nc.Block())

            @block.tensor
            def _(pe):
                few = slice(0, LTILES)
                for k in range(2):
                    pe.wait_ge(deg_made, k + 1)
                    pe.transpose(deg_t[:, :], deg[k][:, :], ident[:, :]).then_inc(deg_turned, 1)
                    pe.wait_ge(counts_made, k + 1)
                    groups, blocks = counts[k][:, 0:1], counts[k][:, 1:2]
                    pe.matmul(sums[:, G_OFF:G_OFF + LTILES], groups, above[few, few], start=True, stop=True)
                    pe.matmul(sums[:, N_BLOCKS:N_BLOCKS + LTILES], blocks, ident[few, few], start=True, stop=True)
                    pe.matmul(sums[:, B_OFF:B_OFF + LTILES], blocks, above[few, few], start=True, stop=True)
                    pe.matmul(sums[:, BODIES:BODIES + 1], groups, ones[few, 0:1], start=True,
                              stop=True).then_inc(sums_made, 1)

            @block.vector
            def _(dve):
                own = Count(dve, v_did)

                def ceil_div(column, by):
                    own.did(dve.tensor_scalar(counts_i[:, column], most[:, :], float(by - 1), None, ALU.add))
                    own.wait()
                    own.did(dve.tensor_scalar(counts_i[:, column], counts_i[:, column], by.bit_length() - 1, None,
                                              ALU.arith_shift_right))
                    own.wait()

                for k in range(2):
                    own.did(dve.tensor_copy(deg[k][:, :], row_info[k][:, :, 1]))
                    own.wait()
                    dve.sem_inc(deg_made, 1)
                    dve.wait_ge(deg_turned, k + 1)
                    own.did(dve.tensor_reduce(most[:, :], deg_t[:, :], AX.X, ALU.max))
                    own.wait()
                    ceil_div(slice(0, 1), GROUP)
                    ceil_div(slice(1, 2), BLOCK)
                    own.did(dve.tensor_copy(counts[k][:, 0:1], counts_i[:, 0:1]))
                    own.did(dve.tensor_scalar(counts[k][:, 1:2], counts_i[:, 1:2], 1.0, None, ALU.max))
                    own.wait()
                    dve.sem_inc(counts_made, 1)
                    dve.wait_ge(sums_made, k + 1)
                    own.did(dve.tensor_copy(tile_info[k][:, 0:BODIES + 1], sums[:, 0:BODIES + 1]))
                    own.wait()
                    total = tile_info[k][:, BODIES:BODIES + 1]
                    own.did(dve.tensor_scalar(total, total, float(GROUPS - 1), None, ALU.add))
                    own.wait()
                    own.did(dve.tensor_scalar(total, total, GROUPS.bit_length() - 1, None, ALU.arith_shift_right))
                    own.wait()

        def tile_value(eng, k, field, t, most):
            return eng.value_load(tile_info[k][0:1, bass.ds(field + t, 1)], min_val=0, max_val=most)

        BLOCKS_MAX = TILES + EDGES // BLOCK + 1

        def lay_out(k):
            with ExitStack() as ctx:
                sb, ps, sem = tensors(ctx, f"_{k}")
                iota_i = sb("l_iota_i", [P, BLOCK], I32)
                iota_f = sb("l_iota_f", [P, BLOCK])
                at = sb("l_at", [P, 1])
                left = sb("l_left", [P, 1])
                where = sb("l_where", [P, 1], I32)
                fetched = sb("l_fetched", [P, BLOCK], I32)
                valid = sb("l_valid", [P, BLOCK])
                shifted = sb("l_shifted", [P, BLOCK])
                laid = sb("l_laid", [P, BLOCK], I32)
                iota_made = sem("l_iota_made")
                v_did = sem("l_v_did")
                where_made = sem("l_where_made")
                block_fetched = sem("l_block_fetched")
                block_laid = sem("l_block_laid")
                block_written = sem("l_block_written")
                block = ctx.enter_context(nc.Block())

                def tile_loop(eng, body):
                    with eng.Fori(0, LTILES) as t:
                        blocks = tile_value(eng, k, N_BLOCKS, t, BLOCKS_MAX)
                        before = tile_value(eng, k, B_OFF, t, BLOCKS_MAX)
                        body(t, blocks, before)

                @block.vector
                def _(dve):
                    dve.wait_ge(iota_made, 1)
                    dve.tensor_copy(iota_f[:, :], iota_i[:, :]).then_inc(v_did, 1)
                    dve.wait_ge(v_did, 1)

                    def body(t, blocks, before):
                        base = t * 2 + before * 6 + 1
                        dve.wait_ge(v_did, base)
                        dve.tensor_copy(at[:, :], row_info[k][:, bass.ds(t, 1), 0]).then_inc(v_did, 1)
                        dve.tensor_copy(left[:, :], row_info[k][:, bass.ds(t, 1), 1]).then_inc(v_did, 1)
                        with dve.Fori(0, blocks) as b:
                            n = before + b
                            done = base + b * 6 + 2
                            dve.wait_ge(v_did, done)
                            dve.tensor_scalar(where[:, :], at[:, :], float(EDGES_PAD - BLOCK), None,
                                              ALU.min).then_inc(v_did, 1)
                            dve.wait_ge(v_did, done + 1)
                            dve.sem_inc(where_made, 1)
                            dve.tensor_scalar(at[:, :], at[:, :], float(BLOCK), None, ALU.add).then_inc(v_did, 1)
                            dve.tensor_scalar(valid[:, :], iota_f[:, :], left[:, :], None,
                                              ALU.is_lt).then_inc(v_did, 1)
                            dve.wait_ge(v_did, done + 3)
                            dve.tensor_scalar(left[:, :], left[:, :], float(-BLOCK), None,
                                              ALU.add).then_inc(v_did, 1)
                            dve.wait_ge(block_fetched, n * 16 + 16)
                            dve.scalar_tensor_tensor(shifted[:, :], fetched[:, :], float(-ZERO_ROW), valid[:, :],
                                                     ALU.add, ALU.mult).then_inc(v_did, 1)
                            dve.wait_ge(v_did, done + 5)
                            dve.wait_ge(block_written, n * 32)
                            dve.tensor_scalar(laid[:, :], shifted[:, :], float(ZERO_ROW), None,
                                              ALU.add).then_inc(v_did, 1)
                            dve.wait_ge(v_did, done + 6)
                            dve.sem_inc(block_laid, 1)
                    tile_loop(dve, body)

                @block.gpsimd
                def _(pool):
                    pool.iota(iota_i[:, :], [[1, BLOCK]], base=0, channel_multiplier=0).then_inc(iota_made, 1)

                    def body(t, blocks, before):
                        with pool.Fori(0, blocks) as b:
                            n = before + b
                            pool.wait_ge(where_made, n + 1)
                            pool.wait_ge(block_laid, n)
                            turn(pool, turns)
                            pool.indirect_dma_start(fetched[:, :], None, nbrs[k],
                                                    bass.IndirectOffsetOnAxis(where[:, 0:1], 0)
                                                    ).then_inc(block_fetched, 16)
                    tile_loop(pool, body)

                @block.sync
                def _(sp):
                    def body(t, blocks, before):
                        first = tile_value(sp, k, G_OFF, t, SLOTS_MAX // GROUP - BLOCK // GROUP)
                        with sp.Fori(0, blocks) as b:
                            n = before + b
                            sp.wait_ge(block_written, n * 32)
                            turn(sp, turns)
                            sp.wait_ge(block_laid, n + 1)
                            at_group = nc.s_assert_within(
                                first + b * (BLOCK // GROUP), 0, (SLOTS_MAX - BLOCK) // GROUP,
                                skip_runtime_bounds_check_because="SLOTS_MAX bounds all tiles' slots")
                            sp.dma_start(slots[k][:, bass.ds(at_group * GROUP, BLOCK)],
                                         laid[:, :]).then_inc(block_written, 16)
                            sp.dma_start(slot_tile[k][:, bass.ds(at_group, BLOCK // GROUP)],
                                         tile_ids[0:1, bass.ds(t, 1), :].squeeze(1)).then_inc(block_written, 16)
                    tile_loop(sp, body)
                    total = tile_value(sp, k, B_OFF, LTILES - 1, BLOCKS_MAX)
                    sp.wait_ge(block_written, total * 32 + 32)
                    turn(sp, turns)

        for k in range(2):
            lay_out(k)

        HALF = BODY // 2
        HALF_GROUPS = GROUPS // 2
        BODIES_MAX = SLOTS_MAX // BODY

        def load_slots(sp, k, before, bodies, slot_rows, slot_tiles, rows_loaded, group_used):
            with sp.Fori(0, bodies) as j:
                n = before + j
                for q in range(2):
                    sp.wait_ge(group_used, n * GROUPS + (q + 1) * HALF_GROUPS)
                    at_slot = nc.s_assert_within(j * BODY + q * HALF, 0, SLOTS_MAX - HALF,
                                                 skip_runtime_bounds_check_because="bodies of the tiles' slots")
                    at_group = nc.s_assert_within(j * GROUPS + q * HALF_GROUPS, 0,
                                                  SLOTS_MAX // GROUP - HALF_GROUPS,
                                                  skip_runtime_bounds_check_because="groups of the tiles' slots")
                    sp.dma_start(slot_rows[q][:, :], slots[k][:, bass.ds(at_slot, HALF)]
                                 ).then_inc(rows_loaded[q], 16)
                    sp.dma_start(slot_tiles[q][:, :], slot_tile[k][:, bass.ds(at_group, HALF_GROUPS)]
                                 ).then_inc(rows_loaded[q], 16)

        def gather(pool, before, bodies, table, rows, slot_rows, rows_loaded, group_used, gathered):
            with pool.Fori(0, bodies) as j:
                n = before + j
                for g in range(GROUPS):
                    q, first = g // HALF_GROUPS, g % HALF_GROUPS * GROUP
                    if first == 0:
                        pool.wait_ge(rows_loaded[q], n * 32 + 32)
                    pool.wait_ge(group_used, n * GROUPS + g + 1)
                    turn(pool, turns)
                    for s in range(GROUP):
                        pool.indirect_dma_start(
                            rows[g][:, s, :], None, table,
                            bass.IndirectOffsetOnAxis(slot_rows[q][:, first + s:first + s + 1], 0)
                        ).then_inc(gathered[g], 16)

        def bodies_of(eng, k):
            return eng.value_load(tile_info[k][0:1, BODIES:BODIES + 1], min_val=0, max_val=BODIES_MAX)

        with ExitStack() as ctx:
            sb, ps, sem = tensors(ctx)
            own_rows = sb("a_own_rows", [P, TILES + 1, 3 * D])
            acc = sb("a_acc", [P, TILES + 1, A0])
            rows = [sb(f"a_rows{g}", [P, GROUP, W0]) for g in range(GROUPS)]
            slot_rows = [sb(f"a_slot_rows{q}", [P, HALF], I32) for q in range(2)]
            slot_tiles = [sb(f"a_slot_tiles{q}", [1, HALF_GROUPS], I32) for q in range(2)]
            hidden = [sb(f"a_hidden{g}", [P, GROUP, D]) for g in range(GROUPS)]
            weighed = sb("a_weighed", [P, GROUP, D])
            logit = [sb(f"a_logit{g}", [P, GROUP]) for g in range(GROUPS)]
            mask = [sb(f"a_mask{g}", [P, GROUP]) for g in range(GROUPS)]
            w2 = sb("a_w2", [P, D])
            b2 = sb("a_b2", [P, 1])
            wl = sb("a_wl", [P, D])
            bl = sb("a_bl", [1, D])
            per_mask = sb("a_per_mask", [P, TILES])
            has_half = sb("a_has_half", [P, TILES])
            emb = [sb(f"a_emb{q}", [P, HEAD, D]) for q in range(2)]
            emb_t = [sb(f"a_emb_t{q}", [P, HEAD, D]) for q in range(2)]
            stats = sb("a_stats", [P, TILES, 6])
            mean = sb("a_mean", [P, TILES])
            spread = sb("a_spread", [P, TILES])
            rstd = sb("a_rstd", [P, TILES])
            turned = [ps(f"a_turned{q}", [P, HEAD, D]) for q in range(2)]
            product = [ps(f"a_product{q}", [P, HEAD, D]) for q in range(2)]
            own_gathered = sem("a_own_gathered")
            w_loaded = sem("a_w_loaded")
            v_did = sem("a_v_did")
            rows_loaded = [sem(f"a_rows_loaded{q}") for q in range(2)]
            gathered = [sem(f"a_gathered{g}") for g in range(GROUPS)]
            group_used = sem("a_group_used")
            logit_made = sem("a_logit_made")
            mask_made = sem("a_mask_made")
            emb_made = [sem(f"a_emb_made{q}") for q in range(2)]
            emb_turned = [sem(f"a_emb_turned{q}") for q in range(2)]
            emb_copied = [sem(f"a_emb_copied{q}") for q in range(2)]
            product_made = [sem(f"a_product_made{q}") for q in range(2)]
            product_used = [sem(f"a_product_used{q}") for q in range(2)]
            var_made = sem("a_var_made")
            std_made = sem("a_std_made")
            centred = sem("a_centred")
            h_made = sem("a_h_made")
            stored = sem("a_stored")
            block = ctx.enter_context(nc.Block())
            own_a, own_h, own_x = (slice(c * D, (c + 1) * D) for c in range(3))

            @block.sync
            def _(sp):
                bodies = bodies_of(sp, 0)
                load_slots(sp, 0, 0, bodies, slot_rows, slot_tiles, rows_loaded, group_used)

            @block.gpsimd
            def _(pool):
                for t in range(TILES):
                    pool.indirect_dma_start(own_rows[:, t, :], None, own0,
                                            bass.IndirectOffsetOnAxis(row_info[0][:, t, 2:3], 0)
                                            ).then_inc(own_gathered, 16)
                bodies = bodies_of(pool, 0)
                gather(pool, 0, bodies, table0, rows, slot_rows, rows_loaded, group_used, gathered)
                pool.wait_ge(h_made, 1)
                for t in range(TILES):
                    node_of = bass.IndirectOffsetOnAxis(row_info[0][:, t, 2:3], 0)
                    pool.indirect_dma_start(own1, node_of, own_rows[:, t, own_x], None).then_inc(stored, 16)
                    pool.indirect_dma_start(table1, node_of, own_rows[:, t, own_h], None).then_inc(stored, 16)
                pool.wait_ge(stored, 2 * TILES * 16)

            @block.scalar
            def _(act):
                act.dma_start(w2[:, :], bc(w2_in.rearrange("k o -> o k"), [P, D])).then_inc(w_loaded, 16)
                act.dma_start(b2[:, :], bc(b2_in.rearrange("(o n) -> o n", o=1), [P, 1])).then_inc(w_loaded, 16)
                act.dma_start(wl[:, :], wl_in).then_inc(w_loaded, 16)
                act.dma_start(bl[:, :], bl_in.rearrange("(o n) -> o n", o=1)).then_inc(w_loaded, 16)
                act.wait_ge(w_loaded, 64)
                bodies = bodies_of(act, 0)
                with act.Fori(0, bodies) as j:
                    for g in range(GROUPS):
                        act.wait_ge(logit_made, j * GROUPS + g + 1)
                        act.activation(mask[g][:, :], logit[g][:, :], ACT.Sigmoid,
                                       bias=b2[:, :]).then_inc(mask_made, 1)
                with act.Fori(0, PASSES) as i:
                    for q, _, n in halves(0):
                        act.wait_ge(emb_turned[q], i + 1)
                        act.wait_ge(product_made[q], i)
                        act.copy(emb_t[q][:, 0:n, :], turned[q][:, 0:n, :]).then_inc(emb_copied[q], 1)
                act.wait_ge(var_made, 1)
                act.sqrt(rstd[:, :], rstd[:, :]).then_inc(std_made, 1)
                act.wait_ge(centred, 1)
                h1 = own_rows[:, 0:TILES, own_h]
                act.activation(h1, h1, ACT.Relu).then_inc(h_made, 1)

            @block.tensor
            def _(pe):
                pe.wait_ge(w_loaded, 64)
                with pe.Fori(0, PASSES) as i:
                    for q, t, n in halves(i * PASS):
                        pe.wait_ge(emb_made[q], i + 1)
                        pe.wait_ge(emb_copied[q], i)
                        for c in range(n):
                            last = pe.transpose(turned[q][:, c, :], emb[q][:, c, :], ident[:, :])
                        last.then_inc(emb_turned[q], 1)
                    for q, t, n in halves(i * PASS):
                        pe.wait_ge(emb_copied[q], i + 1)
                        pe.wait_ge(product_used[q], i)
                        for c in range(n):
                            pe.matmul(product[q][:, c, :], emb_t[q][:, c, :], wl[:, :], start=True, stop=False)
                            last = pe.matmul(product[q][:, c, :], ones[0:1, :], bl[0:1, :], start=False,
                                             stop=True)
                        last.then_inc(product_made[q], 1)

            @block.vector
            def _(dve):
                own = Count(dve, v_did)
                own.did(dve.memset(acc[:, :, :], 0.0))
                own.did(dve.memset(own_rows[:, TILES, :], 0.0))
                own.wait()
                dve.sem_inc(group_used, GROUPS)
                dve.wait_ge(w_loaded, 64)
                dve.wait_ge(own_gathered, TILES * 16)
                bodies = bodies_of(dve, 0)
                with dve.Fori(0, bodies) as j:
                    own.enter(j, GROUPS * (1 + GROUP))
                    tiles = []
                    for g in range(GROUPS + 1):
                        if g < GROUPS:
                            q = g // HALF_GROUPS
                            if g % HALF_GROUPS == 0:
                                dve.wait_ge(rows_loaded[q], j * 32 + 32)
                                turn(dve, turns)
                            tiles.append(dve.value_load(slot_tiles[q][0:1, g % HALF_GROUPS:g % HALF_GROUPS + 1],
                                                        min_val=0, max_val=TILES))
                            dve.wait_ge(gathered[g], j * (GROUP * 16) + GROUP * 16)
                            a = own_rows[:, bass.ds(tiles[g], 1), own_a]
                            own.did(dve.tensor_tensor(hidden[g][:, :, :], rows[g][:, :, 0:D],
                                                      bc(a, [P, GROUP, D]), ALU.add))
                            own.wait()
                            for s in range(GROUP):
                                last = dve.scalar_tensor_tensor(
                                    weighed[:, s, :], hidden[g][:, s, :], 0.0, w2[:, :], ALU.max, ALU.mult,
                                    accum_out=logit[g][:, s:s + 1])
                            last.then_inc(logit_made, 1)
                        if g > 0:
                            f = g - 1
                            dve.wait_ge(mask_made, j * GROUPS + f + 1)
                            sums = acc[:, bass.ds(tiles[f], 1), 0:D + 1].squeeze(1)
                            for s in range(GROUP):
                                own.wait()
                                own.did(dve.scalar_tensor_tensor(
                                    sums, rows[f][:, s, D:2 * D + 1], mask[f][:, s:s + 1], sums,
                                    ALU.mult, ALU.add))
                            own.wait()
                            dve.sem_inc(group_used, 1)
                    own.leave(bodies)
                own.wait()
                own.did(dve.tensor_scalar(per_mask[:, :], acc[:, 0:TILES, D], 1e-9, None, ALU.add))
                own.did(dve.tensor_scalar(has_half[:, :], row_info[0][:, 0:TILES, 1], 0.0, 0.5,
                                          ALU.is_gt, ALU.mult))
                own.wait()
                own.did(dve.reciprocal(per_mask[:, :], per_mask[:, :]))
                own.wait()
                turn(dve, turns)
                with dve.Fori(0, PASSES) as i:
                    own.enter(i, 3 * PASS)
                    for q, t, n in halves(i * PASS):
                        dve.wait_ge(emb_turned[q], i)
                        for c in range(n):
                            col = bass.ds(t + c, 1)
                            h_of = own_rows[:, col, own_h].squeeze(1)
                            own.did(dve.scalar_tensor_tensor(
                                emb[q][:, c, :], acc[:, col, 0:D].squeeze(1), per_mask[:, col], h_of,
                                ALU.mult, ALU.subtract))
                            own.wait()
                            own.did(dve.scalar_tensor_tensor(
                                emb[q][:, c, :], emb[q][:, c, :], has_half[:, col], h_of, ALU.mult, ALU.add))
                        own.wait()
                        dve.sem_inc(emb_made[q], 1)
                    for q, t, n in halves(i * PASS):
                        dve.wait_ge(product_made[q], i + 1)
                        x_of = own_rows[:, bass.ds(t, n), own_x]
                        dve.scalar_tensor_tensor(x_of, product[q][:, 0:n, :], 0.0, x_of, ALU.max,
                                                 ALU.add).then_inc(product_used[q], 1)
                        dve.wait_ge(product_used[q], i + 1)
                        for c in range(n):
                            own.did(dve.bn_stats(stats[:, bass.ds(t + c, 1), :].squeeze(1),
                                                 own_rows[:, bass.ds(t + c, 1), own_x].squeeze(1)))
                    own.leave(PASSES)
                rstd_steps(dve, own, stats, mean, spread, rstd)
                dve.sem_inc(var_made, 1)
                dve.wait_ge(std_made, 1)
                own.did(dve.reciprocal(rstd[:, :], rstd[:, :]))
                h1 = own_rows[:, 0:TILES, own_h]
                own.did(dve.tensor_tensor(h1, own_rows[:, 0:TILES, own_x],
                                          bc(mean[:, :].unsqueeze(2), [P, TILES, D]), ALU.subtract))
                own.wait()
                dve.tensor_tensor(h1, h1, bc(rstd[:, :].unsqueeze(2), [P, TILES, D]),
                                  ALU.mult).then_inc(centred, 1)

        LAYERS = 4
        with ExitStack() as ctx:
            sb, ps, sem = tensors(ctx)
            own_x1 = sb("c_own_x1", [P, TILES, D])
            own_h1 = sb("c_own_h1", [P, TILES, D])
            acc = sb("c_acc", [P, TILES + 1, D])
            acc_t = sb("c_acc_t", [P, NODES_PAD])
            h_t = sb("c_h_t", [P, NODES_PAD])
            rows = [sb(f"c_rows{g}", [P, GROUP, D]) for g in range(GROUPS)]
            pairs = sb("c_pairs", [P, 2, D])
            best = sb("c_best", [P, D])
            slot_rows = [sb(f"c_slot_rows{q}", [P, HALF], I32) for q in range(2)]
            slot_tiles = [sb(f"c_slot_tiles{q}", [1, HALF_GROUPS], I32) for q in range(2)]
            w = [sb(f"c_w{m}", [P, D]) for m in range(2)]
            r = [sb(f"c_r{m}", [P, D]) for m in range(2)]
            b = [sb(f"c_b{m}", [P, 1]) for m in range(2)]
            w_now = sb("c_w_now", [P, D])
            r_now = sb("c_r_now", [P, D])
            b_now = sb("c_b_now", [P, 1])
            stage = [sb(f"c_stage{q}", [P, HEAD, D]) for q in range(2)]
            new_t = [sb(f"c_new_t{q}", [P, HEAD, D]) for q in range(2)]
            new = sb("c_new", [P, TILES, D])
            turned = [ps(f"c_turned{q}", [P, HEAD, D]) for q in range(2)]
            product = [ps(f"c_product{q}", [P, HEAD, D]) for q in range(2)]
            back = [ps(f"c_back{q}", [P, HEAD, D]) for q in range(2)]
            own_gathered = sem("c_own_gathered")
            w_loaded = sem("c_w_loaded")
            v_did = sem("c_v_did")
            rows_loaded = [sem(f"c_rows_loaded{q}") for q in range(2)]
            gathered = [sem(f"c_gathered{g}") for g in range(GROUPS)]
            group_used = sem("c_group_used")
            maxima_done = sem("c_maxima_done")
            staged = [sem(f"c_staged{q}") for q in range(2)]
            tile_turned = [sem(f"c_tile_turned{q}") for q in range(2)]
            tile_copied = [sem(f"c_tile_copied{q}") for q in range(2)]
            product_made = [sem(f"c_product_made{q}") for q in range(2)]
            new_made = [sem(f"c_new_made{q}") for q in range(2)]
            new_turned = [sem(f"c_new_turned{q}") for q in range(2)]
            new_out = [sem(f"c_new_out{q}") for q in range(2)]
            table_stored = sem("c_table_stored")
            out_stored = sem("c_out_stored")
            block = ctx.enter_context(nc.Block())

            @block.sync
            def _(sp):
                for m, (wi, ri, bi) in enumerate(((gw1_in, gr1_in, gb1_in), (gw2_in, gr2_in, gb2_in))):
                    sp.dma_start(w[m][:, :], wi).then_inc(w_loaded, 16)
                    sp.dma_start(r[m][:, :], ri).then_inc(w_loaded, 16)
                    sp.dma_start(b[m][:, :], bi.rearrange("(k o) -> k o", o=1)).then_inc(w_loaded, 16)
                bodies = bodies_of(sp, 1)
                with sp.Fori(0, LAYERS) as layer:
                    load_slots(sp, 1, layer * bodies, bodies, slot_rows, slot_tiles, rows_loaded, group_used)

            @block.gpsimd
            def _(pool):
                for t in range(TILES):
                    node_of = bass.IndirectOffsetOnAxis(row_info[1][:, t, 2:3], 0)
                    pool.indirect_dma_start(own_x1[:, t, :], None, own1, node_of).then_inc(own_gathered, 16)
                    pool.indirect_dma_start(own_h1[:, t, :], None, table1, node_of).then_inc(own_gathered, 16)
                bodies = bodies_of(pool, 1)
                with pool.Fori(0, LAYERS) as layer:
                    pool.wait_ge(table_stored, layer * (TILES * 16))
                    turn(pool, turns)
                    gather(pool, layer * bodies, bodies, table1, rows, slot_rows, rows_loaded, group_used,
                           gathered)
                    pool.wait_ge(maxima_done, layer + 1)
                    turn(pool, turns)
                    with pool.If(layer < LAYERS - 1):
                        for t in range(TILES):
                            q = int(t % PASS >= HEAD)
                            if t % PASS in (0, HEAD):
                                pool.wait_ge(new_out[q], layer * PASSES + t // PASS + 1)
                                turn(pool, turns)
                            pool.indirect_dma_start(table1, bass.IndirectOffsetOnAxis(row_info[1][:, t, 2:3], 0),
                                                    new[:, t, :], None).then_inc(table_stored, 16)
                    with pool.Else():
                        for t in range(TILES):
                            q = int(t % PASS >= HEAD)
                            if t % PASS in (0, HEAD):
                                pool.wait_ge(new_out[q], (LAYERS - 1) * PASSES + t // PASS + 1)
                            pool.indirect_dma_start(out, bass.IndirectOffsetOnAxis(row_info[1][:, t, 2:3], 0),
                                                    new[:, t, :], None, bounds_check=NODES - 1,
                                                    oob_is_err=False).then_inc(out_stored, 16)
                pool.wait_ge(out_stored, TILES * 16)

            @block.scalar
            def _(act):
                with act.Fori(0, PASSES) as i:
                    for q, t, n in halves(i * PASS):
                        act.wait_ge(tile_turned[q], i + 1)
                        act.copy(h_t[:, bass.ds(t * P, n * P)],
                                 turned[q][:, 0:n, :].rearrange("p c m -> p (c m)")).then_inc(tile_copied[q], 1)
                with act.Fori(0, LAYERS) as layer:
                    with act.Fori(0, PASSES) as i:
                        n_pass = layer * PASSES + i
                        for q, t, n in halves(i * PASS):
                            act.wait_ge(tile_turned[q], n_pass + PASSES + 1)
                            act.copy(acc_t[:, bass.ds(t * P, n * P)],
                                     turned[q][:, 0:n, :].rearrange("p c m -> p (c m)")
                                     ).then_inc(tile_copied[q], 1)
                        for q, t, n in halves(i * PASS):
                            act.wait_ge(product_made[q], n_pass + 1)
                            act.wait_ge(new_turned[q], n_pass)
                            act.activation(new_t[q][:, 0:n, :], product[q][:, 0:n, :], ACT.Relu,
                                           bias=b_now[:, :]).then_inc(new_made[q], 1)

            @block.tensor
            def _(pe):
                def turn_tiles(n_pass, q, n):
                    pe.wait_ge(staged[q], n_pass + 1)
                    pe.wait_ge(tile_copied[q], n_pass)
                    for c in range(n):
                        last = pe.transpose(turned[q][:, c, :], stage[q][:, c, :], ident[:, :])
                    last.then_inc(tile_turned[q], 1)

                with pe.Fori(0, PASSES) as i:
                    for q, t, n in halves(i * PASS):
                        turn_tiles(i, q, n)
                with pe.Fori(0, LAYERS) as layer:
                    with pe.Fori(0, PASSES) as i:
                        n_pass = layer * PASSES + i
                        for q, t, n in halves(i * PASS):
                            turn_tiles(n_pass + PASSES, q, n)
                        for q, t, n in halves(i * PASS):
                            cols = bass.ds(t * P, n * P)
                            pe.wait_ge(tile_copied[q], n_pass + PASSES + 1)
                            pe.wait_ge(new_made[q], n_pass)
                            whole_q = product[q][:, 0:n, :].rearrange("p c m -> p (c m)")
                            pe.matmul(whole_q, w_now[:, :], acc_t[:, cols], start=True, stop=False)
                            pe.matmul(whole_q, r_now[:, :], h_t[:, cols], start=False,
                                      stop=True).then_inc(product_made[q], 1)
                        for q, t, n in halves(i * PASS):
                            pe.wait_ge(new_made[q], n_pass + 1)
                            pe.wait_ge(new_out[q], n_pass)
                            for c in range(n):
                                last = pe.transpose(back[q][:, c, :], new_t[q][:, c, :], ident[:, :])
                            last.then_inc(new_turned[q], 1)

            @block.vector
            def _(dve):
                own = Count(dve, v_did)
                own.did(dve.memset(acc[:, :, :], 0.0))
                own.wait()
                dve.sem_inc(group_used, GROUPS)
                dve.wait_ge(w_loaded, 6 * 16)
                dve.wait_ge(own_gathered, 2 * TILES * 16)

                def stage_tiles(n_pass, q, source):
                    dve.wait_ge(tile_turned[q], n_pass)
                    n = source.shape[1]
                    dve.tensor_copy(stage[q][:, 0:n, :], source).then_inc(staged[q], 1)

                with dve.Fori(0, PASSES) as i:
                    for q, t, n in halves(i * PASS):
                        stage_tiles(i, q, own_h1[:, bass.ds(t, n), :])
                own.did(dve.tensor_copy(w_now[:, :], w[0][:, :]))
                own.did(dve.tensor_copy(r_now[:, :], r[0][:, :]))
                own.did(dve.tensor_copy(b_now[:, :], b[0][:, :]))
                bodies = bodies_of(dve, 1)
                with dve.Fori(0, LAYERS) as layer:
                    base = layer * (bodies * (3 * GROUPS) + (2 * PASSES + 4)) + 4
                    with dve.Fori(0, bodies) as j:
                        n = layer * bodies + j
                        for g in range(GROUPS):
                            done = base + j * (3 * GROUPS) + 3 * g
                            q = g // HALF_GROUPS
                            if g % HALF_GROUPS == 0:
                                dve.wait_ge(rows_loaded[q], n * 32 + 32)
                                turn(dve, turns)
                            tile = dve.value_load(slot_tiles[q][0:1, g % HALF_GROUPS:g % HALF_GROUPS + 1],
                                                  min_val=0, max_val=TILES)
                            best_of = acc[:, bass.ds(tile, 1), :].squeeze(1)
                            dve.wait_ge(gathered[g], n * (GROUP * 16) + GROUP * 16)
                            dve.wait_ge(v_did, done)
                            dve.tensor_tensor(pairs[:, :, :], rows[g][:, 0:2, :], rows[g][:, 2:4, :],
                                              ALU.max).then_inc(v_did, 1)
                            dve.wait_ge(v_did, done + 1)
                            dve.sem_inc(group_used, 1)
                            dve.tensor_tensor(best[:, :], pairs[:, 0, :], pairs[:, 1, :],
                                              ALU.max).then_inc(v_did, 1)
                            dve.wait_ge(v_did, done + 2)
                            dve.tensor_tensor(best_of, best_of, best[:, :], ALU.max).then_inc(v_did, 1)
                    after = base + bodies * (3 * GROUPS)
                    dve.wait_ge(v_did, after)
                    dve.sem_inc(maxima_done, 1)
                    dve.wait_ge(table_stored, layer * (TILES * 16))
                    turn(dve, turns)
                    with dve.Fori(0, PASSES) as i:
                        n_pass = layer * PASSES + i
                        for q, t, n in halves(i * PASS):
                            stage_tiles(n_pass + PASSES, q, acc[:, bass.ds(t, n), :])
                        for q, t, n in halves(i * PASS):
                            cols = bass.ds(t * P, n * P)
                            dve.wait_ge(new_made[q], n_pass + 1)
                            dve.tensor_copy(h_t[:, cols],
                                            new_t[q][:, 0:n, :].rearrange("p c m -> p (c m)")
                                            ).then_inc(v_did, 1)
                            dve.wait_ge(new_turned[q], n_pass + 1)
                            turn(dve, turns)
                            with dve.If(layer < LAYERS - 1):
                                dve.tensor_copy(new[:, bass.ds(t, n), :], back[q][:, 0:n, :]
                                                ).then_inc(new_out[q], 1)
                            with dve.Else():
                                dve.tensor_tensor(new[:, bass.ds(t, n), :], back[q][:, 0:n, :],
                                                  own_x1[:, bass.ds(t, n), :], ALU.add).then_inc(new_out[q], 1)
                    for q in range(2):
                        dve.wait_ge(tile_turned[q], layer * PASSES + 2 * PASSES)
                        dve.wait_ge(product_made[q], layer * PASSES + PASSES)
                        dve.wait_ge(new_made[q], layer * PASSES + PASSES)
                        dve.wait_ge(staged[q], layer * PASSES + 2 * PASSES)
                    dve.memset(acc[:, :, :], 0.0).then_inc(v_did, 1)
                    dve.tensor_copy(w_now[:, :], w[1][:, :]).then_inc(v_did, 1)
                    dve.tensor_copy(r_now[:, :], r[1][:, :]).then_inc(v_did, 1)
                    dve.tensor_copy(b_now[:, :], b[1][:, :]).then_inc(v_did, 1)


_INS = ["x", "src", "dst", "L0_gnn_W1", "L0_gnn_b1", "L0_gnn_W2", "L0_gnn_b2", "L0_gnn_Wl", "L0_gnn_bl",
        "L1_gnn_W1", "L1_gnn_b1", "L1_gnn_R1", "L1_gnn_W2", "L1_gnn_b2", "L1_gnn_R2"]


def kernel(**inputs):
    import concourse.bacc as bacc
    from concourse.bass_utils import run_bass_kernel_spmd

    nc = bacc.Bacc("TRN2", target_bir_lowering=False, num_devices=1)
    arrays, args = {}, []
    for name in _INS:
        a = np.ascontiguousarray(inputs[name])
        arrays[f"in_{name}"] = a
        args.append(nc.dram_tensor(f"in_{name}", a.shape, mybir.dt.from_np(a.dtype), kind="ExternalInput").ap())
    args.append(nc.dram_tensor("out_x", (NODES, D), F32, kind="ExternalOutput").ap())
    gnn(nc, *args)
    return run_bass_kernel_spmd(nc, [arrays], core_ids=[0]).results[0]["out_x"]
```

```python
import numpy as np
from contextlib import ExitStack
import concourse.bass as bass
from concourse import mybir
from concourse.alu_op_type import AluOpType as ALU

F32 = mybir.dt.float32
BF16 = mybir.dt.bfloat16
I32 = mybir.dt.int32
U8 = mybir.dt.uint8
F8 = mybir.dt.float8e4
ACT = mybir.ActivationFunctionType
AX = mybir.AxisListType

P = 128
NODES = 6250
EDGES = 200000
D = 128
TILES = -(-NODES // P)
NODES_PAD = TILES * P
LAST_ROWS = NODES - (TILES - 1) * P
PAD_NODE = NODES_PAD - 1
SUB = 8
CHUNKS = 2 * SUB * -(-EDGES // (P * 2 * SUB))
EDGES_PAD = P * CHUNKS
SUBS = CHUNKS // SUB
FULL_PARTS = EDGES // CHUNKS
REST = EDGES - FULL_PARTS * CHUNKS
assert FULL_PARTS == P - 1 and REST > 0 and PAD_NODE >= NODES
GROUP = 4
BODY = (32, 8)
GROUPS = tuple(b // GROUP for b in BODY)
BLOCK = 64
LTILES = TILES + 1
SLOTS_MAX = EDGES + GROUP + EDGES // P + (GROUP + 1) * TILES + 2 * BLOCK
ZERO_ROW = NODES_PAD
TABLE_ROWS = NODES_PAD + P
W0 = 2 * D + 4
A0 = D + 4
DEG_CAP = 1023
KEY_STEP = 8192
HEAD, TAIL = 4, 3
PASS = HEAD + TAIL
PASSES = TILES // PASS
assert PASSES * PASS == TILES
assert EDGES > (TILES - 1) * BODY[0] * P
assert SUBS == 4 * TILES
INFO = 4
RECORD = (INFO, INFO + BLOCK + TILES)
QUICK_SLOTS = TILES * BLOCK + BLOCK
PARTS = 8
PART = NODES_PAD // PARTS
ROUNDS = BLOCK // 8
LIST_STEPS = 2 + (2 * ROUNDS - 1) + 8 + (2 * ROUNDS - 1) + 2
QUARTERS = 4
QUARTER = NODES_PAD // QUARTERS
BANK = 512
WIDE = 4
assert QUARTER * QUARTERS == PART * PARTS == NODES_PAD and BANK < PART <= 2 * BANK


class Count:

    def __init__(self, eng, sem):
        self.eng, self.sem, self.base, self.n = eng, sem, 0, 0

    def of(self, eng):
        self.eng = eng
        return self

    def did(self, instruction):
        instruction.then_inc(self.sem, 1)
        self.n += 1

    def wait(self):
        self.eng.wait_ge(self.sem, self.base + self.n)

    def enter(self, i, per_pass):
        self.before = self.base + self.n
        self.base, self.n, self.per_pass = self.before + i * per_pass, 0, per_pass

    def leave(self, passes):
        assert self.n == self.per_pass, (self.n, self.per_pass)
        self.base, self.n = self.before + passes * self.per_pass, 0


def turn(eng, turns):
    eng.sem_inc(turns, 1)


def bc(ap, shape):
    return ap.to_broadcast(shape)


def gnn(nc, x_in, src_in, dst_in, w1_in, b1_in, w2_in, b2_in, wl_in, bl_in,
        gw1_in, gb1_in, gr1_in, gw2_in, gb2_in, gr2_in, out):
    def dram(name, shape, dt=F32):
        return nc.dram_tensor(name, shape, dt).ap()

    table0 = dram("table0", [TABLE_ROWS, W0])
    own0 = dram("own0", [NODES_PAD, 3 * D])
    table1 = dram("table1", [TABLE_ROWS, D])
    own1 = dram("own1", [NODES_PAD, D])
    nbrs = [dram(f"nbrs{k}", [EDGES_PAD, 1], I32) for k in range(2)]
    meta = [dram(f"meta{k}", [NODES_PAD, RECORD[k]], I32) for k in range(2)]
    picks = dram("picks", [TILES, NODES_PAD], BF16)
    chosen = dram("chosen", [TILES, P, NODES_PAD], U8)
    slots = [dram(f"slots{k}", [P, SLOTS_MAX], I32) for k in range(2)]
    slot_tile = [dram(f"slot_tile{k}", [1, SLOTS_MAX // GROUP], I32) for k in range(2)]

    with ExitStack() as whole:
        def tensors(ctx, tag=""):
            def sb(name, shape, dt=F32):
                return ctx.enter_context(nc.sbuf_tensor(name + tag, shape, dt))

            def ps(name, shape, dt=F32):
                return ctx.enter_context(nc.psum_tensor(name + tag, shape, dt))

            def sem(name):
                return ctx.enter_context(nc.semaphore(name + tag))
            return sb, ps, sem

        sb, ps, sem = tensors(whole)
        turns = sem("turns")
        steps = Count(nc.vector, sem("v_steps"))
        iota_made = sem("iota_made")
        w_loaded = sem("w_loaded")
        whole_sem = sem
        iota_col = sb("iota_col", [P, 1])
        iota_row = sb("iota_row", [P, P])
        ident = sb("ident", [P, P])
        ident_b = sb("ident_b", [P, P], BF16)
        below = sb("below", [P, P])
        above = sb("above", [P, P])
        ones = sb("ones", [P, P])
        tile_ids = sb("tile_ids", [1, LTILES, BLOCK // GROUP], I32)
        iota_block = sb("iota_block", [P, BLOCK])
        one_up = sb("one_up", [P, 1])
        node = sb("node", [P, TILES])
        node_i = sb("node_i", [P, TILES], I32)
        degree = [sb(f"degree{k}", [P, TILES]) for k in range(2)]
        slow = [sb(f"slow{k}", [P, 1]) for k in range(2)]
        start = [sb(f"start{k}", [P, TILES]) for k in range(2)]
        row_info = [sb(f"row_info{k}", [P, LTILES, 4], I32) for k in range(2)]
        tile_info = [sb(f"tile_info{k}", [1, 4 * LTILES + 4], I32) for k in range(2)]
        G_OFF, N_BLOCKS, B_OFF, QUICK_OFF, BODIES, SLOW = (
            0, LTILES, 2 * LTILES, 3 * LTILES, 4 * LTILES, 4 * LTILES + 1)

        lists = ExitStack()
        lsb, _, _ = tensors(lists)
        record = [lsb(f"record{k}", [P, TILES, RECORD[k]], I32) for k in range(2)]
        load = [degree[0], lsb("load1", [P, TILES])]
        fast = lsb("fast", [P, 1])
        higher_0 = lsb("higher_0", [P, QUARTERS, TILES])
        keys = ExitStack()
        ksb, _, _ = tensors(keys)
        ends_i = [ksb(f"ends_i{k}", [P, CHUNKS + SUB], I32) for k in range(2)]
        lo = [ksb(f"lo{k}", [P, CHUNKS + SUB]) for k in range(2)]
        hi = [ksb(f"hi{k}", [P, CHUNKS + SUB]) for k in range(2)]
        lo_b = [ksb(f"lo_b{k}", [P, CHUNKS + SUB], BF16) for k in range(2)]
        hi_b = [ksb(f"hi_b{k}", [P, CHUNKS + SUB], BF16) for k in range(2)]

        with ExitStack() as ctx:
            sb, ps, sem = tensors(ctx)
            iota_i = sb("iota_i", [P, P], I32)
            iota_ci = sb("iota_ci", [P, 1], I32)
            digit_i = sb("digit_i", [P, CHUNKS + SUB], I32)
            zeros_b = sb("zeros_b", [P, P], BF16)
            one_lo = [[sb(f"h_lo{k}{p}", [P, SUB, P], BF16) for p in range(2)] for k in range(2)]
            one_hi = [[sb(f"h_hi{k}{p}", [P, SUB, TILES], BF16) for p in range(2)] for k in range(2)]
            total = [sb(f"total{k}", [P, TILES]) for k in range(2)]
            upto = [sb(f"upto{k}", [P, TILES]) for k in range(2)]
            hist = [ps(f"hist{k}", [P, TILES]) for k in range(2)]
            within = [ps(f"within{k}", [P, TILES]) for k in range(2)]
            totals = [ps(f"totals{k}", [P, TILES]) for k in range(2)]
            pads_set = sem("pads_set")
            ends_loaded = [sem(f"ends_loaded{k}") for k in range(2)]
            nbrs_copied = sem("nbrs_copied")
            digits_made = sem("digits_made")
            ones_made = [sem(f"h_ones_made{k}") for k in range(2)]
            hist_did = [sem(f"hist_did{k}") for k in range(2)]
            hist_out = sem("hist_out")
            prefix_did = sem("prefix_did")
            block = ctx.enter_context(nc.Block())

            @block.sync
            def _(sp):
                sp.wait_ge(pads_set, 2)
                for k, ends in enumerate((src_in, dst_in)):
                    sp.dma_start(ends_i[k][0:FULL_PARTS, 0:CHUNKS],
                                 ends[0:FULL_PARTS * CHUNKS].rearrange("(p c) -> p c", c=CHUNKS)
                                 ).then_inc(ends_loaded[k], 16)
                    sp.dma_start(ends_i[k][FULL_PARTS:P, 0:REST],
                                 ends[FULL_PARTS * CHUNKS:EDGES].rearrange("(p c) -> p c", p=1)
                                 ).then_inc(ends_loaded[k], 16)
                sp.wait_ge(ends_loaded[0], 32)
                sp.dma_start(nbrs[1].rearrange("(p c) o -> p (c o)", p=P),
                             ends_i[0][:, 0:CHUNKS]).then_inc(nbrs_copied, 16)
                sp.wait_ge(nbrs_copied, 16)

            @block.gpsimd
            def _(pool):
                pool.iota(iota_i[:, :], [[1, P]], base=0, channel_multiplier=0).then_inc(iota_made, 1)
                pool.iota(iota_ci[:, :], [[1, 1]], base=0, channel_multiplier=1).then_inc(iota_made, 1)
                pool.iota(tile_ids[:, :, :], [[1, LTILES], [0, BLOCK // GROUP]], base=0,
                          channel_multiplier=0).then_inc(iota_made, 1)

            @block.vector
            def _(dve):
                own = steps.of(dve)
                for k in range(2):
                    dve.memset(ends_i[k][:, :], PAD_NODE).then_inc(pads_set, 1)
                dve.wait_ge(iota_made, 3)
                own.did(dve.tensor_copy(iota_row[:, :], iota_i[:, :]))
                own.did(dve.tensor_copy(iota_col[:, :], iota_ci[:, :]))
                own.did(dve.memset(ones[:, :], 1.0))
                own.did(dve.memset(zeros_b[:, :], 0.0))
                own.wait()
                own.did(dve.tensor_scalar(ident[:, :], iota_row[:, :], iota_col[:, :], None, ALU.is_equal))
                own.did(dve.tensor_scalar(ident_b[:, :], iota_row[:, :], iota_col[:, :], None, ALU.is_equal))
                own.did(dve.tensor_scalar(below[:, :], iota_row[:, :], iota_col[:, :], None, ALU.is_lt))
                own.did(dve.tensor_scalar(above[:, :], iota_row[:, :], iota_col[:, :], None, ALU.is_gt))
                for k in range(2):
                    dve.wait_ge(ends_loaded[k], 32)
                    own.wait()
                    own.did(dve.tensor_scalar(digit_i[:, :], ends_i[k][:, :], P - 1, None, ALU.bitwise_and))
                    own.wait()
                    own.did(dve.tensor_copy(lo[k][:, :], digit_i[:, :]))
                    own.did(dve.tensor_copy(lo_b[k][:, :], digit_i[:, :]))
                    own.wait()
                    own.did(dve.tensor_scalar(digit_i[:, :], ends_i[k][:, :], 7, None,
                                              ALU.arith_shift_right))
                    own.wait()
                    own.did(dve.tensor_copy(hi[k][:, :], digit_i[:, :]))
                    own.did(dve.tensor_scalar(hi_b[k][:, :], digit_i[:, :], float(P), None, ALU.mult))
                own.wait()
                dve.sem_inc(digits_made, 1)
                with dve.Fori(0, SUBS // 2) as i:
                    for p in range(2):
                        for k in range(2):
                            dve.wait_ge(hist_did[k], i * 2 + p + 1)
                            dve.tensor_tensor(
                                one_lo[k][p][:, :, :],
                                bc(lo[k][:, bass.ds((i * 2 + p) * SUB, SUB)].unsqueeze(2), [P, SUB, P]),
                                bc(iota_row[:, :].unsqueeze(1), [P, SUB, P]), ALU.is_equal)
                            dve.tensor_tensor(
                                one_hi[k][p][:, :, :],
                                bc(hi[k][:, bass.ds((i * 2 + p) * SUB, SUB)].unsqueeze(2), [P, SUB, TILES]),
                                bc(iota_row[:, 0:TILES].unsqueeze(1), [P, SUB, TILES]),
                                ALU.is_equal).then_inc(ones_made[k], 1)
                for k in range(2):
                    dve.wait_ge(hist_did[k], SUBS + 3)
                    own.did(dve.tensor_copy(degree[k][:, :], hist[k][:, :]))
                    own.wait()
                    dve.sem_inc(hist_out, 1)
                    dve.wait_ge(prefix_did, 2 * k + 2)
                    own.did(dve.tensor_copy(total[k][:, :], totals[k][:, :]))
                    own.wait()
                    own.did(dve.tensor_tensor_scan(upto[k][:, :], bc(ones[:, 0:1], [P, TILES]), total[k][:, :],
                                                   0.0, ALU.mult, ALU.add))
                    own.wait()
                    own.did(dve.tensor_tensor(upto[k][:, :], upto[k][:, :], total[k][:, :], ALU.subtract))
                    own.wait()
                    own.did(dve.tensor_tensor(start[k][:, :], upto[k][:, :], within[k][:, :], ALU.add))
                own.wait()

            @block.tensor
            def _(pe):
                pe.wait_ge(digits_made, 1)
                for k in range(2):
                    pe.matmul(hist[k][:, :], zeros_b[:, :], zeros_b[:, 0:TILES], start=True,
                              stop=False).then_inc(hist_did[k], 1)
                    pe.matmul(hist[k][:, :], zeros_b[:, :], zeros_b[:, 0:TILES], start=False,
                              stop=False).then_inc(hist_did[k], 1)
                with pe.Fori(0, SUBS // 2) as i:
                    for p in range(2):
                        for k in range(2):
                            pe.wait_ge(ones_made[k], i * 2 + p + 1)
                            for c in range(SUB):
                                last = pe.matmul(hist[k][:, :], one_lo[k][p][:, c, :], one_hi[k][p][:, c, :],
                                                 start=False, stop=False)
                            last.then_inc(hist_did[k], 1)
                for k in range(2):
                    pe.matmul(hist[k][:, :], zeros_b[:, :], zeros_b[:, 0:TILES], start=False,
                              stop=True).then_inc(hist_did[k], 1)
                for k in range(2):
                    pe.wait_ge(hist_out, k + 1)
                    pe.matmul(within[k][:, :], above[:, :], degree[k][:, :], start=True,
                              stop=True).then_inc(prefix_did, 1)
                    pe.matmul(totals[k][:, :], ones[:, :], degree[k][:, :], start=True,
                              stop=True).then_inc(prefix_did, 1)

        def halves(t):
            return ((0, t, HEAD), (1, t + HEAD, TAIL))

        keys_made = whole_sem("keys_made")
        keys_staged = [whole_sem(f"keys_staged{q}") for q in range(2)]
        rows_made = [whole_sem(f"rows_made{q}") for q in range(2)]
        rows_copied = [whole_sem(f"rows_copied{q}") for q in range(2)]

        def stage_keys(pool, k, key, key_stage):
            pool.wait_ge(keys_made, k + 1)
            with pool.Fori(0, PASSES) as i:
                for q, t, n in halves(i * PASS):
                    pool.wait_ge(rows_made[q], i + (k * PASSES + 1))
                    pool.tensor_copy(key_stage[q][:, 0:n], key[:, bass.ds(t, n)]).then_inc(keys_staged[q], 1)

        def spread_keys(pe, k, key_stage, spread_out):
            if k == 0:
                for q in range(2):
                    pe.sem_inc(rows_made[q], 1)
            with pe.Fori(0, PASSES) as i:
                for q, t, n in halves(i * PASS):
                    pe.wait_ge(keys_staged[q], i + (k * PASSES + 1))
                    pe.wait_ge(rows_copied[q], i + (k * PASSES + 1))
                    for c in range(n):
                        last = pe.matmul(spread_out[q][:, c, :], bc(key_stage[q][:, c:c + 1], [P, P]),
                                         ident[:, :], start=True, stop=True)
                    last.then_inc(rows_made[q], 1)

        def copy_keys(act, k, spread_out, key_row):
            if k == 0:
                for q in range(2):
                    act.sem_inc(rows_copied[q], 1)
            with act.Fori(0, PASSES) as i:
                for q, t, n in halves(i * PASS):
                    act.wait_ge(rows_made[q], i + (k * PASSES + 2))
                    act.copy(key_row[:, bass.ds(t * P, n * P)],
                             spread_out[q][:, 0:n, :].rearrange("p c m -> p (c m)")
                             ).then_inc(rows_copied[q], 1)
            for q in range(2):
                act.wait_ge(rows_copied[q], k * PASSES + PASSES + 1)

        def make_key(dve, own, key, k):
            own.did(dve.tensor_scalar(key[:, :], load[k][:, :], float(DEG_CAP), float(KEY_STEP),
                                      ALU.min, ALU.mult))
            own.wait()
            own.did(dve.tensor_tensor(key[:, :], key[:, :], node[:, :], ALU.add))
            own.wait()

        key_row_0 = ksb("key_row_0", [P, NODES_PAD])
        minus_key_0 = ksb("minus_key_0", [P, TILES])

        with ExitStack() as ctx:
            sb, ps, sem = tensors(ctx)
            iota_i = sb("n_iota_i", [P, BLOCK], I32)
            real = sb("n_real", [P, TILES])
            most = [sb(f"n_most{k}", [P, 1]) for k in range(2)]
            key = sb("n_key", [P, TILES])
            key_stage = [sb(f"n_key_stage{q}", [P, HEAD]) for q in range(2)]
            spread_out = [ps(f"n_spread_out{q}", [P, HEAD, P]) for q in range(2)]
            all_most = ps("n_all_most", [P, P])
            most_made = sem("n_most_made")
            most_spread = sem("n_most_spread")
            block = ctx.enter_context(nc.Block())

            @block.gpsimd
            def _(pool):
                pool.iota(node_i[:, :], [[P, TILES]], base=0, channel_multiplier=1).then_inc(iota_made, 1)
                pool.iota(iota_i[:, :], [[1, BLOCK]], base=0, channel_multiplier=0).then_inc(iota_made, 1)
                stage_keys(pool, 0, key, key_stage)

            @block.tensor
            def _(pe):
                for k in range(2):
                    pe.wait_ge(most_made, k + 1)
                    pe.matmul(all_most[:, :], bc(most[k][:, :], [P, P]), ident[:, :], start=True,
                              stop=True).then_inc(most_spread, 1)
                spread_keys(pe, 0, key_stage, spread_out)

            @block.scalar
            def _(act):
                copy_keys(act, 0, spread_out, key_row_0)

            @block.vector
            def _(dve):
                own = steps.of(dve)
                dve.wait_ge(iota_made, 5)
                own.did(dve.tensor_copy(node[:, :], node_i[:, :]))
                own.did(dve.tensor_copy(iota_block[:, :], iota_i[:, :]))
                own.wait()
                own.did(dve.tensor_scalar(real[:, :], node[:, :], float(NODES), None, ALU.is_lt))
                own.wait()
                for k in range(2):
                    own.did(dve.tensor_tensor(degree[k][:, :], degree[k][:, :], real[:, :], ALU.mult))
                    own.wait()
                    if k == 0:
                        make_key(dve, own, key, 0)
                        dve.sem_inc(keys_made, 1)
                        own.did(dve.tensor_scalar(minus_key_0[:, :], key[:, :], -1.0, None, ALU.mult))
                    own.did(dve.tensor_reduce(most[k][:, :], degree[k][:, :], AX.X, ALU.max))
                    own.wait()
                    dve.sem_inc(most_made, 1)
                    dve.wait_ge(most_spread, k + 1)
                    own.did(dve.tensor_reduce(slow[k][:, :], all_most[:, :], AX.X, ALU.max))
                    own.wait()
                    own.did(dve.tensor_scalar(slow[k][:, :], slow[k][:, :], float(BLOCK), None, ALU.is_gt))
                    own.wait()
                own.did(dve.tensor_scalar(fast[:, :], slow[1][:, :], -1.0, 1.0, ALU.mult, ALU.add))
                for k in range(2):
                    own.did(dve.tensor_copy(record[k][:, :, 0], start[k][:, :]))
                    own.did(dve.tensor_copy(record[k][:, :, 2], node_i[:, :]))
                    own.did(dve.memset(record[k][:, :, 3], 0))
                own.did(dve.tensor_copy(record[0][:, :, 1], load[0][:, :]))
                own.wait()

        def sort(k):
            with ExitStack() as ctx:
                sb, ps, sem = tensors(ctx, f"_{k}")
                one_lo = [sb(f"s_lo{p}", [P, SUB, P], BF16) for p in range(2)]
                one_hi = [sb(f"s_hi{p}", [P, SUB, TILES], BF16) for p in range(2)]
                one_lo_t = [sb(f"s_lo_t{p}", [P, SUB, P]) for p in range(2)]
                equal = sb("s_equal", [P, SUB, P], BF16)
                before = [sb(f"s_before{p}", [P, SUB]) for p in range(2)]
                next_sb = [sb(f"s_next{p}", [P, SUB + 1, TILES]) for p in range(2)]
                picked = sb("s_picked", [P, SUB, TILES])
                base = sb("s_base", [P, SUB])
                place = [sb(f"s_place{p}", [P, SUB], I32) for p in range(2)]
                other = [sb(f"s_other{p}", [P, SUB], I32) for p in range(2)]
                key_row = ps("s_key_row", [P, SUB, P])
                lo_row = ps("s_lo_row", [P, SUB, P])
                fetched = sb("n_fetched", [P, TILES, BLOCK], I32)
                valid = sb("n_valid", [P, BLOCK])
                work = [sb(f"n_work{p}", [P, BLOCK]) for p in range(2)]
                top = sb("n_top", [P, BLOCK])
                digit_i = sb("n_digit_i", [P, BLOCK], I32)
                masked_i = sb("n_masked_i", [P, BLOCK], I32)
                again = sb("n_again", [P, BLOCK])
                empty = sb("n_empty", [P, BLOCK])
                counted = sb("n_counted", [P, BLOCK])
                hi_of = sb("n_hi_of", [P, TILES, BLOCK], BF16)
                lo_of = sb("n_lo_of", [P, TILES, BLOCK], BF16)
                here = [sb(f"n_here{m}", [P, TILES, BLOCK >> max(m - 1, 0)], BF16) for m in range(4)]
                picked_rows = sb("n_picked_rows", [P, TILES], BF16)
                compared = sb("n_compared", [P, QUARTER], BF16)
                next_free = ps("s_next_free", [P, SUB + 1, TILES])
                list_did = sem("n_list_did")
                signs_summed = sem("n_signs_summed")
                block_fetched = sem("n_block_fetched")
                looked = [ps(f"s_looked{p}", [P, SUB, TILES]) for p in range(2)]
                rows_made = sem("s_rows_made")
                rows_used = sem("s_rows_used")
                ones_made = sem("s_ones_made")
                next_updated = sem("s_next_updated")
                next_copied = sem("s_next_copied")
                looked_up = sem("s_looked_up")
                looked_free = sem("s_looked_free")
                place_made = sem("s_place_made")
                scattered = [sem(f"s_scattered{p}") for p in range(2)]
                block = ctx.enter_context(nc.Block())

                @block.tensor
                def _(pe):
                    def rows(b):
                        for c in range(SUB):
                            col = bass.ds(b * SUB + c, 1)
                            lo_of, hi_of = bc(lo_b[k][:, col], [P, P]), bc(hi_b[k][:, col], [P, P])
                            pe.matmul(lo_row[:, c, :], lo_of, ident_b[:, :], start=True, stop=True)
                            pe.matmul(key_row[:, c, :], lo_of, ident_b[:, :], start=True, stop=False)
                            last = pe.matmul(key_row[:, c, :], hi_of, ident_b[:, :], start=False, stop=True)
                        last.then_inc(rows_made, 1)

                    pe.sem_inc(looked_up, 2)
                    pe.sem_inc(next_updated, 1)
                    rows(0)
                    with pe.Fori(0, SUBS // 2) as i:
                        for p in range(2):
                            b = i * 2 + p
                            pe.wait_ge(next_copied, b + 1)
                            pe.wait_ge(ones_made, b + 1)
                            pe.matmul(next_free[:, :, :], ident[:, :],
                                      bc(next_sb[1 - p][:, SUB:SUB + 1, :], [P, SUB + 1, TILES]),
                                      start=True, stop=True)
                            for c in range(SUB):
                                last = pe.matmul(next_free[:, c + 1:SUB + 1, :], one_lo[p][:, c, :],
                                                 bc(one_hi[p][:, c:c + 1, :], [P, SUB - c, TILES]),
                                                 start=False, stop=True, skip_group_check=True)
                            last.then_inc(next_updated, 1)
                            pe.wait_ge(rows_used, b + 1)
                            rows(b + 1)
                            pe.wait_ge(next_copied, b + 2)
                            pe.wait_ge(looked_free, b + 1)
                            for c in range(SUB):
                                last = pe.matmul(looked[p][:, c, :], one_lo_t[p][:, c, :], next_sb[p][:, c, :],
                                                 start=True, stop=True)
                            last.then_inc(looked_up, 1)

                @block.scalar
                def _(act):
                    act.copy(next_sb[1][:, SUB, :], start[k][:, :]).then_inc(next_copied, 1)
                    act.sem_inc(signs_summed, 1)
                    with act.Fori(0, TILES) as t:
                        for quarter in range(QUARTERS):
                            p, b = quarter % 2, t * QUARTERS + quarter
                            act.wait_ge(next_updated, b + 2)
                            act.wait_ge(looked_up, b + 1)
                            act.copy(next_sb[p][:, :, :], next_free[:, :, :]).then_inc(next_copied, 1)
                            act.wait_ge(signs_summed, b + 1)
                            act.activation(compared[:, :], key_row_0[:, quarter * QUARTER:(quarter + 1) * QUARTER],
                                           ACT.Sign, bias=minus_key_0[:, bass.ds(t, 1)],
                                           accum_out=higher_0[:, quarter, bass.ds(t, 1)]
                                           ).then_inc(signs_summed, 1)

                @block.vector
                def _(dve):
                    own = steps.of(dve)

                    listed = Count(dve, list_did)

                    def list_round(t, n):
                        if n == 0:
                            listed.did(dve.tensor_scalar(valid[:, :], iota_block[:, :], degree[1][:, bass.ds(t, 1)],
                                                         None, ALU.is_lt))
                            listed.wait()
                            listed.did(dve.scalar_tensor_tensor(work[0][:, :], fetched[:, bass.ds(t, 1), :].squeeze(1),
                                                                1.0, valid[:, :], ALU.add, ALU.mult))
                        m = n % ROUNDS
                        best = top[:, 8 * m:8 * m + 8]
                        listed.wait()
                        turn(dve, turns)
                        listed.did(dve.max(best, work[m % 2][:, :]))
                        listed.wait()
                        if m < ROUNDS - 1:
                            turn(dve, turns)
                            listed.did(dve.match_replace(work[1 - m % 2][:, :], best, work[m % 2][:, :], 0.0))
                        elif n == m:
                            split_list(t)
                        else:
                            listed.did(dve.tensor_scalar(empty[:, :], top[:, :], 0.0, float(ZERO_ROW + 1),
                                                         ALU.is_equal, ALU.mult))
                            listed.wait()
                            listed.did(dve.scalar_tensor_tensor(
                                record[1][:, bass.ds(t, 1), INFO:INFO + BLOCK].squeeze(1), top[:, :], -1.0,
                                empty[:, :], ALU.add, ALU.add))

                    def split_list(t):
                        of_t = bass.ds(t, 1)
                        listed.did(dve.tensor_scalar(digit_i[:, :], top[:, :], -1.0, None, ALU.add))
                        listed.wait()
                        listed.did(dve.tensor_scalar(masked_i[:, :], digit_i[:, :], P - 1, None, ALU.bitwise_and))
                        listed.did(dve.tensor_scalar(digit_i[:, :], digit_i[:, :], 7, None, ALU.arith_shift_right))
                        listed.wait()
                        listed.did(dve.tensor_scalar(lo_of[:, of_t, :].squeeze(1), masked_i[:, :], 1.0, None, ALU.add))
                        listed.did(dve.tensor_copy(hi_of[:, of_t, :].squeeze(1), digit_i[:, :]))
                        listed.did(dve.tensor_tensor(again[:, 1:BLOCK], digit_i[:, 1:BLOCK],
                                                     digit_i[:, 0:BLOCK - 1], ALU.is_equal))
                        listed.wait()
                        listed.did(dve.tensor_tensor(work[0][:, :], again[:, :], top[:, :], ALU.mult))
                        listed.wait()
                        listed.did(dve.tensor_scalar(counted[:, :], work[0][:, :], 0.0, 0.0, ALU.is_gt, ALU.add,
                                                     accum_out=load[1][:, of_t]))

                    def pick_step(s, n):
                        if n % 3 == 0 and n < 15:
                            listed.wait()
                        if n == 0:
                            listed.did(dve.tensor_scalar(here[0][:, :, :], hi_of[:, :, :], iota_row[:, bass.ds(s, 1)],
                                                         None, ALU.is_equal))
                        elif n == 3:
                            listed.did(dve.tensor_tensor(here[1][:, :, :], here[0][:, :, :], lo_of[:, :, :],
                                                         ALU.mult))
                        elif n == 6 or n == 9:
                            m, width = n // 3 - 1, BLOCK >> (n // 3 - 1)
                            listed.did(dve.tensor_tensor(here[m + 1][:, :, :], here[m][:, :, 0:width],
                                                         here[m][:, :, width:2 * width], ALU.max))
                        elif n == 12:
                            listed.did(dve.tensor_reduce(
                                record[1][:, :, bass.ds(s + (INFO + BLOCK), 1)].squeeze(2), here[3][:, :, :],
                                AX.X, ALU.max))

                    def build(b, p, beside=None):
                        col = bass.ds(b * SUB, SUB)
                        dve.tensor_tensor(one_lo[p][:, :, :], bc(lo[k][:, col].unsqueeze(2), [P, SUB, P]),
                                          bc(iota_row[:, :].unsqueeze(1), [P, SUB, P]), ALU.is_equal)
                        dve.tensor_tensor(one_hi[p][:, :, :], bc(hi[k][:, col].unsqueeze(2), [P, SUB, TILES]),
                                          bc(iota_row[:, 0:TILES].unsqueeze(1), [P, SUB, TILES]), ALU.is_equal)
                        dve.wait_ge(rows_made, b + 1)
                        dve.tensor_scalar(one_lo_t[p][:, :, :], lo_row[:, :, :], iota_col[:, :], None,
                                          ALU.is_equal).then_inc(ones_made, 1)
                        for c in range(SUB):
                            last = dve.scalar_tensor_tensor(
                                equal[:, c, :], key_row[:, c, :], key_f[:, bass.ds(b * SUB + c, 1)], below[:, :],
                                ALU.is_equal, ALU.mult, accum_out=before[p][:, c:c + 1])
                            if c == SUB - 1:
                                last.then_inc(rows_used, 1)
                            if beside:
                                beside(c)

                    def finish(b, i, p):
                        dve.wait_ge(looked_up, b + 3)
                        own.wait()
                        own.did(dve.tensor_tensor(picked[:, :, :], looked[p][:, :, :], one_hi[p][:, :, :],
                                                  ALU.mult))
                        own.wait()
                        dve.sem_inc(looked_free, 1)
                        own.did(dve.tensor_reduce(base[:, :], picked[:, :, :], AX.X, ALU.add))
                        own.wait()
                        dve.wait_ge(scattered[p], i * (SUB * 16))
                        dve.wait_ge(rows_used, b + 1)
                        own.did(dve.tensor_tensor(place[p][:, :], base[:, :], before[p][:, :], ALU.add))
                        own.did(dve.tensor_copy(other[p][:, :], ends_i[1 - k][:, bass.ds(b * SUB, SUB)]))
                        own.wait()
                        dve.sem_inc(place_made, 1)

                    key_f = sb_key
                    own.did(dve.scalar_tensor_tensor(key_f[:, :], hi[k][:, :], float(P), lo[k][:, :],
                                                     ALU.mult, ALU.add))
                    own.wait()
                    dve.sem_inc(looked_free, 2)
                    build(0, 0)
                    listed.did(dve.memset(again[:, 0:1], 0.0))
                    dve.wait_ge(block_fetched, TILES * 16)
                    for first, step, count in ((0, list_round, LIST_STEPS), (TILES, pick_step, 5)):
                        with dve.Fori(0, TILES) as t:
                            i = t + first
                            own.enter(t, 8)
                            listed.enter(t, count)
                            for p in range(2):
                                b = i * 2 + p
                                dve.wait_ge(next_updated, b + 1)
                                build(b + 1, 1 - p, lambda c: step(t, p * SUB + c))
                                finish(b, i, p)
                            own.leave(TILES)
                            listed.leave(TILES)
                    listed.wait()
                    picks_of = record[1][:, :, INFO + BLOCK:RECORD[1]]
                    own.did(dve.tensor_scalar(picks_of, picks_of, fast[:, :], None, ALU.mult))
                    own.did(dve.tensor_scalar(load[1][:, :], load[1][:, :], fast[:, :], None, ALU.mult))
                    own.wait()
                    own.did(dve.scalar_tensor_tensor(load[1][:, :], degree[1][:, :], slow[1][:, :], load[1][:, :],
                                                     ALU.mult, ALU.add))
                    own.wait()
                    own.did(dve.tensor_copy(record[1][:, :, 1], load[1][:, :]))

                @block.gpsimd
                def _(pool):
                    for t in range(TILES):
                        pool.indirect_dma_start(fetched[:, t, :], None, nbrs[1],
                                                bass.IndirectOffsetOnAxis(record[1][:, t, 0:1], 0)
                                                ).then_inc(block_fetched, 16)
                    with pool.Fori(0, SUBS // 2) as i:
                        for p in range(2):
                            pool.wait_ge(place_made, i * 2 + p + 1)
                            turn(pool, turns)
                            for c in range(SUB):
                                pool.indirect_dma_start(
                                    nbrs[k], bass.IndirectOffsetOnAxis(place[p][:, c:c + 1], 0),
                                    other[p][:, c:c + 1], None).then_inc(scattered[p], 16)
                    for p in range(2):
                        pool.wait_ge(scattered[p], SUBS // 2 * SUB * 16)

        sb_key = ksb("s_key_f", [P, CHUNKS + SUB])
        sort(0)
        keys.close()

        def rstd_steps(dve, own, stats, mean, spread, rstd):
            own.wait()
            own.did(dve.tensor_tensor(mean[:, :], stats[:, :, 1], stats[:, :, 4], ALU.add))
            own.did(dve.tensor_tensor(spread[:, :], stats[:, :, 1], stats[:, :, 4], ALU.subtract))
            own.did(dve.tensor_tensor(rstd[:, :], stats[:, :, 2], stats[:, :, 5], ALU.add))
            own.wait()
            own.did(dve.tensor_scalar(mean[:, :], mean[:, :], 0.5, None, ALU.mult))
            own.did(dve.tensor_tensor(spread[:, :], spread[:, :], spread[:, :], ALU.mult))
            own.did(dve.tensor_scalar(rstd[:, :], rstd[:, :], 1.0 / D, 1e-5, ALU.mult, ALU.add))
            own.wait()
            own.did(dve.scalar_tensor_tensor(rstd[:, :], spread[:, :], 0.25, rstd[:, :], ALU.mult, ALU.add))
            own.wait()

        with ExitStack() as ctx:
            sb, ps, sem = tensors(ctx)
            x = sb("f_x", [P, TILES, D])
            h = sb("f_h", [P, TILES, D])
            ab = sb("f_ab", [P, TILES, 2 * D])
            w1 = sb("f_w1", [P, 2 * D])
            b1 = sb("f_b1", [1, 2 * D])
            stats = sb("f_stats", [P, TILES, 6])
            mean = sb("f_mean", [P, TILES])
            spread = sb("f_spread", [P, TILES])
            rstd = sb("f_rstd", [P, TILES])
            one_cols = sb("f_one_cols", [P, TILES, W0 - 2 * D])
            zero_rows = sb("f_zero_rows", [P, W0])
            h_stage = [sb(f"f_h_stage{q}", [P, HEAD, D]) for q in range(2)]
            h_t = [sb(f"f_h_t{q}", [P, HEAD, D]) for q in range(2)]
            turned = [ps(f"f_turned{q}", [P, HEAD, D]) for q in range(2)]
            product = [ps(f"f_product{q}", [P, HEAD, 2 * D]) for q in range(2)]
            x_clear = sem("f_x_clear")
            x_loaded = sem("f_x_loaded")
            var_made = sem("f_var_made")
            std_made = sem("f_std_made")
            centred = sem("f_centred")
            h_made = sem("f_h_made")
            h_staged = [sem(f"f_h_staged{q}") for q in range(2)]
            h_turned = [sem(f"f_h_turned{q}") for q in range(2)]
            h_copied = [sem(f"f_h_copied{q}") for q in range(2)]
            ab_made = [sem(f"f_ab_made{q}") for q in range(2)]
            ab_copied = [sem(f"f_ab_copied{q}") for q in range(2)]
            pads_made = sem("f_pads_made")
            stored = sem("f_stored")
            block = ctx.enter_context(nc.Block())

            def by_node(ap):
                return ap[0:NODES_PAD, :].rearrange("(t p) f -> p t f", p=P)

            @block.sync
            def _(sp):
                sp.dma_start(w1[:, 0:D], w1_in[0:D, :]).then_inc(w_loaded, 16)
                sp.dma_start(w1[:, D:2 * D], w1_in[D:2 * D, :]).then_inc(w_loaded, 16)
                sp.dma_start(x[:, 0:TILES - 1, :],
                             x_in[0:(TILES - 1) * P, :].rearrange("(t p) f -> p t f", p=P)
                             ).then_inc(x_loaded, 16)
                sp.wait_ge(x_clear, 2)
                sp.dma_start(x[0:LAST_ROWS, TILES - 1, :], x_in[(TILES - 1) * P:NODES, :]).then_inc(x_loaded, 16)
                sp.dma_start(b1[0:1, 0:D], b1_in.rearrange("(o n) -> o n", o=1)).then_inc(w_loaded, 16)
                sp.wait_ge(x_loaded, 32)
                sp.dma_start(by_node(own0)[:, :, 2 * D:3 * D], x[:, :, :]).then_inc(stored, 16)
                sp.wait_ge(pads_made, 2)
                sp.dma_start(by_node(table0)[:, :, 2 * D:W0], one_cols[:, :, :]).then_inc(stored, 16)
                sp.dma_start(table0[NODES_PAD:TABLE_ROWS, :], zero_rows[:, :]).then_inc(stored, 16)
                sp.dma_start(table1[NODES_PAD:TABLE_ROWS, :], zero_rows[:, 0:D]).then_inc(stored, 16)
                sp.wait_ge(h_made, 1)
                sp.dma_start(by_node(own0)[:, :, D:2 * D], h[:, :, :]).then_inc(stored, 16)
                sp.dma_start(by_node(table0)[:, :, D:2 * D], h[:, :, :]).then_inc(stored, 16)
                for q in range(2):
                    sp.wait_ge(ab_copied[q], PASSES)
                sp.dma_start(by_node(own0)[:, :, 0:D], ab[:, :, 0:D]).then_inc(stored, 16)
                sp.dma_start(by_node(table0)[:, :, 0:D], ab[:, :, D:2 * D]).then_inc(stored, 16)
                sp.wait_ge(stored, 8 * 16)

            @block.scalar
            def _(act):
                act.wait_ge(var_made, 1)
                act.sqrt(rstd[:, :], rstd[:, :]).then_inc(std_made, 1)
                act.wait_ge(centred, 1)
                act.activation(h[:, :, :], h[:, :, :], ACT.Relu).then_inc(h_made, 1)
                with act.Fori(0, PASSES) as i:
                    for q, _, n in halves(0):
                        act.wait_ge(h_turned[q], i + 1)
                        act.wait_ge(ab_made[q], i)
                        act.copy(h_t[q][:, 0:n, :], turned[q][:, 0:n, :]).then_inc(h_copied[q], 1)

            @block.gpsimd
            def _(pool):
                pool.wait_ge(h_made, 1)
                with pool.Fori(0, PASSES) as i:
                    for q, t, n in halves(i * PASS):
                        pool.wait_ge(h_turned[q], i)
                        pool.tensor_copy(h_stage[q][:, 0:n, :], h[:, bass.ds(t, n), :]).then_inc(h_staged[q], 1)

            @block.tensor
            def _(pe):
                pe.wait_ge(w_loaded, 3 * 16)
                with pe.Fori(0, PASSES) as i:
                    for q, t, n in halves(i * PASS):
                        pe.wait_ge(h_staged[q], i + 1)
                        pe.wait_ge(h_copied[q], i)
                        for c in range(n):
                            last = pe.transpose(turned[q][:, c, :], h_stage[q][:, c, :], ident[:, :])
                        last.then_inc(h_turned[q], 1)
                    for q, t, n in halves(i * PASS):
                        pe.wait_ge(h_copied[q], i + 1)
                        pe.wait_ge(ab_copied[q], i)
                        for c in range(n):
                            pe.matmul(product[q][:, c, :], h_t[q][:, c, :], w1[:, :], start=True, stop=False)
                            last = pe.matmul(product[q][:, c, :], ones[0:1, :], b1[0:1, :], start=False,
                                             stop=True)
                        last.then_inc(ab_made[q], 1)

            @block.vector
            def _(dve):
                own = steps.of(dve)
                dve.memset(x[:, TILES - 1, :], 0.0).then_inc(x_clear, 1)
                dve.memset(b1[:, :], 0.0).then_inc(x_clear, 1)
                own.did(dve.memset(one_cols[:, :, :], 0.0))
                own.wait()
                dve.memset(one_cols[:, :, 0:1], 1.0).then_inc(pads_made, 1)
                dve.memset(zero_rows[:, :], 0.0).then_inc(pads_made, 1)
                dve.wait_ge(x_loaded, 32)
                with dve.Fori(0, TILES) as t:
                    own.enter(t, 1)
                    own.did(dve.bn_stats(stats[:, bass.ds(t, 1), :].squeeze(1), x[:, bass.ds(t, 1), :].squeeze(1)))
                    own.leave(TILES)
                rstd_steps(dve, own, stats, mean, spread, rstd)
                dve.sem_inc(var_made, 1)
                dve.wait_ge(std_made, 1)
                own.did(dve.reciprocal(rstd[:, :], rstd[:, :]))
                own.did(dve.tensor_tensor(h[:, :, :], x[:, :, :], bc(mean[:, :].unsqueeze(2), [P, TILES, D]),
                                          ALU.subtract))
                own.wait()
                dve.tensor_tensor(h[:, :, :], h[:, :, :], bc(rstd[:, :].unsqueeze(2), [P, TILES, D]),
                                  ALU.mult).then_inc(centred, 1)
                with dve.Fori(0, PASSES) as i:
                    for q, t, n in halves(i * PASS):
                        dve.wait_ge(ab_made[q], i + 1)
                        dve.tensor_copy(ab[:, bass.ds(t, n), :], product[q][:, 0:n, :]).then_inc(ab_copied[q], 1)

        in_order = ExitStack()
        osb, _, _ = tensors(in_order)
        row_lists = [osb(f"row_lists{k}", [P, TILES, BLOCK], I32) for k in range(2)]
        row_picks = osb("row_picks", [P, TILES, TILES], I32)

        with ExitStack() as ctx:
            sb, ps, sem = tensors(ctx)
            key = sb("r_key", [P, TILES])
            minus_key = sb("r_minus_key", [P, TILES])
            key_row = sb("r_key_row", [P, NODES_PAD])
            compared = [sb(f"r_compared{m}", [P, NODES_PAD], BF16) for m in range(2)]
            higher = [sb(f"r_higher{m}", [P, TILES]) for m in range(2)]
            rank = [sb(f"r_rank{k}", [P, TILES], I32) for k in range(2)]
            key_stage = [sb(f"r_key_stage{q}", [P, HEAD]) for q in range(2)]
            spread_out = [ps(f"r_spread_out{q}", [P, HEAD, P]) for q in range(2)]
            signs_summed = sem("r_signs_summed")
            ranked = sem("r_ranked")
            recorded = [sem(f"r_recorded{k}") for k in range(2)]
            info_cleared = sem("r_info_cleared")
            info_loaded = [sem(f"r_info_loaded{k}") for k in range(2)]
            block_fetched = sem("r_block_fetched")
            block = ctx.enter_context(nc.Block())
            SHARED = (TILES + 1) // 2

            @block.gpsimd
            def _(pool):
                def scatter_records(k):
                    for t in range(TILES):
                        pool.indirect_dma_start(meta[k], bass.IndirectOffsetOnAxis(rank[k][:, t:t + 1], 0),
                                                record[k][:, t, :], None).then_inc(recorded[k], 16)
                stage_keys(pool, 1, key, key_stage)
                pool.wait_ge(ranked, 1)
                scatter_records(0)
                pool.wait_ge(info_loaded[0], 16)
                for t in range(TILES):
                    pool.indirect_dma_start(row_lists[0][:, t, :], None, nbrs[0],
                                            bass.IndirectOffsetOnAxis(row_info[0][:, t, 0:1], 0)
                                            ).then_inc(block_fetched, 16)
                pool.wait_ge(ranked, 2)
                scatter_records(1)
                pool.wait_ge(block_fetched, TILES * 16)

            @block.sync
            def _(sp):
                sp.wait_ge(info_cleared, 1)
                for k in range(2):
                    sp.wait_ge(recorded[k], TILES * 16)
                    by_rank = meta[k].rearrange("(t p) c -> p t c", p=P)
                    sp.dma_start(row_info[k][:, 0:TILES, :], by_rank[:, :, 0:INFO]).then_inc(info_loaded[k], 16)
                sp.dma_start(row_lists[1][:, :, :], by_rank[:, :, INFO:INFO + BLOCK]).then_inc(info_loaded[1], 16)
                sp.dma_start(row_picks[:, :, :], by_rank[:, :, INFO + BLOCK:RECORD[1]]).then_inc(info_loaded[1], 16)
                sp.wait_ge(info_loaded[1], 48)

            @block.tensor
            def _(pe):
                spread_keys(pe, 1, key_stage, spread_out)

            @block.scalar
            def _(act):
                copy_keys(act, 1, spread_out, key_row)
                act.sem_inc(signs_summed, 1)
                with act.Fori(SHARED, TILES) as t:
                    act.wait_ge(signs_summed, t - SHARED + 1)
                    act.activation(compared[0][:, :], key_row[:, :], ACT.Sign, bias=minus_key[:, bass.ds(t, 1)],
                                   accum_out=higher[0][:, bass.ds(t, 1)]).then_inc(signs_summed, 1)

            @block.vector
            def _(dve):
                own = steps.of(dve)
                own.did(dve.tensor_reduce(higher[1][:, :], higher_0[:, :, :].rearrange("p q t -> p t q"), AX.X,
                                          ALU.add))
                for k in range(2):
                    own.did(dve.memset(row_info[k][:, :, :], 0))
                make_key(dve, own, key, 1)
                own.did(dve.tensor_scalar(minus_key[:, :], key[:, :], -1.0, None, ALU.mult))
                own.did(dve.tensor_scalar(rank[0][:, :], higher[1][:, :], float(NODES_PAD - 1), 0.5,
                                          ALU.add, ALU.mult))
                own.wait()
                dve.sem_inc(info_cleared, 1)
                dve.sem_inc(keys_made, 1)
                dve.sem_inc(ranked, 1)
                for q in range(2):
                    dve.wait_ge(rows_copied[q], 2 * PASSES + 1)
                with dve.Fori(0, SHARED) as t:
                    own.enter(t, 1)
                    own.wait()
                    own.did(dve.tensor_scalar(compared[1][:, :], key_row[:, :], key[:, bass.ds(t, 1)], 0.0,
                                              ALU.is_gt, ALU.add, accum_out=higher[1][:, bass.ds(t, 1)]))
                    own.leave(SHARED)
                own.wait()
                own.did(dve.tensor_copy(rank[1][:, 0:SHARED], higher[1][:, 0:SHARED]))
                dve.wait_ge(signs_summed, TILES - SHARED + 1)
                own.did(dve.tensor_scalar(rank[1][:, SHARED:TILES], higher[0][:, SHARED:TILES],
                                          float(NODES_PAD - 1), 0.5, ALU.add, ALU.mult))
                own.wait()
                dve.sem_inc(ranked, 1)

        with ExitStack() as ctx:
            sb, ps, sem = tensors(ctx)
            deg = [sb(f"t_deg{k}", [P, LTILES]) for k in range(2)]
            most = sb("t_most", [LTILES, 1])
            counts_i = sb("t_counts_i", [LTILES, 2], I32)
            counts = [sb(f"t_counts{k}", [LTILES, 2]) for k in range(2)]
            value = sb("t_value", [P, TILES, BLOCK])
            shifted = sb("t_shifted", [P, TILES, BLOCK])
            laid = [sb(f"t_laid{k}", [P, QUICK_SLOTS], I32) for k in range(2)]
            laid_tile = [sb(f"t_laid_tile{k}", [1, QUICK_SLOTS // GROUP], I32) for k in range(2)]
            deg_t = ps("t_deg_t", [LTILES, P])
            sums = ps("t_sums", [1, 4 * LTILES + 4])
            a_did = sem("t_a_did")
            deg_made = sem("t_deg_made")
            deg_turned = sem("t_deg_turned")
            counts_made = sem("t_counts_made")
            sums_made = sem("t_sums_made")
            info_made = sem("t_info_made")
            laid_out = sem("t_laid_out")
            tiles_laid = sem("t_tiles_laid")
            stored = sem("t_stored")
            block = ctx.enter_context(nc.Block())

            @block.sync
            def _(sp):
                sp.wait_ge(laid_out, 1)
                for k in range(2):
                    sp.dma_start(slots[k][:, 0:QUICK_SLOTS], laid[k][:, :]).then_inc(stored, 16)
                    sp.wait_ge(tiles_laid, k + 1)
                    sp.dma_start(slot_tile[k][:, 0:QUICK_SLOTS // GROUP], laid_tile[k][:, :]).then_inc(stored, 16)
                sp.wait_ge(stored, 64)

            @block.tensor
            def _(pe):
                few = slice(0, LTILES)
                for k in range(2):
                    pe.wait_ge(deg_made, k + 1)
                    pe.transpose(deg_t[:, :], deg[k][:, :], ident[:, :]).then_inc(deg_turned, 1)
                    pe.wait_ge(counts_made, k + 1)
                    groups, blocks = counts[k][:, 0:1], counts[k][:, 1:2]
                    pe.matmul(sums[:, G_OFF:G_OFF + LTILES], groups, above[few, few], start=True, stop=True)
                    pe.matmul(sums[:, N_BLOCKS:N_BLOCKS + LTILES], blocks, ident[few, few], start=True, stop=True)
                    pe.matmul(sums[:, B_OFF:B_OFF + LTILES], blocks, above[few, few], start=True, stop=True)
                    pe.matmul(sums[:, QUICK_OFF:QUICK_OFF + LTILES], groups, above[few, few], start=True,
                              stop=True)
                    pe.matmul(sums[:, BODIES:BODIES + 1], groups, ones[few, 0:1], start=True,
                              stop=True).then_inc(sums_made, 1)

            @block.scalar
            def _(act):
                act.sem_inc(a_did, 1)
                for m, k in enumerate((0, 1)):
                    act.wait_ge(info_made, m + 1)
                    with act.Fori(0, TILES) as t:
                        first = act.value_load(tile_info[k][0:1, bass.ds(QUICK_OFF + t, 1)], min_val=0,
                                               max_val=TILES * BLOCK // GROUP)
                        act.wait_ge(a_did, m * TILES + t + 1)
                        act.copy(laid_tile[k][0:1, bass.ds(first, BLOCK // GROUP)],
                                 tile_ids[0:1, bass.ds(t, 1), :].squeeze(1)).then_inc(a_did, 1)
                    act.wait_ge(a_did, (m + 1) * TILES + 1)
                    act.sem_inc(tiles_laid, 1)

            @block.vector
            def _(dve):
                own = steps.of(dve)
                full = [P, TILES, BLOCK]

                def ceil_div(column, by):
                    own.did(dve.tensor_scalar(counts_i[:, column], most[:, :], float(by - 1), None, ALU.add))
                    own.wait()
                    own.did(dve.tensor_scalar(counts_i[:, column], counts_i[:, column], by.bit_length() - 1, None,
                                              ALU.arith_shift_right))
                    own.wait()

                for k in range(2):
                    own.did(dve.memset(laid[k][:, :], ZERO_ROW))
                    own.did(dve.memset(laid_tile[k][:, :], TILES))
                    own.did(dve.tensor_copy(deg[k][:, :], row_info[k][:, :, 1]))
                    own.wait()
                    dve.sem_inc(deg_made, 1)
                    dve.wait_ge(deg_turned, k + 1)
                    own.did(dve.tensor_reduce(most[:, :], deg_t[:, :], AX.X, ALU.max))
                    own.wait()
                    ceil_div(slice(0, 1), GROUP)
                    ceil_div(slice(1, 2), BLOCK)
                    own.did(dve.tensor_copy(counts[k][:, 0:1], counts_i[:, 0:1]))
                    own.did(dve.tensor_scalar(counts[k][:, 1:2], counts_i[:, 1:2], 1.0, None, ALU.max))
                    own.wait()
                    dve.sem_inc(counts_made, 1)
                    dve.wait_ge(sums_made, k + 1)
                    own.did(dve.tensor_copy(tile_info[k][:, 0:BODIES + 1], sums[:, 0:BODIES + 1]))
                    own.did(dve.tensor_copy(tile_info[k][:, SLOW:SLOW + 1], slow[k][0:1, :]))
                    own.wait()
                    quick = tile_info[k][:, QUICK_OFF:QUICK_OFF + LTILES]
                    own.did(dve.tensor_scalar(quick, quick, float(TILES * BLOCK // GROUP), None, ALU.min))
                    total = tile_info[k][:, BODIES:BODIES + 1]
                    own.did(dve.tensor_scalar(total, total, float(GROUPS[k] - 1), None, ALU.add))
                    own.wait()
                    own.did(dve.tensor_scalar(total, total, GROUPS[k].bit_length() - 1, None,
                                              ALU.arith_shift_right))
                    own.wait()
                    if k == 1:
                        own.did(dve.tensor_scalar(total, total, float(TILES), None, ALU.max))
                        own.wait()

                    dve.sem_inc(info_made, 1)
                own.did(dve.tensor_tensor(value[:, :, :], bc(iota_block[:, :].unsqueeze(1), full),
                                          bc(deg[0][:, 0:TILES].unsqueeze(2), full), ALU.is_lt))
                own.wait()
                own.did(dve.scalar_tensor_tensor(shifted[:, :, :], row_lists[0][:, :, :], float(-ZERO_ROW),
                                                 value[:, :, :], ALU.add, ALU.mult))
                own.wait()
                own.did(dve.tensor_scalar(row_lists[0][:, :, :], shifted[:, :, :], float(ZERO_ROW), None, ALU.add))
                own.wait()
                with dve.Fori(0, TILES) as t:
                    own.enter(t, 2)
                    first = [dve.value_load(tile_info[k][0:1, bass.ds(QUICK_OFF + t, 1)], min_val=0,
                                            max_val=TILES * BLOCK // GROUP) for k in range(2)]
                    own.wait()
                    for k in range(2):
                        own.did(dve.tensor_copy(laid[k][:, bass.ds(first[k] * GROUP, BLOCK)],
                                                row_lists[k][:, bass.ds(t, 1), :].squeeze(1)))
                    own.leave(TILES)
                own.wait()
                dve.sem_inc(laid_out, 1)

        with ExitStack() as ctx:
            sb, ps, sem = tensors(ctx)
            picks_b = sb("p_picks_b", [P, TILES, P], BF16)
            turned_b = sb("p_turned_b", [TILES, NODES_PAD], BF16)
            turned = [ps(f"p_turned{q}", [P, HEAD, P], BF16) for q in range(2)]
            ready = sem("p_ready")
            tile_turned = [sem(f"p_tile_turned{q}") for q in range(2)]
            tile_copied = [sem(f"p_tile_copied{q}") for q in range(2)]
            picks_stored = sem("p_picks_stored")
            block = ctx.enter_context(nc.Block())

            @block.tensor
            def _(pe):
                pe.wait_ge(ready, 1)
                with pe.Fori(0, PASSES) as i:
                    for q, t, n in halves(i * PASS):
                        pe.wait_ge(tile_copied[q], i + 1)
                        for c in range(n):
                            last = pe.transpose(turned[q][:, c, :], picks_b[:, bass.ds(t + c, 1), :].squeeze(1),
                                                ident_b[:, :])
                        last.then_inc(tile_turned[q], 1)

            @block.scalar
            def _(act):
                for q in range(2):
                    act.sem_inc(tile_copied[q], 1)
                with act.Fori(0, PASSES) as i:
                    for q, t, n in halves(i * PASS):
                        act.wait_ge(tile_turned[q], i + 1)
                        act.copy(turned_b[:, bass.ds(t * P, n * P)],
                                 turned[q][0:TILES, 0:n, :].rearrange("p c m -> p (c m)")).then_inc(tile_copied[q], 1)
                for q in range(2):
                    act.wait_ge(tile_copied[q], PASSES + 1)
                act.dma_start(picks[:, :], turned_b[:, :]).then_inc(picks_stored, 16)
                act.wait_ge(picks_stored, 16)

            @block.vector
            def _(dve):
                own = steps.of(dve)
                own.did(dve.memset(picks_b[:, :, :], 0.0))
                own.wait()
                own.did(dve.tensor_copy(picks_b[:, :, 0:TILES], row_picks[:, :, :]))
                own.did(dve.tensor_scalar(one_up[:, :], iota_col[:, :], 1.0, None, ALU.add))
                own.wait()
                dve.sem_inc(ready, 1)
        in_order.close()
        lists.close()

        def tile_value(eng, k, field, t, most):
            return eng.value_load(tile_info[k][0:1, bass.ds(field + t, 1)], min_val=0, max_val=most)

        BLOCKS_MAX = TILES + EDGES // BLOCK + 1

        def lay_out(k):
            with ExitStack() as ctx:
                sb, ps, sem = tensors(ctx, f"_{k}")
                at = sb("l_at", [P, 1])
                left = sb("l_left", [P, 1])
                where = sb("l_where", [P, 1], I32)
                fetched = sb("l_fetched", [P, BLOCK], I32)
                valid = sb("l_valid", [P, BLOCK])
                shifted = sb("l_shifted", [P, BLOCK])
                laid = sb("l_laid", [P, BLOCK], I32)
                v_did = sem("l_v_did")
                where_made = sem("l_where_made")
                block_fetched = sem("l_block_fetched")
                block_laid = sem("l_block_laid")
                block_written = sem("l_block_written")
                block = ctx.enter_context(nc.Block())

                def tile_loop(eng, body):
                    with eng.Fori(0, LTILES) as t:
                        blocks = tile_value(eng, k, N_BLOCKS, t, BLOCKS_MAX)
                        before = tile_value(eng, k, B_OFF, t, BLOCKS_MAX)
                        body(t, blocks, before)

                def is_slow(eng):
                    return eng.If(tile_value(eng, k, SLOW, 0, 1) > 0)

                @block.vector
                def _(dve):
                    def body(t, blocks, before):
                        base = t * 2 + before * 6 + 1
                        dve.wait_ge(v_did, base)
                        dve.tensor_copy(at[:, :], row_info[k][:, bass.ds(t, 1), 0]).then_inc(v_did, 1)
                        dve.tensor_copy(left[:, :], row_info[k][:, bass.ds(t, 1), 1]).then_inc(v_did, 1)
                        with dve.Fori(0, blocks) as b:
                            n = before + b
                            done = base + b * 6 + 2
                            dve.wait_ge(v_did, done)
                            dve.tensor_scalar(where[:, :], at[:, :], float(EDGES_PAD - BLOCK), None,
                                              ALU.min).then_inc(v_did, 1)
                            dve.wait_ge(v_did, done + 1)
                            dve.sem_inc(where_made, 1)
                            dve.tensor_scalar(at[:, :], at[:, :], float(BLOCK), None, ALU.add).then_inc(v_did, 1)
                            dve.tensor_scalar(valid[:, :], iota_block[:, :], left[:, :], None,
                                              ALU.is_lt).then_inc(v_did, 1)
                            dve.wait_ge(v_did, done + 3)
                            dve.tensor_scalar(left[:, :], left[:, :], float(-BLOCK), None,
                                              ALU.add).then_inc(v_did, 1)
                            dve.wait_ge(block_fetched, n * 16 + 16)
                            dve.scalar_tensor_tensor(shifted[:, :], fetched[:, :], float(-ZERO_ROW), valid[:, :],
                                                     ALU.add, ALU.mult).then_inc(v_did, 1)
                            dve.wait_ge(v_did, done + 5)
                            dve.wait_ge(block_written, n * 32 + 1)
                            dve.tensor_scalar(laid[:, :], shifted[:, :], float(ZERO_ROW), None,
                                              ALU.add).then_inc(v_did, 1)
                            dve.wait_ge(v_did, done + 6)
                            dve.sem_inc(block_laid, 1)
                    with is_slow(dve):
                        dve.sem_inc(v_did, 1)
                        dve.sem_inc(block_laid, 1)
                        tile_loop(dve, body)

                @block.gpsimd
                def _(pool):
                    def body(t, blocks, before):
                        with pool.Fori(0, blocks) as b:
                            n = before + b
                            pool.wait_ge(where_made, n + 1)
                            pool.wait_ge(block_laid, n + 1)
                            turn(pool, turns)
                            pool.indirect_dma_start(fetched[:, :], None, nbrs[k],
                                                    bass.IndirectOffsetOnAxis(where[:, 0:1], 0)
                                                    ).then_inc(block_fetched, 16)
                    with is_slow(pool):
                        tile_loop(pool, body)

                @block.sync
                def _(sp):
                    def body(t, blocks, before):
                        first = tile_value(sp, k, G_OFF, t, SLOTS_MAX // GROUP - BLOCK // GROUP)
                        with sp.Fori(0, blocks) as b:
                            n = before + b
                            sp.wait_ge(block_written, n * 32 + 1)
                            turn(sp, turns)
                            sp.wait_ge(block_laid, n + 2)
                            at_group = nc.s_assert_within(
                                first + b * (BLOCK // GROUP), 0, (SLOTS_MAX - BLOCK) // GROUP,
                                skip_runtime_bounds_check_because="SLOTS_MAX bounds all tiles' slots")
                            sp.dma_start(slots[k][:, bass.ds(at_group * GROUP, BLOCK)],
                                         laid[:, :]).then_inc(block_written, 16)
                            sp.dma_start(slot_tile[k][:, bass.ds(at_group, BLOCK // GROUP)],
                                         tile_ids[0:1, bass.ds(t, 1), :].squeeze(1)).then_inc(block_written, 16)
                    with is_slow(sp):
                        sp.sem_inc(block_written, 1)
                        tile_loop(sp, body)
                        total = tile_value(sp, k, B_OFF, LTILES - 1, BLOCKS_MAX)
                        sp.wait_ge(block_written, total * 32 + 33)
                        turn(sp, turns)

        for k in range(2):
            lay_out(k)

        def load_slots(sp, k, before, bodies, slot_rows, slot_tiles, rows_loaded, group_used):
            groups, half, half_groups = GROUPS[k], BODY[k] // 2, GROUPS[k] // 2
            with sp.Fori(0, bodies) as j:
                n = before + j
                for q in range(2):
                    sp.wait_ge(group_used, n * groups + (q + 1) * half_groups)
                    at_slot = nc.s_assert_within(j * BODY[k] + q * half, 0, SLOTS_MAX - half,
                                                 skip_runtime_bounds_check_because="bodies of the tiles' slots")
                    at_group = nc.s_assert_within(j * groups + q * half_groups, 0,
                                                  SLOTS_MAX // GROUP - half_groups,
                                                  skip_runtime_bounds_check_because="groups of the tiles' slots")
                    sp.dma_start(slot_rows[q][:, :], slots[k][:, bass.ds(at_slot, half)]
                                 ).then_inc(rows_loaded[q], 16)
                    sp.dma_start(slot_tiles[q][:, :], slot_tile[k][:, bass.ds(at_group, half_groups)]
                                 ).then_inc(rows_loaded[q], 16)

        def gather(pool, k, before, bodies, table, rows, slot_rows, rows_loaded, group_used, gathered):
            groups, half_groups = GROUPS[k], GROUPS[k] // 2
            with pool.Fori(0, bodies) as j:
                n = before + j
                for g in range(groups):
                    q, first = g // half_groups, g % half_groups * GROUP
                    if first == 0:
                        pool.wait_ge(rows_loaded[q], n * 32 + 32)
                    pool.wait_ge(group_used, n * groups + g + 1)
                    turn(pool, turns)
                    for s in range(GROUP):
                        pool.indirect_dma_start(
                            rows[g][:, s, :], None, table,
                            bass.IndirectOffsetOnAxis(slot_rows[q][:, first + s:first + s + 1], 0)
                        ).then_inc(gathered[g], 16)

        def bodies_of(eng, k):
            return eng.value_load(tile_info[k][0:1, BODIES:BODIES + 1], min_val=0, max_val=SLOTS_MAX // BODY[k])

        with ExitStack() as ctx:
            sb, ps, sem = tensors(ctx)
            own_rows = sb("a_own_rows", [P, TILES + 1, 3 * D])
            acc = sb("a_acc", [P, TILES + 1, A0])
            rows = [sb(f"a_rows{g}", [P, GROUP, W0]) for g in range(GROUPS[0])]
            slot_rows = [sb(f"a_slot_rows{q}", [P, BODY[0] // 2], I32) for q in range(2)]
            slot_tiles = [sb(f"a_slot_tiles{q}", [1, GROUPS[0] // 2], I32) for q in range(2)]
            hidden = [sb(f"a_hidden{p}", [P, GROUP, D]) for p in range(2)]
            weighed = sb("a_weighed", [P, GROUP, D])
            logit = [sb(f"a_logit{g}", [P, GROUP]) for g in range(GROUPS[0])]
            mask = [sb(f"a_mask{g}", [P, GROUP]) for g in range(GROUPS[0])]
            pick_row = sb("a_pick_row", [P, NODES_PAD], BF16)
            is_pick = sb("a_is_pick", [P, NODES_PAD], F8)
            w2 = sb("a_w2", [P, D])
            b2 = sb("a_b2", [P, 1])
            wl = sb("a_wl", [P, D])
            bl = sb("a_bl", [1, D])
            per_mask = sb("a_per_mask", [P, TILES])
            has_half = sb("a_has_half", [P, TILES])
            emb = [sb(f"a_emb{q}", [P, HEAD, D]) for q in range(2)]
            emb_t = [sb(f"a_emb_t{q}", [P, HEAD, D]) for q in range(2)]
            stats = sb("a_stats", [P, TILES, 6])
            mean = sb("a_mean", [P, TILES])
            spread = sb("a_spread", [P, TILES])
            rstd = sb("a_rstd", [P, TILES])
            turned = [ps(f"a_turned{q}", [P, HEAD, D]) for q in range(2)]
            product = [ps(f"a_product{q}", [P, HEAD, D]) for q in range(2)]
            own_gathered = sem("a_own_gathered")
            v_did = sem("a_v_did")
            rows_loaded = [sem(f"a_rows_loaded{q}") for q in range(2)]
            gathered = [sem(f"a_gathered{g}") for g in range(GROUPS[0])]
            pick_row_loaded = sem("a_pick_row_loaded")
            compared = sem("a_compared")
            choice_stored = sem("a_choice_stored")
            group_used = sem("a_group_used")
            logit_made = sem("a_logit_made")
            mask_made = sem("a_mask_made")
            emb_made = [sem(f"a_emb_made{q}") for q in range(2)]
            emb_turned = [sem(f"a_emb_turned{q}") for q in range(2)]
            emb_copied = [sem(f"a_emb_copied{q}") for q in range(2)]
            product_made = [sem(f"a_product_made{q}") for q in range(2)]
            product_used = [sem(f"a_product_used{q}") for q in range(2)]
            var_made = sem("a_var_made")
            std_made = sem("a_std_made")
            centred = sem("a_centred")
            h_made = sem("a_h_made")
            stored = sem("a_stored")
            block = ctx.enter_context(nc.Block())
            half_groups = GROUPS[0] // 2
            own_a, own_h, own_x = (slice(c * D, (c + 1) * D) for c in range(3))

            @block.sync
            def _(sp):
                bodies = bodies_of(sp, 0)
                load_slots(sp, 0, 0, bodies, slot_rows, slot_tiles, rows_loaded, group_used)

            @block.gpsimd
            def _(pool):
                for t in range(TILES):
                    pool.indirect_dma_start(own_rows[:, t, :], None, own0,
                                            bass.IndirectOffsetOnAxis(row_info[0][:, t, 2:3], 0)
                                            ).then_inc(own_gathered, 16)
                bodies = bodies_of(pool, 0)
                gather(pool, 0, 0, bodies, table0, rows, slot_rows, rows_loaded, group_used, gathered)
                pool.wait_ge(h_made, 1)
                for t in range(TILES):
                    node_of = bass.IndirectOffsetOnAxis(row_info[0][:, t, 2:3], 0)
                    pool.indirect_dma_start(own1, node_of, own_rows[:, t, own_x], None).then_inc(stored, 16)
                    pool.indirect_dma_start(table1, node_of, own_rows[:, t, own_h], None).then_inc(stored, 16)
                pool.wait_ge(stored, 2 * TILES * 16)

            @block.scalar
            def _(act):
                act.dma_start(w2[:, :], bc(w2_in.rearrange("k o -> o k"), [P, D])).then_inc(w_loaded, 16)
                act.dma_start(b2[:, :], bc(b2_in.rearrange("(o n) -> o n", o=1), [P, 1])).then_inc(w_loaded, 16)
                act.dma_start(wl[:, :], wl_in).then_inc(w_loaded, 16)
                act.dma_start(bl[:, :], bl_in.rearrange("(o n) -> o n", o=1)).then_inc(w_loaded, 16)
                act.wait_ge(w_loaded, (3 + 4) * 16)
                bodies = bodies_of(act, 0)

                def masks(j):
                    for g in range(GROUPS[0]):
                        act.wait_ge(logit_made, j * GROUPS[0] + g + 1)
                        act.activation(mask[g][:, :], logit[g][:, :], ACT.Sigmoid,
                                       bias=b2[:, :]).then_inc(mask_made, 1)
                act.sem_inc(compared, 1)
                act.sem_inc(choice_stored, 1)
                with act.Fori(0, TILES) as s:
                    act.wait_ge(compared, s + 1)
                    act.dma_start(pick_row[:, :], bc(picks[bass.ds(s, 1), :], [P, NODES_PAD])
                                  ).then_inc(pick_row_loaded, 16)
                    masks(s)
                    act.wait_ge(compared, s + 2)
                    act.dma_start(chosen[bass.ds(s, 1), :, :].squeeze(0),
                                  is_pick[:, :].bitcast(U8)).then_inc(choice_stored, 16)
                with act.If(bodies > TILES):
                    with act.Fori(TILES, bodies) as j:
                        masks(j)
                act.wait_ge(choice_stored, TILES * 16 + 1)
                with act.Fori(0, PASSES) as i:
                    for q, _, n in halves(0):
                        act.wait_ge(emb_turned[q], i + 1)
                        act.wait_ge(product_made[q], i)
                        act.copy(emb_t[q][:, 0:n, :], turned[q][:, 0:n, :]).then_inc(emb_copied[q], 1)
                act.wait_ge(var_made, 1)
                act.sqrt(rstd[:, :], rstd[:, :]).then_inc(std_made, 1)
                act.wait_ge(centred, 1)
                h1 = own_rows[:, 0:TILES, own_h]
                act.activation(h1, h1, ACT.Relu).then_inc(h_made, 1)

            @block.tensor
            def _(pe):
                pe.wait_ge(w_loaded, (3 + 4) * 16)
                with pe.Fori(0, PASSES) as i:
                    for q, t, n in halves(i * PASS):
                        pe.wait_ge(emb_made[q], i + 1)
                        pe.wait_ge(emb_copied[q], i)
                        for c in range(n):
                            last = pe.transpose(turned[q][:, c, :], emb[q][:, c, :], ident[:, :])
                        last.then_inc(emb_turned[q], 1)
                    for q, t, n in halves(i * PASS):
                        pe.wait_ge(emb_copied[q], i + 1)
                        pe.wait_ge(product_used[q], i)
                        for c in range(n):
                            pe.matmul(product[q][:, c, :], emb_t[q][:, c, :], wl[:, :], start=True, stop=False)
                            last = pe.matmul(product[q][:, c, :], ones[0:1, :], bl[0:1, :], start=False,
                                             stop=True)
                        last.then_inc(product_made[q], 1)

            @block.vector
            def _(dve):
                own = Count(dve, v_did)
                own.did(dve.memset(acc[:, :, :], 0.0))
                own.did(dve.memset(own_rows[:, TILES, :], 0.0))
                own.wait()
                dve.sem_inc(group_used, GROUPS[0])
                dve.wait_ge(w_loaded, (3 + 4) * 16)
                dve.wait_ge(own_gathered, TILES * 16)
                bodies = bodies_of(dve, 0)

                def body(j):
                    tiles = []
                    for g in range(GROUPS[0] + 1):
                        if g < GROUPS[0]:
                            q = g // half_groups
                            if g % half_groups == 0:
                                dve.wait_ge(rows_loaded[q], j * 32 + 32)
                                turn(dve, turns)
                            tiles.append(dve.value_load(slot_tiles[q][0:1, g % half_groups:g % half_groups + 1],
                                                        min_val=0, max_val=TILES))
                            dve.wait_ge(gathered[g], j * (GROUP * 16) + GROUP * 16)
                            a = own_rows[:, bass.ds(tiles[g], 1), own_a]
                            own.did(dve.tensor_tensor(hidden[g % 2][:, :, :], rows[g][:, :, 0:D],
                                                      bc(a, [P, GROUP, D]), ALU.add))
                            own.wait()
                            for s in range(GROUP):
                                last = dve.scalar_tensor_tensor(
                                    weighed[:, s, :], hidden[g % 2][:, s, :], 0.0, w2[:, :], ALU.max, ALU.mult,
                                    accum_out=logit[g][:, s:s + 1])
                            last.then_inc(logit_made, 1)
                        if g > 0:
                            f = g - 1
                            dve.wait_ge(mask_made, j * GROUPS[0] + f + 1)
                            sums = acc[:, bass.ds(tiles[f], 1), 0:D + 1].squeeze(1)
                            for s in range(GROUP):
                                own.wait()
                                own.did(dve.scalar_tensor_tensor(
                                    sums, rows[f][:, s, D:2 * D + 1], mask[f][:, s:s + 1], sums,
                                    ALU.mult, ALU.add))
                            own.wait()
                            dve.sem_inc(group_used, 1)

                with dve.Fori(0, TILES) as s:
                    own.enter(s, GROUPS[0] * (1 + GROUP))
                    body(s)
                    dve.wait_ge(pick_row_loaded, s * 16 + 16)
                    dve.wait_ge(choice_stored, s * 16 + 1)
                    turn(dve, turns)
                    dve.tensor_scalar(is_pick[:, :], pick_row[:, :], one_up[:, :], None, ALU.is_equal,
                                      saturate=False).then_inc(compared, 1)
                    own.leave(TILES)
                with dve.If(bodies > TILES):
                    with dve.Fori(TILES, bodies) as j:
                        own.enter(j - TILES, GROUPS[0] * (1 + GROUP))
                        body(j)
                        own.leave(bodies - TILES)
                own.wait()
                own.did(dve.tensor_scalar(per_mask[:, :], acc[:, 0:TILES, D], 1e-9, None, ALU.add))
                own.did(dve.tensor_scalar(has_half[:, :], row_info[0][:, 0:TILES, 1], 0.0, 0.5,
                                          ALU.is_gt, ALU.mult))
                own.wait()
                own.did(dve.reciprocal(per_mask[:, :], per_mask[:, :]))
                own.wait()
                turn(dve, turns)
                with dve.Fori(0, PASSES) as i:
                    own.enter(i, 3 * PASS)
                    for q, t, n in halves(i * PASS):
                        dve.wait_ge(emb_turned[q], i)
                        for c in range(n):
                            col = bass.ds(t + c, 1)
                            h_of = own_rows[:, col, own_h].squeeze(1)
                            own.did(dve.scalar_tensor_tensor(
                                emb[q][:, c, :], acc[:, col, 0:D].squeeze(1), per_mask[:, col], h_of,
                                ALU.mult, ALU.subtract))
                            own.wait()
                            own.did(dve.scalar_tensor_tensor(
                                emb[q][:, c, :], emb[q][:, c, :], has_half[:, col], h_of, ALU.mult, ALU.add))
                        own.wait()
                        dve.sem_inc(emb_made[q], 1)
                    for q, t, n in halves(i * PASS):
                        dve.wait_ge(product_made[q], i + 1)
                        x_of = own_rows[:, bass.ds(t, n), own_x]
                        dve.scalar_tensor_tensor(x_of, product[q][:, 0:n, :], 0.0, x_of, ALU.max,
                                                 ALU.add).then_inc(product_used[q], 1)
                        dve.wait_ge(product_used[q], i + 1)
                        for c in range(n):
                            own.did(dve.bn_stats(stats[:, bass.ds(t + c, 1), :].squeeze(1),
                                                 own_rows[:, bass.ds(t + c, 1), own_x].squeeze(1)))
                    own.leave(PASSES)
                rstd_steps(dve, own, stats, mean, spread, rstd)
                dve.sem_inc(var_made, 1)
                dve.wait_ge(std_made, 1)
                own.did(dve.reciprocal(rstd[:, :], rstd[:, :]))
                h1 = own_rows[:, 0:TILES, own_h]
                own.did(dve.tensor_tensor(h1, own_rows[:, 0:TILES, own_x],
                                          bc(mean[:, :].unsqueeze(2), [P, TILES, D]), ALU.subtract))
                own.wait()
                dve.tensor_tensor(h1, h1, bc(rstd[:, :].unsqueeze(2), [P, TILES, D]),
                                  ALU.mult).then_inc(centred, 1)

        LAYERS = 4
        with ExitStack() as ctx:
            sb, ps, sem = tensors(ctx)
            own_x1 = sb("c_own_x1", [P, TILES, D])
            new = sb("c_new", [P, TILES, D])
            acc = sb("c_acc", [P, TILES + 1, D])
            acc_t = sb("c_acc_t", [P, NODES_PAD])
            h_t = sb("c_h_t", [P, NODES_PAD])
            rows = [sb(f"c_rows{g}", [P, GROUP, D]) for g in range(GROUPS[1])]
            pairs = sb("c_pairs", [P, 2, D])
            best = sb("c_best", [P, D])
            slot_rows = [sb(f"c_slot_rows{q}", [P, BODY[1] // 2], I32) for q in range(2)]
            slot_tiles = [sb(f"c_slot_tiles{q}", [1, GROUPS[1] // 2], I32) for q in range(2)]
            source = [sb(f"c_source{p}", [P, D]) for p in range(2)]
            rest = [sb(f"c_rest{m}", [P, D]) for m in range(2)]
            parts = [sb(f"c_parts{p}", [P, 3, D], BF16) for p in range(2)]
            choice = [sb(f"c_choice{p}", [P, NODES_PAD], F8) for p in range(2)]
            w = [sb(f"c_w{m}", [P, D]) for m in range(2)]
            r = [sb(f"c_r{m}", [P, D]) for m in range(2)]
            b = [sb(f"c_b{m}", [P, 1]) for m in range(2)]
            w_now = sb("c_w_now", [P, D])
            r_now = sb("c_r_now", [P, D])
            b_now = sb("c_b_now", [P, 1])
            stage = [sb(f"c_stage{q}", [P, HEAD, D]) for q in range(2)]
            new_t = [sb(f"c_new_t{q}", [P, HEAD, D]) for q in range(2)]
            wide = [ps(f"c_wide{q}", [P, 2 * BANK]) for q in range(WIDE)]
            product = [wide[q][:, 0:BANK].rearrange("p (c m) -> p c m", m=D) for q in range(2)]
            back = [wide[q][:, BANK:2 * BANK].rearrange("p (c m) -> p c m", m=D) for q in range(2)]
            turned = [wide[2 + q][:, 0:BANK].rearrange("p (c m) -> p c m", m=D) for q in range(2)]
            own_gathered = sem("c_own_gathered")
            v_did = sem("c_v_did")
            weights_set = sem("c_weights_set")
            rows_loaded = [sem(f"c_rows_loaded{q}") for q in range(2)]
            gathered = [sem(f"c_gathered{g}") for g in range(GROUPS[1])]
            group_used = sem("c_group_used")
            choice_loaded = [sem(f"c_choice_loaded{p}") for p in range(2)]
            rest_made = sem("c_rest_made")
            parts_made = sem("c_parts_made")
            part_selected = sem("c_part_selected")
            part_used = sem("c_part_used")
            source_loaded = [sem(f"c_source_loaded{p}") for p in range(2)]
            tile_done = sem("c_tile_done")
            maxima_done = sem("c_maxima_done")
            staged = [sem(f"c_staged{q}") for q in range(2)]
            tile_turned = [sem(f"c_tile_turned{q}") for q in range(2)]
            tile_copied = [sem(f"c_tile_copied{q}") for q in range(2)]
            product_made = [sem(f"c_product_made{q}") for q in range(2)]
            new_made = [sem(f"c_new_made{q}") for q in range(2)]
            new_turned = [sem(f"c_new_turned{q}") for q in range(2)]
            new_out = [sem(f"c_new_out{q}") for q in range(2)]
            table_stored = sem("c_table_stored")
            table_ready = sem("c_table_ready")
            out_stored = sem("c_out_stored")
            block = ctx.enter_context(nc.Block())
            STEPS = TILES * PARTS
            PAIRS = TILES // 2
            EVENS, ODDS = PAIRS + 1, PAIRS

            def uses(layer, s_pair, p, first):
                return layer * EVENS if first else layer * ODDS + s_pair if p else layer * EVENS + s_pair + 1

            def over_sources(eng, layer, body):
                body(0, uses(layer, 0, 0, True), 0)
                with eng.Fori(0, PAIRS) as i:
                    for p in (1, 0):
                        body(i * 2 + 2 - p, uses(layer, i, p, False), p)

            @block.sync
            def _(sp):
                for m, (wi, ri, bi) in enumerate(((gw1_in, gr1_in, gb1_in), (gw2_in, gr2_in, gb2_in))):
                    sp.dma_start(w[m][:, :], wi).then_inc(w_loaded, 16)
                    sp.dma_start(r[m][:, :], ri).then_inc(w_loaded, 16)
                    sp.dma_start(b[m][:, :], bi.rearrange("(k o) -> k o", o=1)).then_inc(w_loaded, 16)
                bodies = bodies_of(sp, 1)
                with sp.Fori(0, LAYERS) as layer:
                    load_slots(sp, 1, layer * bodies, bodies, slot_rows, slot_tiles, rows_loaded, group_used)

            @block.gpsimd
            def _(pool):
                for t in range(TILES):
                    node_of = bass.IndirectOffsetOnAxis(row_info[1][:, t, 2:3], 0)
                    pool.indirect_dma_start(own_x1[:, t, :], None, own1, node_of).then_inc(own_gathered, 16)
                    pool.indirect_dma_start(new[:, t, :], None, table1, node_of).then_inc(own_gathered, 16)
                bodies = bodies_of(pool, 1)
                pool.sem_inc(table_ready, 1)
                with pool.Fori(0, LAYERS) as layer:
                    pool.wait_ge(table_ready, layer + 1)
                    turn(pool, turns)
                    gather(pool, 1, layer * bodies, bodies, table1, rows, slot_rows, rows_loaded, group_used,
                           gathered)
                    pool.wait_ge(maxima_done, layer + 1)
                    turn(pool, turns)
                    with pool.If(layer < LAYERS - 1):
                        for t in range(TILES):
                            q = int(t % PASS >= HEAD)
                            if t % PASS in (0, HEAD):
                                pool.wait_ge(new_out[q], layer * PASSES + t // PASS + 2)
                                turn(pool, turns)
                            pool.indirect_dma_start(table1, bass.IndirectOffsetOnAxis(row_info[1][:, t, 2:3], 0),
                                                    new[:, t, :], None).then_inc(table_stored, 16)
                        pool.wait_ge(table_stored, layer * (TILES * 16) + TILES * 16)
                        pool.sem_inc(table_ready, 1)
                    with pool.Else():
                        for t in range(TILES):
                            q = int(t % PASS >= HEAD)
                            if t % PASS in (0, HEAD):
                                pool.wait_ge(new_out[q], (LAYERS - 1) * PASSES + t // PASS + 2)
                            pool.indirect_dma_start(out, bass.IndirectOffsetOnAxis(row_info[1][:, t, 2:3], 0),
                                                    new[:, t, :], None, bounds_check=NODES - 1,
                                                    oob_is_err=False).then_inc(out_stored, 16)
                pool.wait_ge(out_stored, TILES * 16)

            @block.scalar
            def _(act):
                for q in range(2):
                    act.sem_inc(new_made[q], 1)
                act.sem_inc(parts_made, 1)
                with act.Fori(0, PASSES) as i:
                    for q, t, n in halves(i * PASS):
                        act.wait_ge(tile_turned[q], i + 2)
                        act.copy(h_t[:, bass.ds(t * P, n * P)],
                                 turned[q][:, 0:n, :].rearrange("p c m -> p (c m)")).then_inc(tile_copied[q], 1)

                with act.Fori(0, LAYERS) as layer:
                    act.wait_ge(table_ready, layer + 1)
                    turn(act, turns)

                    def split(s, used, p):
                        done = layer * STEPS + s * PARTS
                        act.wait_ge(tile_done, layer * TILES + s + 1)
                        turn(act, turns)
                        act.dma_start(choice[p][:, :].bitcast(U8),
                                      chosen[bass.ds(s, 1), :, :].squeeze(0)).then_inc(choice_loaded[p], 16)
                        act.dma_start(source[p][:, :], table1[bass.ds(s * P, P), :]).then_inc(source_loaded[p], 16)
                        return done

                    def convert(s, used, p):
                        act.wait_ge(source_loaded[p], used * 16 + 16)
                        n = layer * TILES + s
                        act.copy(parts[p][:, 0, :], source[p][:, :]).then_inc(parts_made, 1)
                        act.wait_ge(rest_made, n * 2 + 1)
                        act.copy(parts[p][:, 1, :], rest[0][:, :]).then_inc(parts_made, 1)
                        act.wait_ge(rest_made, n * 2 + 2)
                        act.copy(parts[p][:, 2, :], rest[1][:, :]).then_inc(parts_made, 1)

                    def body(s, used, p):
                        split(s, used, p)
                        convert(s, used, p)
                    over_sources(act, layer, body)
                    with act.Fori(0, PASSES) as i:
                        n_pass = layer * PASSES + i
                        for q, t, n in halves(i * PASS):
                            act.wait_ge(tile_turned[q], n_pass + PASSES + 1)
                            act.wait_ge(maxima_done, layer + 1)
                            act.copy(stage[q][:, 0:n, :], acc[:, bass.ds(t, n), :]).then_inc(staged[q], 1)
                        for q, t, n in halves(i * PASS):
                            cols = bass.ds(t * P, n * P)
                            act.wait_ge(product_made[q], n_pass + 1)
                            act.wait_ge(new_turned[q], n_pass + 1)
                            act.activation(new_t[q][:, 0:n, :], product[q][:, 0:n, :], ACT.Relu, bias=b_now[:, :])
                            act.activation(h_t[:, cols], product[q][:, 0:n, :].rearrange("p c m -> p (c m)"),
                                           ACT.Relu, bias=b_now[:, :]).then_inc(new_made[q], 1)

            @block.tensor
            def _(pe):
                for q in range(2):
                    pe.sem_inc(tile_turned[q], 1)
                    pe.sem_inc(new_turned[q], 1)
                pe.sem_inc(tile_done, 2)

                def turn_tiles(n_pass, q, n):
                    pe.wait_ge(staged[q], n_pass + 1)
                    pe.wait_ge(tile_copied[q], n_pass + 1)
                    for c in range(n):
                        last = pe.transpose(turned[q][:, c, :], stage[q][:, c, :], ident[:, :])
                    last.then_inc(tile_turned[q], 1)

                with pe.Fori(0, PASSES) as i:
                    for q, t, n in halves(i * PASS):
                        turn_tiles(i, q, n)
                with pe.Fori(0, LAYERS) as layer:
                    def select(s, used, p):
                        n = layer * TILES + s
                        pe.wait_ge(parts_made, n * 3 + 4)
                        pe.wait_ge(choice_loaded[p], used * 16 + 16)
                        for c in range(PARTS):
                            q = c % WIDE
                            pe.wait_ge(part_used, layer * STEPS + s * PARTS + c + 1)
                            turn(pe, turns)
                            for m in range(3):
                                for lo_c, hi_c in ((0, BANK), (BANK, PART)):
                                    last = pe.matmul(wide[q][:, lo_c:hi_c], parts[p][:, m, :],
                                                     choice[p][:, c * PART + lo_c:c * PART + hi_c],
                                                     start=(m == 0), stop=(m == 2))
                            last.then_inc(part_selected, 1)
                        pe.wait_ge(part_selected, layer * STEPS + s * PARTS + PARTS)
                        pe.sem_inc(tile_done, 1)
                    over_sources(pe, layer, select)
                    pe.wait_ge(part_used, layer * STEPS + STEPS + WIDE)
                    pe.wait_ge(weights_set, layer * 3 + 3)
                    turn(pe, turns)
                    with pe.Fori(0, PASSES) as i:
                        n_pass = layer * PASSES + i
                        for q, t, n in halves(i * PASS):
                            turn_tiles(n_pass + PASSES, q, n)
                        for q, t, n in halves(i * PASS):
                            cols = bass.ds(t * P, n * P)
                            pe.wait_ge(tile_copied[q], n_pass + PASSES + 2)
                            pe.wait_ge(new_made[q], n_pass + 1)
                            whole_q = wide[q][:, 0:n * P]
                            pe.matmul(whole_q, w_now[:, :], acc_t[:, cols], start=True, stop=False)
                            pe.matmul(whole_q, r_now[:, :], h_t[:, cols], start=False,
                                      stop=True).then_inc(product_made[q], 1)
                        for q, t, n in halves(i * PASS):
                            pe.wait_ge(new_made[q], n_pass + 2)
                            pe.wait_ge(new_out[q], n_pass + 1)
                            for c in range(n):
                                last = pe.transpose(back[q][:, c, :], new_t[q][:, c, :], ident[:, :])
                            last.then_inc(new_turned[q], 1)

            @block.vector
            def _(dve):
                dve.memset(acc[:, :, :], 0.0).then_inc(v_did, 1)
                dve.wait_ge(v_did, 1)
                dve.sem_inc(group_used, GROUPS[1])
                dve.sem_inc(part_used, WIDE)
                for q in range(2):
                    dve.sem_inc(tile_copied[q], 1)
                    dve.sem_inc(new_out[q], 1)
                dve.wait_ge(w_loaded, (3 + 4 + 6) * 16)
                dve.tensor_copy(w_now[:, :], w[0][:, :]).then_inc(weights_set, 1)
                dve.tensor_copy(r_now[:, :], r[0][:, :]).then_inc(weights_set, 1)
                dve.tensor_copy(b_now[:, :], b[0][:, :]).then_inc(weights_set, 1)
                dve.wait_ge(own_gathered, 2 * TILES * 16)
                with dve.Fori(0, PASSES) as i:
                    for q, t, n in halves(i * PASS):
                        dve.wait_ge(tile_turned[q], i + 1)
                        dve.tensor_copy(stage[q][:, 0:n, :], new[:, bass.ds(t, n), :]).then_inc(staged[q], 1)
                bodies = bodies_of(dve, 1)
                with dve.Fori(0, LAYERS) as layer:
                    base = layer * (bodies * (3 * GROUPS[1]) + 1) + 1

                    def take_group(j, g):
                        n = layer * bodies + j
                        done = base + j * (3 * GROUPS[1]) + 3 * g
                        dve.wait_ge(rows_loaded[g], n * 32 + 32)
                        turn(dve, turns)
                        tile = dve.value_load(slot_tiles[g][0:1, 0:1], min_val=0, max_val=TILES)
                        best_of = acc[:, bass.ds(tile, 1), :].squeeze(1)
                        dve.wait_ge(gathered[g], n * (GROUP * 16) + GROUP * 16)
                        dve.wait_ge(v_did, done)
                        dve.tensor_tensor(pairs[:, :, :], rows[g][:, 0:2, :], rows[g][:, 2:4, :],
                                          ALU.max).then_inc(v_did, 1)
                        dve.wait_ge(v_did, done + 1)
                        dve.sem_inc(group_used, 1)
                        dve.tensor_tensor(best[:, :], pairs[:, 0, :], pairs[:, 1, :], ALU.max).then_inc(v_did, 1)
                        dve.wait_ge(v_did, done + 2)
                        dve.tensor_tensor(best_of, best_of, best[:, :], ALU.max).then_inc(v_did, 1)

                    def take_parts(s, c, first):
                        n = layer * STEPS + s * PARTS + c
                        part = acc_t[:, c * PART:(c + 1) * PART]
                        dve.wait_ge(part_selected, n + 1)
                        if first:
                            dve.tensor_copy(part, wide[c % WIDE][:, 0:PART]).then_inc(part_used, 1)
                        else:
                            dve.wait_ge(part_used, n - PARTS + WIDE + 1)
                            dve.tensor_tensor(part, part, wide[c % WIDE][:, 0:PART], ALU.max).then_inc(part_used, 1)

                    def split(s, used, p):
                        n = layer * TILES + s
                        dve.wait_ge(parts_made, n * 3 + 2)
                        dve.tensor_tensor(rest[0][:, :], source[p][:, :], parts[p][:, 0, :],
                                          ALU.subtract).then_inc(rest_made, 1)
                        dve.wait_ge(parts_made, n * 3 + 3)
                        dve.tensor_tensor(rest[1][:, :], rest[0][:, :], parts[p][:, 1, :],
                                          ALU.subtract).then_inc(rest_made, 1)

                    def body(s, next_uses, next_p, first=False):
                        for c in range(PARTS):
                            take_parts(s, c, first)
                            if c == 0 and next_p is not None:
                                split(s + 1, next_uses, next_p)
                            if c == PARTS // 2 - 1:
                                take_group(s, 0)
                        take_group(s, 1)

                    split(0, 0, 0)
                    body(0, 0, 1, first=True)
                    with dve.Fori(0, PAIRS - 1) as i:
                        for p in (1, 0):
                            body(i * 2 + 2 - p, 0, 1 - p)
                    body(TILES - 2, 0, 0)
                    body(TILES - 1, 0, None)
                    with dve.If(bodies > TILES):
                        with dve.Fori(TILES, bodies) as j:
                            for g in range(GROUPS[1]):
                                take_group(j, g)
                    dve.wait_ge(v_did, base + bodies * (3 * GROUPS[1]))
                    dve.wait_ge(part_used, layer * STEPS + STEPS + WIDE)
                    dve.wait_ge(table_ready, layer + 1)
                    dve.sem_inc(maxima_done, 1)
                    with dve.Fori(0, PASSES) as i:
                        n_pass = layer * PASSES + i
                        for q, t, n in halves(i * PASS):
                            cols = bass.ds(t * P, n * P)
                            dve.wait_ge(tile_turned[q], n_pass + PASSES + 2)
                            dve.tensor_tensor(acc_t[:, cols], acc_t[:, cols],
                                              turned[q][:, 0:n, :].rearrange("p c m -> p (c m)"),
                                              ALU.max).then_inc(tile_copied[q], 1)
                        for q, t, n in halves(i * PASS):
                            dve.wait_ge(new_turned[q], n_pass + 2)
                            turn(dve, turns)
                            with dve.If(layer < LAYERS - 1):
                                dve.tensor_copy(new[:, bass.ds(t, n), :], back[q][:, 0:n, :]
                                                ).then_inc(new_out[q], 1)
                            with dve.Else():
                                dve.tensor_tensor(new[:, bass.ds(t, n), :], back[q][:, 0:n, :],
                                                  own_x1[:, bass.ds(t, n), :], ALU.add).then_inc(new_out[q], 1)
                    for q in range(2):
                        dve.wait_ge(staged[q], layer * PASSES + 2 * PASSES)
                        dve.wait_ge(new_made[q], layer * PASSES + PASSES + 1)
                    dve.memset(acc[:, :, :], 0.0).then_inc(v_did, 1)
                    dve.tensor_copy(w_now[:, :], w[1][:, :]).then_inc(weights_set, 1)
                    dve.tensor_copy(r_now[:, :], r[1][:, :]).then_inc(weights_set, 1)
                    dve.tensor_copy(b_now[:, :], b[1][:, :]).then_inc(weights_set, 1)


_INS = ["x", "src", "dst", "L0_gnn_W1", "L0_gnn_b1", "L0_gnn_W2", "L0_gnn_b2", "L0_gnn_Wl", "L0_gnn_bl",
        "L1_gnn_W1", "L1_gnn_b1", "L1_gnn_R1", "L1_gnn_W2", "L1_gnn_b2", "L1_gnn_R2"]


def kernel(**inputs):
    import concourse.bacc as bacc
    from concourse.bass_utils import run_bass_kernel_spmd

    nc = bacc.Bacc("TRN2", target_bir_lowering=False, num_devices=1)
    arrays, args = {}, []
    for name in _INS:
        a = np.ascontiguousarray(inputs[name])
        arrays[f"in_{name}"] = a
        args.append(nc.dram_tensor(f"in_{name}", a.shape, mybir.dt.from_np(a.dtype), kind="ExternalInput").ap())
    args.append(nc.dram_tensor("out_x", (NODES, D), F32, kind="ExternalOutput").ap())
    gnn(nc, *args)
    return run_bass_kernel_spmd(nc, [arrays], core_ids=[0]).results[0]["out_x"]
```

```python
import numpy as np
from contextlib import ExitStack
import concourse.bass as bass
from concourse import mybir
from concourse.alu_op_type import AluOpType as ALU

F32 = mybir.dt.float32
BF16 = mybir.dt.bfloat16
I32 = mybir.dt.int32
U8 = mybir.dt.uint8
F8 = mybir.dt.float8e4
ACT = mybir.ActivationFunctionType
AX = mybir.AxisListType

P = 128
NODES = 6250
EDGES = 200000
D = 128
TILES = -(-NODES // P)
NODES_PAD = TILES * P
LAST_ROWS = NODES - (TILES - 1) * P
PAD_NODE = NODES_PAD - 1
SUB = 8
CHUNKS = 2 * SUB * -(-EDGES // (P * 2 * SUB))
EDGES_PAD = P * CHUNKS
SUBS = CHUNKS // SUB
FULL_PARTS = EDGES // CHUNKS
REST = EDGES - FULL_PARTS * CHUNKS
assert FULL_PARTS == P - 1 and REST > 0 and PAD_NODE >= NODES
GROUP = 4
BODY = (32, 20)
GROUPS = tuple(b // GROUP for b in BODY)
BLOCK = 64
LTILES = TILES + 1
SLOTS_MAX = EDGES + GROUP + EDGES // P + (GROUP + 1) * TILES + 2 * BLOCK
ZERO_ROW = NODES_PAD
TABLE_ROWS = NODES_PAD + P
W0 = 2 * D + 4
A0 = D + 4
BUCKETS = P
HEAD, TAIL = 4, 3
PASS = HEAD + TAIL
PASSES = TILES // PASS
assert PASSES * PASS == TILES
assert EDGES > (TILES - 1) * BODY[0] * P
assert SUBS == 4 * TILES
INFO = 4
RECORD = (INFO, INFO + BLOCK + TILES)
QUICK_SLOTS = TILES * BLOCK + BLOCK
PARTS = 8
PART = NODES_PAD // PARTS
ROUNDS = BLOCK // 8
LIST_STEPS = 2 + (2 * ROUNDS - 1) + 8 + (2 * ROUNDS - 1) + 2
PICK_STEPS = 5
assert SUB == ROUNDS
BANK = 512
WIDE = 4
assert PART * PARTS == NODES_PAD and BANK < PART <= 2 * BANK


class Count:

    def __init__(self, eng, sem):
        self.eng, self.sem, self.base, self.n = eng, sem, 0, 0

    def of(self, eng):
        self.eng = eng
        return self

    def did(self, instruction):
        instruction.then_inc(self.sem, 1)
        self.n += 1

    def wait(self, but=0):
        self.eng.wait_ge(self.sem, self.base + (self.n - but))

    def enter(self, i, per_pass):
        self.before = self.base + self.n
        self.base, self.n, self.per_pass = self.before + i * per_pass, 0, per_pass

    def leave(self, passes):
        assert self.n == self.per_pass, (self.n, self.per_pass)
        self.base, self.n = self.before + passes * self.per_pass, 0


def turn(eng, turns):
    eng.sem_inc(turns, 1)


def bc(ap, shape):
    return ap.to_broadcast(shape)


def gnn(nc, x_in, src_in, dst_in, w1_in, b1_in, w2_in, b2_in, wl_in, bl_in,
        gw1_in, gb1_in, gr1_in, gw2_in, gb2_in, gr2_in, out):
    def dram(name, shape, dt=F32):
        return nc.dram_tensor(name, shape, dt).ap()

    table0 = dram("table0", [TABLE_ROWS, W0])
    own0 = dram("own0", [NODES_PAD, 3 * D])
    table1 = dram("table1", [TABLE_ROWS, D])
    own1 = dram("own1", [NODES_PAD, D])
    nbrs = [dram(f"nbrs{k}", [EDGES_PAD, 1], I32) for k in range(2)]
    meta = [dram(f"meta{k}", [NODES_PAD, RECORD[k]], I32) for k in range(2)]
    picks = dram("picks", [TILES, NODES_PAD], BF16)
    chosen = dram("chosen", [TILES, P, NODES_PAD], U8)
    slots = [dram(f"slots{k}", [P, SLOTS_MAX], I32) for k in range(2)]
    slot_tile = [dram(f"slot_tile{k}", [1, SLOTS_MAX // GROUP], I32) for k in range(2)]

    with ExitStack() as whole:
        def tensors(ctx, tag=""):
            def sb(name, shape, dt=F32):
                return ctx.enter_context(nc.sbuf_tensor(name + tag, shape, dt))

            def ps(name, shape, dt=F32):
                return ctx.enter_context(nc.psum_tensor(name + tag, shape, dt))

            def sem(name):
                return ctx.enter_context(nc.semaphore(name + tag))
            return sb, ps, sem

        sb, ps, sem = tensors(whole)
        turns = sem("turns")
        steps = Count(nc.vector, sem("v_steps"))
        iota_made = sem("iota_made")
        w_loaded = sem("w_loaded")
        whole_sem = sem
        iota_col = sb("iota_col", [P, 1])
        iota_row = sb("iota_row", [P, P])
        ident = sb("ident", [P, P])
        ident_b = sb("ident_b", [P, P], BF16)
        above_b = sb("above_b", [P, P], BF16)
        ones_b = sb("ones_b", [P, P], BF16)
        below = sb("below", [P, P])
        above = sb("above", [P, P])
        ones = sb("ones", [P, P])
        tile_ids = sb("tile_ids", [1, LTILES, BLOCK // GROUP], I32)
        iota_block = sb("iota_block", [P, BLOCK])
        one_up = sb("one_up", [P, 1])
        node = sb("node", [P, TILES])
        node_i = sb("node_i", [P, TILES], I32)
        degree = [sb(f"degree{k}", [P, TILES]) for k in range(2)]
        slow = [sb(f"slow{k}", [P, 1]) for k in range(2)]
        start = [sb(f"start{k}", [P, TILES]) for k in range(2)]
        row_info = [sb(f"row_info{k}", [P, LTILES, 4], I32) for k in range(2)]
        tile_info = [sb(f"tile_info{k}", [1, 4 * LTILES + 4], I32) for k in range(2)]
        G_OFF, N_BLOCKS, B_OFF, QUICK_OFF, BODIES, SLOW = (
            0, LTILES, 2 * LTILES, 3 * LTILES, 4 * LTILES, 4 * LTILES + 1)

        lists = ExitStack()
        lsb, _, _ = tensors(lists)
        record = [lsb(f"record{k}", [P, TILES, RECORD[k]], I32) for k in range(2)]
        load = [degree[0], lsb("load1", [P, TILES])]
        fast = lsb("fast", [P, 1])
        rank = [lsb(f"rank{k}", [P, TILES], I32) for k in range(2)]
        keys = ExitStack()
        ksb, _, _ = tensors(keys)
        ends_i = [ksb(f"ends_i{k}", [P, CHUNKS + SUB], I32) for k in range(2)]
        lo = [ksb(f"lo{k}", [P, CHUNKS + SUB]) for k in range(2)]
        hi = [ksb(f"hi{k}", [P, CHUNKS + SUB]) for k in range(2)]
        lo_b = [ksb(f"lo_b{k}", [P, CHUNKS + SUB], BF16) for k in range(2)]
        hi_b = [ksb(f"hi_b{k}", [P, CHUNKS + SUB], BF16) for k in range(2)]
        each_lo = ksb("each_lo", [P, P, SUB], BF16)
        each_hi = ksb("each_hi", [P, TILES, SUB], BF16)

        def one_hots(dve, k, col, one_lo, one_hi):
            dve.tensor_tensor(one_lo[:, :, :], bc(lo_b[k][:, bass.ds(col, SUB)].unsqueeze(1), [P, P, SUB]),
                              each_lo[:, :, :], ALU.is_equal)
            return dve.tensor_tensor(one_hi[:, :, :],
                                     bc(hi_b[k][:, bass.ds(col, SUB)].unsqueeze(1), [P, TILES, SUB]),
                                     each_hi[:, :, :], ALU.is_equal)

        with nc.cleanup_on_exit(), ExitStack() as ctx:
            sb, ps, _ = tensors(ctx)
            sem = nc.alloc_semaphore
            iota_i = sb("iota_i", [P, P], I32)
            iota_ci = sb("iota_ci", [P, 1], I32)
            digit_i = sb("digit_i", [P, CHUNKS + SUB], I32)
            zeros_b = sb("zeros_b", [P, P], BF16)
            one_lo = [[sb(f"h_lo{k}{p}", [P, P, SUB], BF16) for p in range(2)] for k in range(2)]
            one_hi = [[sb(f"h_hi{k}{p}", [P, TILES, SUB], BF16) for p in range(2)] for k in range(2)]
            total = [sb(f"total{k}", [P, TILES]) for k in range(2)]
            upto = [sb(f"upto{k}", [P, TILES]) for k in range(2)]
            hist = [ps(f"hist{k}", [P, TILES]) for k in range(2)]
            within = [ps(f"within{k}", [P, TILES]) for k in range(2)]
            totals = [ps(f"totals{k}", [P, TILES]) for k in range(2)]
            pads_set = sem("pads_set")
            ends_loaded = [sem(f"ends_loaded{k}") for k in range(2)]
            nbrs_copied = sem("nbrs_copied")
            digits_made = sem("digits_made")
            ones_made = [sem(f"h_ones_made{k}") for k in range(2)]
            hist_did = [sem(f"hist_did{k}") for k in range(2)]
            hist_out = sem("hist_out")
            prefix_did = sem("prefix_did")
            block = ctx.enter_context(nc.Block())

            @block.sync
            def _(sp):
                sp.wait_ge(pads_set, 2)
                for k, ends in enumerate((src_in, dst_in)):
                    sp.dma_start(ends_i[k][0:FULL_PARTS, 0:CHUNKS],
                                 ends[0:FULL_PARTS * CHUNKS].rearrange("(p c) -> p c", c=CHUNKS)
                                 ).then_inc(ends_loaded[k], 16)
                    sp.dma_start(ends_i[k][FULL_PARTS:P, 0:REST],
                                 ends[FULL_PARTS * CHUNKS:EDGES].rearrange("(p c) -> p c", p=1)
                                 ).then_inc(ends_loaded[k], 16)
                sp.wait_ge(ends_loaded[0], 32)
                sp.dma_start(nbrs[1].rearrange("(p c) o -> p (c o)", p=P),
                             ends_i[0][:, 0:CHUNKS]).then_inc(nbrs_copied, 16)
                sp.wait_ge(nbrs_copied, 16)

            @block.gpsimd
            def _(pool):
                pool.iota(iota_i[:, :], [[1, P]], base=0, channel_multiplier=0).then_inc(iota_made, 1)
                pool.iota(iota_ci[:, :], [[1, 1]], base=0, channel_multiplier=1).then_inc(iota_made, 1)
                pool.iota(tile_ids[:, :, :], [[1, LTILES], [0, BLOCK // GROUP]], base=0,
                          channel_multiplier=0).then_inc(iota_made, 1)

            @block.vector
            def _(dve):
                own = steps.of(dve)
                for k in range(2):
                    dve.memset(ends_i[k][:, :], PAD_NODE).then_inc(pads_set, 1)
                dve.wait_ge(iota_made, 3)
                own.did(dve.tensor_copy(iota_row[:, :], iota_i[:, :]))
                own.did(dve.tensor_copy(iota_col[:, :], iota_ci[:, :]))
                own.did(dve.memset(ones[:, :], 1.0))
                own.did(dve.memset(zeros_b[:, :], 0.0))
                own.wait()
                own.did(dve.tensor_copy(each_lo[:, :, :], bc(iota_row[:, :].unsqueeze(2), [P, P, SUB])))
                own.did(dve.tensor_scalar(each_hi[:, :, :], bc(iota_row[:, 0:TILES].unsqueeze(2), [P, TILES, SUB]),
                                          float(P), None, ALU.mult))
                own.did(dve.tensor_scalar(ident[:, :], iota_row[:, :], iota_col[:, :], None, ALU.is_equal))
                own.did(dve.tensor_scalar(ident_b[:, :], iota_row[:, :], iota_col[:, :], None, ALU.is_equal))
                own.did(dve.tensor_scalar(above_b[:, :], iota_row[:, :], iota_col[:, :], None, ALU.is_gt))
                own.did(dve.memset(ones_b[:, :], 1.0))
                own.did(dve.tensor_scalar(below[:, :], iota_row[:, :], iota_col[:, :], None, ALU.is_lt))
                own.did(dve.tensor_scalar(above[:, :], iota_row[:, :], iota_col[:, :], None, ALU.is_gt))
                for k in range(2):
                    dve.wait_ge(ends_loaded[k], 32)
                    own.wait()
                    own.did(dve.tensor_scalar(digit_i[:, :], ends_i[k][:, :], P - 1, None, ALU.bitwise_and))
                    own.wait()
                    own.did(dve.tensor_copy(lo[k][:, :], digit_i[:, :]))
                    own.did(dve.tensor_copy(lo_b[k][:, :], digit_i[:, :]))
                    own.wait()
                    own.did(dve.tensor_scalar(digit_i[:, :], ends_i[k][:, :], 7, None,
                                              ALU.arith_shift_right))
                    own.wait()
                    own.did(dve.tensor_copy(hi[k][:, :], digit_i[:, :]))
                    own.did(dve.tensor_scalar(hi_b[k][:, :], digit_i[:, :], float(P), None, ALU.mult))
                own.wait()
                dve.sem_inc(digits_made, 1)
                with dve.Fori(0, SUBS // 2) as i:
                    for p in range(2):
                        for k in range(2):
                            dve.wait_ge(hist_did[k], i * 2 + p + 1)
                            one_hots(dve, k, (i * 2 + p) * SUB, one_lo[k][p], one_hi[k][p]
                                     ).then_inc(ones_made[k], 1)
                for k in range(2):
                    dve.wait_ge(hist_did[k], SUBS + 3)
                    own.did(dve.tensor_copy(degree[k][:, :], hist[k][:, :]))
                    own.wait()
                    dve.sem_inc(hist_out, 1)
                    dve.wait_ge(prefix_did, 2 * k + 2)
                    own.did(dve.tensor_copy(total[k][:, :], totals[k][:, :]))
                    own.wait()
                    own.did(dve.tensor_tensor_scan(upto[k][:, :], bc(ones[:, 0:1], [P, TILES]), total[k][:, :],
                                                   0.0, ALU.mult, ALU.add))
                    own.wait()
                    own.did(dve.tensor_tensor(upto[k][:, :], upto[k][:, :], total[k][:, :], ALU.subtract))
                    own.wait()
                    own.did(dve.tensor_tensor(start[k][:, :], upto[k][:, :], within[k][:, :], ALU.add))
                own.wait()

            @block.tensor
            def _(pe):
                pe.wait_ge(digits_made, 1)
                for k in range(2):
                    pe.matmul(hist[k][:, :], zeros_b[:, :], zeros_b[:, 0:TILES], start=True,
                              stop=False).then_inc(hist_did[k], 1)
                    pe.matmul(hist[k][:, :], zeros_b[:, :], zeros_b[:, 0:TILES], start=False,
                              stop=False).then_inc(hist_did[k], 1)
                with pe.Fori(0, SUBS // 2) as i:
                    for p in range(2):
                        for k in range(2):
                            pe.wait_ge(ones_made[k], i * 2 + p + 1)
                            for c in range(SUB):
                                last = pe.matmul(hist[k][:, :], one_lo[k][p][:, :, c], one_hi[k][p][:, :, c],
                                                 start=False, stop=False)
                            last.then_inc(hist_did[k], 1)
                for k in range(2):
                    pe.matmul(hist[k][:, :], zeros_b[:, :], zeros_b[:, 0:TILES], start=False,
                              stop=True).then_inc(hist_did[k], 1)
                for k in range(2):
                    pe.wait_ge(hist_out, k + 1)
                    pe.matmul(within[k][:, :], above[:, :], degree[k][:, :], start=True,
                              stop=True).then_inc(prefix_did, 1)
                    pe.matmul(totals[k][:, :], ones[:, :], degree[k][:, :], start=True,
                              stop=True).then_inc(prefix_did, 1)

        def halves(t):
            return ((0, t, HEAD), (1, t + HEAD, TAIL))

        onehots_made = whole_sem("onehots_made")
        counted = whole_sem("counted")
        totals_made = whole_sem("totals_made")
        base_made = whole_sem("base_made")
        ranks_spread = whole_sem("ranks_spread")
        ranks_read = whole_sem("ranks_read")

        def rank_buffers(sb, ps, tag):
            return dict(bucket=sb(tag + "k_bucket", [P, TILES]),
                        onehot=sb(tag + "k_onehot", [P, TILES, BUCKETS], BF16),
                        counts_sb=sb(tag + "k_counts_sb", [P, TILES]),
                        upto=sb(tag + "k_upto", [P, TILES]),
                        total=sb(tag + "k_total", [P, 1]),
                        higher_sb=sb(tag + "k_higher_sb", [P, 1]),
                        base=sb(tag + "k_base", [P, TILES]),
                        looked=[sb(tag + f"k_looked{p}", [P, PASS, BUCKETS]) for p in range(2)],
                        rank_f=sb(tag + "k_rank_f", [P, TILES]),
                        counts=ps(tag + "k_counts", [P, TILES]),
                        higher=ps(tag + "k_higher", [P, 1]),
                        spread=[ps(tag + f"k_spread{p}", [P, PASS + 1, BUCKETS]) for p in range(2)])

        def rank_products(pe, k, r):
            pe.wait_ge(onehots_made, k + 1)
            for t in range(TILES):
                last = pe.matmul(r["counts"][:, t:t + 1], r["onehot"][:, t, :], ones_b[:, 0:1], start=True,
                                 stop=True)
            last.then_inc(counted, 1)
            pe.wait_ge(totals_made, k + 1)
            pe.matmul(r["higher"][:, :], below[:, :], r["total"][:, :], start=True, stop=True).then_inc(counted, 1)
            pe.wait_ge(base_made, k + 1)
            for i in range(PASSES):
                if i >= 2:
                    pe.wait_ge(ranks_read, k * PASSES + i - 1)
                for c in range(PASS):
                    t, out_of = i * PASS + c, r["spread"][i % 2][:, c, :]
                    pe.matmul(out_of, bc(r["base"][:, t:t + 1], [P, P]), ident[:, :], start=True, stop=False)
                    last = pe.matmul(out_of, above_b[:, :], r["onehot"][:, t, :], start=False, stop=True)
                last.then_inc(ranks_spread, 1)

        def rank_sums(dve, own, k, r):
            own.did(dve.tensor_scalar(r["bucket"][:, :], load[k][:, :], float(BUCKETS - 1), None, ALU.min))
            own.wait()
            full = [P, TILES, BUCKETS]
            own.did(dve.tensor_tensor(r["onehot"][:, :, :], bc(r["bucket"][:, :].unsqueeze(2), full),
                                      bc(iota_row[:, :].unsqueeze(1), full), ALU.is_equal))
            own.wait()
            dve.sem_inc(onehots_made, 1)
            dve.wait_ge(counted, 2 * k + 1)
            own.did(dve.tensor_copy(r["counts_sb"][:, :], r["counts"][:, :]))
            own.wait()
            own.did(dve.tensor_reduce(r["total"][:, :], r["counts_sb"][:, :], AX.X, ALU.add))
            own.did(dve.tensor_tensor_scan(r["upto"][:, :], bc(ones[:, 0:1], [P, TILES]), r["counts_sb"][:, :],
                                           0.0, ALU.mult, ALU.add))
            own.wait()
            dve.sem_inc(totals_made, 1)
            own.did(dve.tensor_tensor(r["upto"][:, :], r["upto"][:, :], r["counts_sb"][:, :], ALU.subtract))
            dve.wait_ge(counted, 2 * k + 2)
            own.did(dve.tensor_copy(r["higher_sb"][:, :], r["higher"][:, :]))
            own.wait()
            own.did(dve.tensor_scalar(r["base"][:, :], r["upto"][:, :], r["higher_sb"][:, :], None, ALU.add))
            own.wait()
            dve.sem_inc(base_made, 1)
            for i in range(PASSES):
                dve.wait_ge(ranks_spread, k * PASSES + i + 1)
                tiles, looked = slice(i * PASS, (i + 1) * PASS), r["looked"][i % 2]
                own.wait()
                own.did(dve.tensor_tensor(looked[:, :, :], r["spread"][i % 2][:, 0:PASS, :],
                                          r["onehot"][:, tiles, :], ALU.mult))
                own.wait()
                dve.sem_inc(ranks_read, 1)
                own.did(dve.tensor_reduce(r["rank_f"][:, tiles], looked[:, :, :], AX.X, ALU.add))
            own.wait()
            own.did(dve.tensor_copy(rank[k][:, :], r["rank_f"][:, :]))
            own.wait()

        with ExitStack() as ctx:
            sb, ps, sem = tensors(ctx)
            iota_i = sb("n_iota_i", [P, BLOCK], I32)
            real = sb("n_real", [P, TILES])
            most = [sb(f"n_most{k}", [P, 1]) for k in range(2)]
            ranking = rank_buffers(sb, ps, "n_")
            all_most = ps("n_all_most", [P, P])
            most_made = sem("n_most_made")
            most_spread = sem("n_most_spread")
            block = ctx.enter_context(nc.Block())

            @block.gpsimd
            def _(pool):
                pool.iota(node_i[:, :], [[P, TILES]], base=0, channel_multiplier=1).then_inc(iota_made, 1)
                pool.iota(iota_i[:, :], [[1, BLOCK]], base=0, channel_multiplier=0).then_inc(iota_made, 1)

            @block.tensor
            def _(pe):
                for k in range(2):
                    pe.wait_ge(most_made, k + 1)
                    pe.matmul(all_most[:, :], bc(most[k][:, :], [P, P]), ident[:, :], start=True,
                              stop=True).then_inc(most_spread, 1)
                rank_products(pe, 0, ranking)

            @block.vector
            def _(dve):
                own = steps.of(dve)
                dve.wait_ge(iota_made, 5)
                own.did(dve.tensor_copy(node[:, :], node_i[:, :]))
                own.did(dve.tensor_copy(iota_block[:, :], iota_i[:, :]))
                own.wait()
                own.did(dve.tensor_scalar(real[:, :], node[:, :], float(NODES), None, ALU.is_lt))
                own.wait()
                for k in range(2):
                    own.did(dve.tensor_tensor(degree[k][:, :], degree[k][:, :], real[:, :], ALU.mult))
                    own.wait()
                    own.did(dve.tensor_reduce(most[k][:, :], degree[k][:, :], AX.X, ALU.max))
                    own.wait()
                    dve.sem_inc(most_made, 1)
                    dve.wait_ge(most_spread, k + 1)
                    own.did(dve.tensor_reduce(slow[k][:, :], all_most[:, :], AX.X, ALU.max))
                    own.wait()
                    own.did(dve.tensor_scalar(slow[k][:, :], slow[k][:, :], float(BLOCK), None, ALU.is_gt))
                    own.wait()
                own.did(dve.tensor_scalar(fast[:, :], slow[1][:, :], -1.0, 1.0, ALU.mult, ALU.add))
                for k in range(2):
                    own.did(dve.tensor_copy(record[k][:, :, 0], start[k][:, :]))
                    own.did(dve.tensor_copy(record[k][:, :, 2], node_i[:, :]))
                    own.did(dve.memset(record[k][:, :, 3], 0))
                    own.did(dve.memset(row_info[k][:, :, :], 0))
                own.did(dve.tensor_copy(record[0][:, :, 1], load[0][:, :]))
                own.wait()
                rank_sums(dve, own, 0, ranking)

        def sort(k):
            with ExitStack() as ctx:
                sb, ps, sem = tensors(ctx, f"_{k}")
                one_lo = [sb(f"s_lo{p}", [P, P, SUB], BF16) for p in range(2)]
                one_hi = [sb(f"s_hi{p}", [P, TILES, SUB], BF16) for p in range(2)]
                one_lo_t = [sb(f"s_lo_t{p}", [P, SUB, P]) for p in range(2)]
                equal = sb("s_equal", [P, SUB, P], BF16)
                before = [sb(f"s_before{p}", [P, SUB]) for p in range(2)]
                next_sb = [sb(f"s_next{p}", [P, SUB + 1, TILES]) for p in range(2)]
                picked = sb("s_picked", [P, SUB, TILES])
                base = sb("s_base", [P, SUB])
                place = [sb(f"s_place{p}", [P, SUB], I32) for p in range(2)]
                other = [sb(f"s_other{p}", [P, SUB], I32) for p in range(2)]
                key_row = ps("s_key_row", [P, SUB, P])
                lo_row = ps("s_lo_row", [P, SUB, P])
                fetched = sb("n_fetched", [P, TILES, BLOCK], I32)
                valid = sb("n_valid", [P, BLOCK])
                work = [[sb(f"n_work{m}{p}", [P, BLOCK]) for p in range(2)] for m in range(2)]
                top = [sb(f"n_top{m}", [P, BLOCK]) for m in range(2)]
                digit_i = sb("n_digit_i", [P, BLOCK], I32)
                masked_i = sb("n_masked_i", [P, BLOCK], I32)
                again = sb("n_again", [P, BLOCK])
                empty = sb("n_empty", [P, BLOCK])
                counted = sb("n_counted", [P, BLOCK])
                hi_of = sb("n_hi_of", [P, TILES, BLOCK], BF16)
                lo_of = sb("n_lo_of", [P, TILES, BLOCK], BF16)
                here = [sb(f"n_here{m}", [P, TILES, BLOCK >> max(m - 1, 0)], BF16) for m in range(4)]
                picked_rows = sb("n_picked_rows", [P, TILES], BF16)
                next_free = ps("s_next_free", [P, SUB + 1, TILES])
                list_did = sem("n_list_did")
                recorded = sem("n_recorded")
                info_loaded = sem("n_info_loaded")
                block_fetched = sem("n_block_fetched")
                looked = [ps(f"s_looked{p}", [P, SUB, TILES]) for p in range(2)]
                rows_made = sem("s_rows_made")
                rows_used = sem("s_rows_used")
                ones_made = sem("s_ones_made")
                next_updated = sem("s_next_updated")
                next_copied = sem("s_next_copied")
                looked_up = sem("s_looked_up")
                looked_free = sem("s_looked_free")
                place_made = sem("s_place_made")
                scattered = [sem(f"s_scattered{p}") for p in range(2)]
                block = ctx.enter_context(nc.Block())

                @block.tensor
                def _(pe):
                    def rows(b):
                        for c in range(SUB):
                            col = bass.ds(b * SUB + c, 1)
                            lo_of, hi_of = bc(lo_b[k][:, col], [P, P]), bc(hi_b[k][:, col], [P, P])
                            pe.matmul(lo_row[:, c, :], lo_of, ident_b[:, :], start=True, stop=True)
                            pe.matmul(key_row[:, c, :], lo_of, ident_b[:, :], start=True, stop=False)
                            last = pe.matmul(key_row[:, c, :], hi_of, ident_b[:, :], start=False, stop=True)
                        last.then_inc(rows_made, 1)

                    pe.sem_inc(looked_up, 2)
                    pe.sem_inc(next_updated, 1)
                    rows(0)
                    with pe.Fori(0, SUBS // 2) as i:
                        for p in range(2):
                            b = i * 2 + p
                            pe.wait_ge(next_copied, b + 1)
                            pe.wait_ge(ones_made, b + 1)
                            pe.matmul(next_free[:, :, :], ident[:, :],
                                      bc(next_sb[1 - p][:, SUB:SUB + 1, :], [P, SUB + 1, TILES]),
                                      start=True, stop=True)
                            for c in range(SUB):
                                last = pe.matmul(next_free[:, c + 1:SUB + 1, :], one_lo[p][:, :, c],
                                                 bc(one_hi[p][:, :, c].unsqueeze(1), [P, SUB - c, TILES]),
                                                 start=False, stop=True, skip_group_check=True)
                            last.then_inc(next_updated, 1)
                            pe.wait_ge(rows_used, b + 1)
                            rows(b + 1)
                            pe.wait_ge(next_copied, b + 2)
                            pe.wait_ge(looked_free, b + 1)
                            for c in range(SUB):
                                last = pe.matmul(looked[p][:, c, :], one_lo_t[p][:, c, :], next_sb[p][:, c, :],
                                                 start=True, stop=True)
                            last.then_inc(looked_up, 1)

                @block.scalar
                def _(act):
                    act.copy(next_sb[1][:, SUB, :], start[k][:, :]).then_inc(next_copied, 1)
                    with act.Fori(0, SUBS // 2) as i:
                        for p in range(2):
                            b = i * 2 + p
                            act.wait_ge(next_updated, b + 2)
                            act.wait_ge(looked_up, b + 1)
                            act.copy(next_sb[p][:, :, :], next_free[:, :, :]).then_inc(next_copied, 1)

                @block.sync
                def _(sp):
                    sp.wait_ge(recorded, TILES * 16)
                    sp.dma_start(row_info[k][:, 0:TILES, :], meta[k].rearrange("(t p) c -> p t c", p=P)
                                 ).then_inc(info_loaded, 16)
                    sp.wait_ge(info_loaded, 16)

                @block.vector
                def _(dve):
                    own = steps.of(dve)

                    listed = Count(dve, list_did)

                    def list_begin(t):
                        listed.did(dve.tensor_scalar(valid[:, :], iota_block[:, :], degree[1][:, bass.ds(t, 1)],
                                                     None, ALU.is_lt))
                        listed.wait()
                        listed.did(dve.scalar_tensor_tensor(
                            work[0][0][:, :], fetched[:, bass.ds(t, 1), :].squeeze(1), 1.0, valid[:, :],
                            ALU.add, ALU.mult))

                    def find(m, r, but):
                        listed.wait(but)
                        turn(dve, turns)
                        listed.did(dve.max(top[m][:, 8 * r:8 * r + 8], work[m][r % 2][:, :]))

                    def remove(m, r, but):
                        listed.wait(but)
                        turn(dve, turns)
                        listed.did(dve.match_replace(work[m][1 - r % 2][:, :], top[m][:, 8 * r:8 * r + 8],
                                                     work[m][r % 2][:, :], 0.0))

                    def list_end(t, but):
                        listed.wait(but)
                        listed.did(dve.scalar_tensor_tensor(
                            record[1][:, bass.ds(t, 1), INFO:INFO + BLOCK].squeeze(1), top[1][:, :], -1.0,
                            empty[:, :], ALU.add, ALU.add))

                    def list_split(t, n, but=0):
                        of_t = bass.ds(t, 1)
                        listed.wait(but)
                        if n == 0:
                            listed.did(dve.tensor_scalar(digit_i[:, :], top[0][:, :], -1.0, None, ALU.add))
                        elif n == 1:
                            listed.did(dve.tensor_scalar(masked_i[:, :], digit_i[:, :], P - 1, None,
                                                         ALU.bitwise_and))
                            listed.did(dve.tensor_scalar(digit_i[:, :], digit_i[:, :], 7, None,
                                                         ALU.arith_shift_right))
                        elif n == 2:
                            listed.did(dve.tensor_scalar(lo_of[:, of_t, :].squeeze(1), masked_i[:, :], 1.0, None,
                                                         ALU.add))
                            listed.did(dve.tensor_copy(hi_of[:, of_t, :].squeeze(1), digit_i[:, :]))
                            listed.did(dve.tensor_tensor(again[:, 1:BLOCK], digit_i[:, 1:BLOCK],
                                                         digit_i[:, 0:BLOCK - 1], ALU.is_equal))
                        elif n == 3:
                            listed.did(dve.tensor_tensor(work[1][0][:, :], again[:, :], top[0][:, :], ALU.mult))
                        else:
                            listed.did(dve.tensor_scalar(counted[:, :], work[1][0][:, :], 0.0, 0.0, ALU.is_gt,
                                                         ALU.add, accum_out=load[1][:, of_t]))

                    def list_step(t, n, ahead):
                        r, but = n // 2, int(ahead)
                        if n % 2 == 0:
                            find(1, r, but)
                            if ahead and n == 0:
                                list_begin(t + 1)
                            elif ahead:
                                remove(0, r - 1, but)
                        else:
                            if r < ROUNDS - 1:
                                remove(1, r, but)
                            else:
                                listed.wait(but)
                                listed.did(dve.tensor_scalar(empty[:, :], top[1][:, :], 0.0,
                                                             float(ZERO_ROW + 1), ALU.is_equal, ALU.mult))
                            if ahead:
                                find(0, r, but)

                    def list_close(t, n, ahead):
                        if n == 0:
                            list_end(t, int(ahead))
                        if ahead:
                            list_split(t + 1, n, but=int(n == 0))

                    def pick_step(s, n):
                        if n % 3 == 0 and n < 15:
                            listed.wait()
                        if n == 0:
                            listed.did(dve.tensor_scalar(here[0][:, :, :], hi_of[:, :, :], iota_row[:, bass.ds(s, 1)],
                                                         None, ALU.is_equal))
                        elif n == 3:
                            listed.did(dve.tensor_tensor(here[1][:, :, :], here[0][:, :, :], lo_of[:, :, :],
                                                         ALU.mult))
                        elif n == 6 or n == 9:
                            m, width = n // 3 - 1, BLOCK >> (n // 3 - 1)
                            listed.did(dve.tensor_tensor(here[m + 1][:, :, :], here[m][:, :, 0:width],
                                                         here[m][:, :, width:2 * width], ALU.max))
                        elif n == 12:
                            listed.did(dve.tensor_reduce(
                                record[1][:, :, bass.ds(s + (INFO + BLOCK), 1)].squeeze(2), here[3][:, :, :],
                                AX.X, ALU.max))

                    def build(b, p, beside=None):
                        one_hots(dve, k, b * SUB, one_lo[p], one_hi[p])
                        dve.wait_ge(rows_made, b + 1)
                        dve.tensor_scalar(one_lo_t[p][:, :, :], lo_row[:, :, :], iota_col[:, :], None,
                                          ALU.is_equal).then_inc(ones_made, 1)
                        for c in range(SUB):
                            last = dve.scalar_tensor_tensor(
                                equal[:, c, :], key_row[:, c, :], key_f[:, bass.ds(b * SUB + c, 1)], below[:, :],
                                ALU.is_equal, ALU.mult, accum_out=before[p][:, c:c + 1])
                            if c == SUB - 1:
                                last.then_inc(rows_used, 1)
                            if beside:
                                beside(c)

                    def finish(b, i, p, between=None):
                        def step(n):
                            if between:
                                between(n)
                        step(0)
                        dve.wait_ge(looked_up, b + 3)
                        own.wait()
                        own.did(dve.tensor_tensor(picked[:, :, :], looked[p][:, :, :],
                                                  one_hi[p][:, :, :].rearrange("p t c -> p c t"), ALU.mult))
                        step(1)
                        own.wait()
                        dve.sem_inc(looked_free, 1)
                        own.did(dve.tensor_reduce(base[:, :], picked[:, :, :], AX.X, ALU.add))
                        step(2)
                        own.wait()
                        dve.wait_ge(scattered[p], i * (SUB * 16))
                        dve.wait_ge(rows_used, b + 1)
                        own.did(dve.tensor_tensor(place[p][:, :], base[:, :], before[p][:, :], ALU.add))
                        own.did(dve.tensor_copy(other[p][:, :], ends_i[1 - k][:, bass.ds(b * SUB, SUB)]))
                        step(3)
                        own.wait()
                        dve.sem_inc(place_made, 1)
                        step(4)

                    key_f = sb_key
                    own.did(dve.scalar_tensor_tensor(key_f[:, :], hi[k][:, :], float(P), lo[k][:, :],
                                                     ALU.mult, ALU.add))
                    own.wait()
                    dve.sem_inc(looked_free, 2)
                    build(0, 0)
                    listed.did(dve.memset(again[:, 0:1], 0.0))
                    dve.wait_ge(block_fetched, TILES * 16)
                    list_begin(0)
                    for r in range(ROUNDS):
                        find(0, r, 0)
                        if r < ROUNDS - 1:
                            remove(0, r, 0)
                    for n in range(5):
                        list_split(0, n)

                    def two_steps(i, beside, between=None):
                        for p in range(2):
                            b = i * 2 + p
                            dve.wait_ge(next_updated, b + 1)
                            build(b + 1, 1 - p, lambda c: beside(p * SUB + c))
                            finish(b, i, p, between if p == 1 else None)

                    with dve.Fori(0, TILES - 1) as t:
                        own.enter(t, 8)
                        listed.enter(t, LIST_STEPS)
                        two_steps(t, lambda n: list_step(t, n, True), lambda n: list_close(t, n, True))
                        own.leave(TILES - 1)
                        listed.leave(TILES - 1)
                    two_steps(TILES - 1, lambda n: list_step(TILES - 1, n, False),
                              lambda n: list_close(TILES - 1, n, False))
                    with dve.Fori(0, TILES) as s:
                        own.enter(s, 8)
                        listed.enter(s, PICK_STEPS)
                        two_steps(s + TILES, lambda n: pick_step(s, n))
                        own.leave(TILES)
                        listed.leave(TILES)
                    listed.wait()
                    picks_of = record[1][:, :, INFO + BLOCK:RECORD[1]]
                    own.did(dve.tensor_scalar(picks_of, picks_of, fast[:, :], None, ALU.mult))
                    own.did(dve.tensor_scalar(load[1][:, :], load[1][:, :], fast[:, :], None, ALU.mult))
                    own.wait()
                    own.did(dve.scalar_tensor_tensor(load[1][:, :], degree[1][:, :], slow[1][:, :], load[1][:, :],
                                                     ALU.mult, ALU.add))
                    own.wait()
                    own.did(dve.tensor_copy(record[1][:, :, 1], load[1][:, :]))

                @block.gpsimd
                def _(pool):
                    for t in range(TILES):
                        pool.indirect_dma_start(fetched[:, t, :], None, nbrs[1],
                                                bass.IndirectOffsetOnAxis(record[1][:, t, 0:1], 0)
                                                ).then_inc(block_fetched, 16)
                    for t in range(TILES):
                        pool.indirect_dma_start(meta[k], bass.IndirectOffsetOnAxis(rank[k][:, t:t + 1], 0),
                                                record[k][:, t, :], None).then_inc(recorded, 16)
                    with pool.Fori(0, SUBS // 2) as i:
                        for p in range(2):
                            pool.wait_ge(place_made, i * 2 + p + 1)
                            turn(pool, turns)
                            for c in range(SUB):
                                pool.indirect_dma_start(
                                    nbrs[k], bass.IndirectOffsetOnAxis(place[p][:, c:c + 1], 0),
                                    other[p][:, c:c + 1], None).then_inc(scattered[p], 16)
                    for p in range(2):
                        pool.wait_ge(scattered[p], SUBS // 2 * SUB * 16)

        sb_key = ksb("s_key_f", [P, CHUNKS + SUB])
        sort(0)
        keys.close()

        def rstd_steps(dve, own, stats, mean, spread, rstd):
            own.wait()
            own.did(dve.tensor_tensor(mean[:, :], stats[:, :, 1], stats[:, :, 4], ALU.add))
            own.did(dve.tensor_tensor(spread[:, :], stats[:, :, 1], stats[:, :, 4], ALU.subtract))
            own.did(dve.tensor_tensor(rstd[:, :], stats[:, :, 2], stats[:, :, 5], ALU.add))
            own.wait()
            own.did(dve.tensor_scalar(mean[:, :], mean[:, :], 0.5, None, ALU.mult))
            own.did(dve.tensor_tensor(spread[:, :], spread[:, :], spread[:, :], ALU.mult))
            own.did(dve.tensor_scalar(rstd[:, :], rstd[:, :], 1.0 / D, 1e-5, ALU.mult, ALU.add))
            own.wait()
            own.did(dve.scalar_tensor_tensor(rstd[:, :], spread[:, :], 0.25, rstd[:, :], ALU.mult, ALU.add))
            own.wait()

        with ExitStack() as ctx:
            sb, ps, sem = tensors(ctx)
            x = sb("f_x", [P, TILES, D])
            h = sb("f_h", [P, TILES, D])
            ab = sb("f_ab", [P, TILES, 2 * D])
            w1 = sb("f_w1", [P, 2 * D])
            b1 = sb("f_b1", [1, 2 * D])
            stats = sb("f_stats", [P, TILES, 6])
            mean = sb("f_mean", [P, TILES])
            spread = sb("f_spread", [P, TILES])
            rstd = sb("f_rstd", [P, TILES])
            one_cols = sb("f_one_cols", [P, TILES, W0 - 2 * D])
            zero_rows = sb("f_zero_rows", [P, W0])
            h_stage = [sb(f"f_h_stage{q}", [P, HEAD, D]) for q in range(2)]
            h_t = [sb(f"f_h_t{q}", [P, HEAD, D]) for q in range(2)]
            turned = [ps(f"f_turned{q}", [P, HEAD, D]) for q in range(2)]
            product = [ps(f"f_product{q}", [P, HEAD, 2 * D]) for q in range(2)]
            x_clear = sem("f_x_clear")
            x_loaded = sem("f_x_loaded")
            var_made = sem("f_var_made")
            std_made = sem("f_std_made")
            centred = sem("f_centred")
            h_made = sem("f_h_made")
            h_staged = [sem(f"f_h_staged{q}") for q in range(2)]
            h_turned = [sem(f"f_h_turned{q}") for q in range(2)]
            h_copied = [sem(f"f_h_copied{q}") for q in range(2)]
            ab_made = [sem(f"f_ab_made{q}") for q in range(2)]
            ab_copied = [sem(f"f_ab_copied{q}") for q in range(2)]
            pads_made = sem("f_pads_made")
            stored = sem("f_stored")
            block = ctx.enter_context(nc.Block())

            def by_node(ap):
                return ap[0:NODES_PAD, :].rearrange("(t p) f -> p t f", p=P)

            @block.sync
            def _(sp):
                sp.dma_start(w1[:, 0:D], w1_in[0:D, :]).then_inc(w_loaded, 16)
                sp.dma_start(w1[:, D:2 * D], w1_in[D:2 * D, :]).then_inc(w_loaded, 16)
                sp.dma_start(x[:, 0:TILES - 1, :],
                             x_in[0:(TILES - 1) * P, :].rearrange("(t p) f -> p t f", p=P)
                             ).then_inc(x_loaded, 16)
                sp.wait_ge(x_clear, 2)
                sp.dma_start(x[0:LAST_ROWS, TILES - 1, :], x_in[(TILES - 1) * P:NODES, :]).then_inc(x_loaded, 16)
                sp.dma_start(b1[0:1, 0:D], b1_in.rearrange("(o n) -> o n", o=1)).then_inc(w_loaded, 16)
                sp.wait_ge(x_loaded, 32)
                sp.dma_start(by_node(own0)[:, :, 2 * D:3 * D], x[:, :, :]).then_inc(stored, 16)
                sp.wait_ge(pads_made, 2)
                sp.dma_start(by_node(table0)[:, :, 2 * D:W0], one_cols[:, :, :]).then_inc(stored, 16)
                sp.dma_start(table0[NODES_PAD:TABLE_ROWS, :], zero_rows[:, :]).then_inc(stored, 16)
                sp.dma_start(table1[NODES_PAD:TABLE_ROWS, :], zero_rows[:, 0:D]).then_inc(stored, 16)
                sp.wait_ge(h_made, 1)
                sp.dma_start(by_node(own0)[:, :, D:2 * D], h[:, :, :]).then_inc(stored, 16)
                sp.dma_start(by_node(table0)[:, :, D:2 * D], h[:, :, :]).then_inc(stored, 16)
                for q in range(2):
                    sp.wait_ge(ab_copied[q], PASSES)
                sp.dma_start(by_node(own0)[:, :, 0:D], ab[:, :, 0:D]).then_inc(stored, 16)
                sp.dma_start(by_node(table0)[:, :, 0:D], ab[:, :, D:2 * D]).then_inc(stored, 16)
                sp.wait_ge(stored, 8 * 16)

            @block.scalar
            def _(act):
                act.wait_ge(var_made, 1)
                act.sqrt(rstd[:, :], rstd[:, :]).then_inc(std_made, 1)
                act.wait_ge(centred, 1)
                act.activation(h[:, :, :], h[:, :, :], ACT.Relu).then_inc(h_made, 1)
                with act.Fori(0, PASSES) as i:
                    for q, _, n in halves(0):
                        act.wait_ge(h_turned[q], i + 1)
                        act.wait_ge(ab_made[q], i)
                        act.copy(h_t[q][:, 0:n, :], turned[q][:, 0:n, :]).then_inc(h_copied[q], 1)

            @block.gpsimd
            def _(pool):
                pool.wait_ge(h_made, 1)
                with pool.Fori(0, PASSES) as i:
                    for q, t, n in halves(i * PASS):
                        pool.wait_ge(h_turned[q], i)
                        pool.tensor_copy(h_stage[q][:, 0:n, :], h[:, bass.ds(t, n), :]).then_inc(h_staged[q], 1)

            @block.tensor
            def _(pe):
                pe.wait_ge(w_loaded, 3 * 16)
                with pe.Fori(0, PASSES) as i:
                    for q, t, n in halves(i * PASS):
                        pe.wait_ge(h_staged[q], i + 1)
                        pe.wait_ge(h_copied[q], i)
                        for c in range(n):
                            last = pe.transpose(turned[q][:, c, :], h_stage[q][:, c, :], ident[:, :])
                        last.then_inc(h_turned[q], 1)
                    for q, t, n in halves(i * PASS):
                        pe.wait_ge(h_copied[q], i + 1)
                        pe.wait_ge(ab_copied[q], i)
                        for c in range(n):
                            pe.matmul(product[q][:, c, :], h_t[q][:, c, :], w1[:, :], start=True, stop=False)
                            last = pe.matmul(product[q][:, c, :], ones[0:1, :], b1[0:1, :], start=False,
                                             stop=True)
                        last.then_inc(ab_made[q], 1)

            @block.vector
            def _(dve):
                own = steps.of(dve)
                dve.memset(x[:, TILES - 1, :], 0.0).then_inc(x_clear, 1)
                dve.memset(b1[:, :], 0.0).then_inc(x_clear, 1)
                own.did(dve.memset(one_cols[:, :, :], 0.0))
                own.wait()
                dve.memset(one_cols[:, :, 0:1], 1.0).then_inc(pads_made, 1)
                dve.memset(zero_rows[:, :], 0.0).then_inc(pads_made, 1)
                dve.wait_ge(x_loaded, 32)
                with dve.Fori(0, TILES) as t:
                    own.enter(t, 1)
                    own.did(dve.bn_stats(stats[:, bass.ds(t, 1), :].squeeze(1), x[:, bass.ds(t, 1), :].squeeze(1)))
                    own.leave(TILES)
                rstd_steps(dve, own, stats, mean, spread, rstd)
                dve.sem_inc(var_made, 1)
                dve.wait_ge(std_made, 1)
                own.did(dve.reciprocal(rstd[:, :], rstd[:, :]))
                own.did(dve.tensor_tensor(h[:, :, :], x[:, :, :], bc(mean[:, :].unsqueeze(2), [P, TILES, D]),
                                          ALU.subtract))
                own.wait()
                dve.tensor_tensor(h[:, :, :], h[:, :, :], bc(rstd[:, :].unsqueeze(2), [P, TILES, D]),
                                  ALU.mult).then_inc(centred, 1)
                with dve.Fori(0, PASSES) as i:
                    for q, t, n in halves(i * PASS):
                        dve.wait_ge(ab_made[q], i + 1)
                        dve.tensor_copy(ab[:, bass.ds(t, n), :], product[q][:, 0:n, :]).then_inc(ab_copied[q], 1)

        in_order = ExitStack()
        osb, _, _ = tensors(in_order)
        row_lists = [osb(f"row_lists{k}", [P, TILES, BLOCK], I32) for k in range(2)]
        row_picks = osb("row_picks", [P, TILES, TILES], I32)

        with ExitStack() as ctx:
            sb, ps, sem = tensors(ctx)
            ranking = rank_buffers(sb, ps, "r_")
            ranked = sem("r_ranked")
            recorded = sem("r_recorded")
            info_loaded = sem("r_info_loaded")
            block_fetched = sem("r_block_fetched")
            block = ctx.enter_context(nc.Block())

            @block.gpsimd
            def _(pool):
                for t in range(TILES):
                    pool.indirect_dma_start(row_lists[0][:, t, :], None, nbrs[0],
                                            bass.IndirectOffsetOnAxis(row_info[0][:, t, 0:1], 0)
                                            ).then_inc(block_fetched, 16)
                pool.wait_ge(ranked, 1)
                for t in range(TILES):
                    pool.indirect_dma_start(meta[1], bass.IndirectOffsetOnAxis(rank[1][:, t:t + 1], 0),
                                            record[1][:, t, :], None).then_inc(recorded, 16)
                pool.wait_ge(block_fetched, TILES * 16)

            @block.sync
            def _(sp):
                sp.wait_ge(recorded, TILES * 16)
                by_rank = meta[1].rearrange("(t p) c -> p t c", p=P)
                sp.dma_start(row_info[1][:, 0:TILES, :], by_rank[:, :, 0:INFO]).then_inc(info_loaded, 16)
                sp.dma_start(row_lists[1][:, :, :], by_rank[:, :, INFO:INFO + BLOCK]).then_inc(info_loaded, 16)
                sp.dma_start(row_picks[:, :, :], by_rank[:, :, INFO + BLOCK:RECORD[1]]).then_inc(info_loaded, 16)
                sp.wait_ge(info_loaded, 48)

            @block.tensor
            def _(pe):
                rank_products(pe, 1, ranking)

            @block.vector
            def _(dve):
                own = steps.of(dve)
                rank_sums(dve, own, 1, ranking)
                dve.sem_inc(ranked, 1)

        with ExitStack() as ctx:
            sb, ps, sem = tensors(ctx)
            deg = [sb(f"t_deg{k}", [P, LTILES]) for k in range(2)]
            most = sb("t_most", [LTILES, 1])
            counts_i = sb("t_counts_i", [LTILES, 2], I32)
            counts = [sb(f"t_counts{k}", [LTILES, 2]) for k in range(2)]
            value = sb("t_value", [P, TILES, BLOCK])
            shifted = sb("t_shifted", [P, TILES, BLOCK])
            laid = [sb(f"t_laid{k}", [P, QUICK_SLOTS], I32) for k in range(2)]
            laid_tile = [sb(f"t_laid_tile{k}", [1, QUICK_SLOTS // GROUP], I32) for k in range(2)]
            deg_t = ps("t_deg_t", [LTILES, P])
            sums = ps("t_sums", [1, 4 * LTILES + 4])
            a_did = sem("t_a_did")
            deg_made = sem("t_deg_made")
            deg_turned = sem("t_deg_turned")
            counts_made = sem("t_counts_made")
            sums_made = sem("t_sums_made")
            info_made = sem("t_info_made")
            laid_out = sem("t_laid_out")
            tiles_laid = sem("t_tiles_laid")
            stored = sem("t_stored")
            block = ctx.enter_context(nc.Block())

            @block.sync
            def _(sp):
                sp.wait_ge(laid_out, 1)
                for k in range(2):
                    sp.dma_start(slots[k][:, 0:QUICK_SLOTS], laid[k][:, :]).then_inc(stored, 16)
                    sp.wait_ge(tiles_laid, k + 1)
                    sp.dma_start(slot_tile[k][:, 0:QUICK_SLOTS // GROUP], laid_tile[k][:, :]).then_inc(stored, 16)
                sp.wait_ge(stored, 64)

            @block.tensor
            def _(pe):
                few = slice(0, LTILES)
                for k in range(2):
                    pe.wait_ge(deg_made, k + 1)
                    pe.transpose(deg_t[:, :], deg[k][:, :], ident[:, :]).then_inc(deg_turned, 1)
                    pe.wait_ge(counts_made, k + 1)
                    groups, blocks = counts[k][:, 0:1], counts[k][:, 1:2]
                    pe.matmul(sums[:, G_OFF:G_OFF + LTILES], groups, above[few, few], start=True, stop=True)
                    pe.matmul(sums[:, N_BLOCKS:N_BLOCKS + LTILES], blocks, ident[few, few], start=True, stop=True)
                    pe.matmul(sums[:, B_OFF:B_OFF + LTILES], blocks, above[few, few], start=True, stop=True)
                    pe.matmul(sums[:, QUICK_OFF:QUICK_OFF + LTILES], groups, above[few, few], start=True,
                              stop=True)
                    pe.matmul(sums[:, BODIES:BODIES + 1], groups, ones[few, 0:1], start=True,
                              stop=True).then_inc(sums_made, 1)

            @block.scalar
            def _(act):
                act.sem_inc(a_did, 1)
                for m, k in enumerate((0, 1)):
                    act.wait_ge(info_made, m + 1)
                    with act.Fori(0, TILES) as t:
                        first = act.value_load(tile_info[k][0:1, bass.ds(QUICK_OFF + t, 1)], min_val=0,
                                               max_val=TILES * BLOCK // GROUP)
                        act.wait_ge(a_did, m * TILES + t + 1)
                        act.copy(laid_tile[k][0:1, bass.ds(first, BLOCK // GROUP)],
                                 tile_ids[0:1, bass.ds(t, 1), :].squeeze(1)).then_inc(a_did, 1)
                    act.wait_ge(a_did, (m + 1) * TILES + 1)
                    act.sem_inc(tiles_laid, 1)

            @block.vector
            def _(dve):
                own = steps.of(dve)
                full = [P, TILES, BLOCK]

                def ceil_div(column, by):
                    own.did(dve.tensor_scalar(counts_i[:, column], most[:, :], float(by - 1), None, ALU.add))
                    own.wait()
                    own.did(dve.tensor_scalar(counts_i[:, column], counts_i[:, column], by.bit_length() - 1, None,
                                              ALU.arith_shift_right))
                    own.wait()

                for k in range(2):
                    own.did(dve.memset(laid[k][:, :], ZERO_ROW))
                    own.did(dve.memset(laid_tile[k][:, :], TILES))
                    own.did(dve.tensor_copy(deg[k][:, :], row_info[k][:, :, 1]))
                    own.wait()
                    dve.sem_inc(deg_made, 1)
                    dve.wait_ge(deg_turned, k + 1)
                    own.did(dve.tensor_reduce(most[:, :], deg_t[:, :], AX.X, ALU.max))
                    own.wait()
                    ceil_div(slice(0, 1), GROUP)
                    ceil_div(slice(1, 2), BLOCK)
                    own.did(dve.tensor_copy(counts[k][:, 0:1], counts_i[:, 0:1]))
                    own.did(dve.tensor_scalar(counts[k][:, 1:2], counts_i[:, 1:2], 1.0, None, ALU.max))
                    own.wait()
                    dve.sem_inc(counts_made, 1)
                    dve.wait_ge(sums_made, k + 1)
                    own.did(dve.tensor_copy(tile_info[k][:, 0:BODIES + 1], sums[:, 0:BODIES + 1]))
                    own.did(dve.tensor_copy(tile_info[k][:, SLOW:SLOW + 1], slow[k][0:1, :]))
                    own.wait()
                    quick = tile_info[k][:, QUICK_OFF:QUICK_OFF + LTILES]
                    own.did(dve.tensor_scalar(quick, quick, float(TILES * BLOCK // GROUP), None, ALU.min))
                    total = tile_info[k][:, BODIES:BODIES + 1]
                    own.did(dve.tensor_scalar(total, sums[:, BODIES:BODIES + 1], 1.0 / GROUPS[k],
                                              1.0 - 0.5 / GROUPS[k], ALU.mult, ALU.add))
                    own.wait()
                    if k == 1:
                        own.did(dve.tensor_scalar(total, total, float(TILES // 2), None, ALU.max))
                        own.wait()
                    dve.sem_inc(info_made, 1)
                own.did(dve.tensor_tensor(value[:, :, :], bc(iota_block[:, :].unsqueeze(1), full),
                                          bc(deg[0][:, 0:TILES].unsqueeze(2), full), ALU.is_lt))
                own.wait()
                own.did(dve.scalar_tensor_tensor(shifted[:, :, :], row_lists[0][:, :, :], float(-ZERO_ROW),
                                                 value[:, :, :], ALU.add, ALU.mult))
                own.wait()
                own.did(dve.tensor_scalar(row_lists[0][:, :, :], shifted[:, :, :], float(ZERO_ROW), None, ALU.add))
                own.wait()
                with dve.Fori(0, TILES) as t:
                    own.enter(t, 2)
                    first = [dve.value_load(tile_info[k][0:1, bass.ds(QUICK_OFF + t, 1)], min_val=0,
                                            max_val=TILES * BLOCK // GROUP) for k in range(2)]
                    own.wait()
                    for k in range(2):
                        own.did(dve.tensor_copy(laid[k][:, bass.ds(first[k] * GROUP, BLOCK)],
                                                row_lists[k][:, bass.ds(t, 1), :].squeeze(1)))
                    own.leave(TILES)
                own.wait()
                dve.sem_inc(laid_out, 1)

        with ExitStack() as ctx:
            sb, ps, sem = tensors(ctx)
            picks_b = sb("p_picks_b", [P, TILES, P], BF16)
            turned_b = sb("p_turned_b", [TILES, NODES_PAD], BF16)
            turned = [ps(f"p_turned{q}", [P, HEAD, P], BF16) for q in range(2)]
            ready = sem("p_ready")
            tile_turned = [sem(f"p_tile_turned{q}") for q in range(2)]
            tile_copied = [sem(f"p_tile_copied{q}") for q in range(2)]
            picks_stored = sem("p_picks_stored")
            block = ctx.enter_context(nc.Block())

            @block.tensor
            def _(pe):
                pe.wait_ge(ready, 1)
                with pe.Fori(0, PASSES) as i:
                    for q, t, n in halves(i * PASS):
                        pe.wait_ge(tile_copied[q], i + 1)
                        for c in range(n):
                            last = pe.transpose(turned[q][:, c, :], picks_b[:, bass.ds(t + c, 1), :].squeeze(1),
                                                ident_b[:, :])
                        last.then_inc(tile_turned[q], 1)

            @block.scalar
            def _(act):
                for q in range(2):
                    act.sem_inc(tile_copied[q], 1)
                with act.Fori(0, PASSES) as i:
                    for q, t, n in halves(i * PASS):
                        act.wait_ge(tile_turned[q], i + 1)
                        act.copy(turned_b[:, bass.ds(t * P, n * P)],
                                 turned[q][0:TILES, 0:n, :].rearrange("p c m -> p (c m)")).then_inc(tile_copied[q], 1)
                for q in range(2):
                    act.wait_ge(tile_copied[q], PASSES + 1)
                act.dma_start(picks[:, :], turned_b[:, :]).then_inc(picks_stored, 16)
                act.wait_ge(picks_stored, 16)

            @block.vector
            def _(dve):
                own = steps.of(dve)
                own.did(dve.memset(picks_b[:, :, :], 0.0))
                own.wait()
                own.did(dve.tensor_copy(picks_b[:, :, 0:TILES], row_picks[:, :, :]))
                own.did(dve.tensor_scalar(one_up[:, :], iota_col[:, :], 1.0, None, ALU.add))
                own.wait()
                dve.sem_inc(ready, 1)
        in_order.close()
        lists.close()

        def tile_value(eng, k, field, t, most):
            return eng.value_load(tile_info[k][0:1, bass.ds(field + t, 1)], min_val=0, max_val=most)

        BLOCKS_MAX = TILES + EDGES // BLOCK + 1

        def lay_out(k):
            with ExitStack() as ctx:
                sb, ps, sem = tensors(ctx, f"_{k}")
                at = sb("l_at", [P, 1])
                left = sb("l_left", [P, 1])
                where = sb("l_where", [P, 1], I32)
                fetched = sb("l_fetched", [P, BLOCK], I32)
                valid = sb("l_valid", [P, BLOCK])
                shifted = sb("l_shifted", [P, BLOCK])
                laid = sb("l_laid", [P, BLOCK], I32)
                v_did = sem("l_v_did")
                where_made = sem("l_where_made")
                block_fetched = sem("l_block_fetched")
                block_laid = sem("l_block_laid")
                block_written = sem("l_block_written")
                block = ctx.enter_context(nc.Block())

                def tile_loop(eng, body):
                    with eng.Fori(0, LTILES) as t:
                        blocks = tile_value(eng, k, N_BLOCKS, t, BLOCKS_MAX)
                        before = tile_value(eng, k, B_OFF, t, BLOCKS_MAX)
                        body(t, blocks, before)

                def is_slow(eng):
                    return eng.If(tile_value(eng, k, SLOW, 0, 1) > 0)

                @block.vector
                def _(dve):
                    def body(t, blocks, before):
                        base = t * 2 + before * 6 + 1
                        dve.wait_ge(v_did, base)
                        dve.tensor_copy(at[:, :], row_info[k][:, bass.ds(t, 1), 0]).then_inc(v_did, 1)
                        dve.tensor_copy(left[:, :], row_info[k][:, bass.ds(t, 1), 1]).then_inc(v_did, 1)
                        with dve.Fori(0, blocks) as b:
                            n = before + b
                            done = base + b * 6 + 2
                            dve.wait_ge(v_did, done)
                            dve.tensor_scalar(where[:, :], at[:, :], float(EDGES_PAD - BLOCK), None,
                                              ALU.min).then_inc(v_did, 1)
                            dve.wait_ge(v_did, done + 1)
                            dve.sem_inc(where_made, 1)
                            dve.tensor_scalar(at[:, :], at[:, :], float(BLOCK), None, ALU.add).then_inc(v_did, 1)
                            dve.tensor_scalar(valid[:, :], iota_block[:, :], left[:, :], None,
                                              ALU.is_lt).then_inc(v_did, 1)
                            dve.wait_ge(v_did, done + 3)
                            dve.tensor_scalar(left[:, :], left[:, :], float(-BLOCK), None,
                                              ALU.add).then_inc(v_did, 1)
                            dve.wait_ge(block_fetched, n * 16 + 16)
                            dve.scalar_tensor_tensor(shifted[:, :], fetched[:, :], float(-ZERO_ROW), valid[:, :],
                                                     ALU.add, ALU.mult).then_inc(v_did, 1)
                            dve.wait_ge(v_did, done + 5)
                            dve.wait_ge(block_written, n * 32 + 1)
                            dve.tensor_scalar(laid[:, :], shifted[:, :], float(ZERO_ROW), None,
                                              ALU.add).then_inc(v_did, 1)
                            dve.wait_ge(v_did, done + 6)
                            dve.sem_inc(block_laid, 1)
                    with is_slow(dve):
                        dve.sem_inc(v_did, 1)
                        dve.sem_inc(block_laid, 1)
                        tile_loop(dve, body)

                @block.gpsimd
                def _(pool):
                    def body(t, blocks, before):
                        with pool.Fori(0, blocks) as b:
                            n = before + b
                            pool.wait_ge(where_made, n + 1)
                            pool.wait_ge(block_laid, n + 1)
                            turn(pool, turns)
                            pool.indirect_dma_start(fetched[:, :], None, nbrs[k],
                                                    bass.IndirectOffsetOnAxis(where[:, 0:1], 0)
                                                    ).then_inc(block_fetched, 16)
                    with is_slow(pool):
                        tile_loop(pool, body)

                @block.sync
                def _(sp):
                    def body(t, blocks, before):
                        first = tile_value(sp, k, G_OFF, t, SLOTS_MAX // GROUP - BLOCK // GROUP)
                        with sp.Fori(0, blocks) as b:
                            n = before + b
                            sp.wait_ge(block_written, n * 32 + 1)
                            turn(sp, turns)
                            sp.wait_ge(block_laid, n + 2)
                            at_group = nc.s_assert_within(
                                first + b * (BLOCK // GROUP), 0, (SLOTS_MAX - BLOCK) // GROUP,
                                skip_runtime_bounds_check_because="SLOTS_MAX bounds all tiles' slots")
                            sp.dma_start(slots[k][:, bass.ds(at_group * GROUP, BLOCK)],
                                         laid[:, :]).then_inc(block_written, 16)
                            sp.dma_start(slot_tile[k][:, bass.ds(at_group, BLOCK // GROUP)],
                                         tile_ids[0:1, bass.ds(t, 1), :].squeeze(1)).then_inc(block_written, 16)
                    with is_slow(sp):
                        sp.sem_inc(block_written, 1)
                        tile_loop(sp, body)
                        total = tile_value(sp, k, B_OFF, LTILES - 1, BLOCKS_MAX)
                        sp.wait_ge(block_written, total * 32 + 33)
                        turn(sp, turns)

        for k in range(2):
            lay_out(k)

        def shares(k):
            first = (GROUPS[k] + 1) // 2
            return (0, 0, first), (1, first, GROUPS[k] - first)

        def share_of(k, g):
            first = (GROUPS[k] + 1) // 2
            return (0, g) if g < first else (1, g - first)

        def load_slots(sp, k, before, bodies, slot_rows, slot_tiles, rows_loaded, group_used):
            groups = GROUPS[k]
            with sp.Fori(0, bodies) as j:
                n = before + j
                for q, first, count in shares(k):
                    sp.wait_ge(group_used, n * groups + (first + count))
                    at_slot = nc.s_assert_within(j * BODY[k] + first * GROUP, 0, SLOTS_MAX - count * GROUP,
                                                 skip_runtime_bounds_check_because="bodies of the tiles' slots")
                    at_group = nc.s_assert_within(j * groups + first, 0, SLOTS_MAX // GROUP - count,
                                                  skip_runtime_bounds_check_because="groups of the tiles' slots")
                    sp.dma_start(slot_rows[q][:, :], slots[k][:, bass.ds(at_slot, count * GROUP)]
                                 ).then_inc(rows_loaded[q], 16)
                    sp.dma_start(slot_tiles[q][:, :], slot_tile[k][:, bass.ds(at_group, count)]
                                 ).then_inc(rows_loaded[q], 16)

        def gather(pool, k, before, bodies, table, rows, slot_rows, rows_loaded, group_used, gathered):
            groups = GROUPS[k]
            with pool.Fori(0, bodies) as j:
                n = before + j
                for g in range(groups):
                    q, place = share_of(k, g)
                    first = place * GROUP
                    if place == 0:
                        pool.wait_ge(rows_loaded[q], n * 32 + 32)
                    pool.wait_ge(group_used, n * groups + g + 1)
                    turn(pool, turns)
                    for s in range(GROUP):
                        pool.indirect_dma_start(
                            rows[g][:, s, :], None, table,
                            bass.IndirectOffsetOnAxis(slot_rows[q][:, first + s:first + s + 1], 0)
                        ).then_inc(gathered[g], 16)

        def bodies_of(eng, k):
            return eng.value_load(tile_info[k][0:1, BODIES:BODIES + 1], min_val=0, max_val=SLOTS_MAX // BODY[k])

        with ExitStack() as ctx:
            sb, ps, sem = tensors(ctx)
            own_rows = sb("a_own_rows", [P, TILES + 1, 3 * D])
            acc = sb("a_acc", [P, TILES + 1, A0])
            rows = [sb(f"a_rows{g}", [P, GROUP, W0]) for g in range(GROUPS[0])]
            slot_rows = [sb(f"a_slot_rows{q}", [P, n * GROUP], I32) for q, _, n in shares(0)]
            slot_tiles = [sb(f"a_slot_tiles{q}", [1, n], I32) for q, _, n in shares(0)]
            hidden = [sb(f"a_hidden{p}", [P, GROUP, D]) for p in range(2)]
            weighed = sb("a_weighed", [P, GROUP, D])
            logit = [sb(f"a_logit{g}", [P, GROUP]) for g in range(GROUPS[0])]
            mask = [sb(f"a_mask{g}", [P, GROUP]) for g in range(GROUPS[0])]
            pick_row = sb("a_pick_row", [P, NODES_PAD], BF16)
            is_pick = sb("a_is_pick", [P, NODES_PAD], F8)
            w2 = sb("a_w2", [P, D])
            b2 = sb("a_b2", [P, 1])
            wl = sb("a_wl", [P, D])
            bl = sb("a_bl", [1, D])
            per_mask = sb("a_per_mask", [P, TILES])
            has_half = sb("a_has_half", [P, TILES])
            emb = [sb(f"a_emb{q}", [P, HEAD, D]) for q in range(2)]
            emb_t = [sb(f"a_emb_t{q}", [P, HEAD, D]) for q in range(2)]
            stats = sb("a_stats", [P, TILES, 6])
            mean = sb("a_mean", [P, TILES])
            spread = sb("a_spread", [P, TILES])
            rstd = sb("a_rstd", [P, TILES])
            turned = [ps(f"a_turned{q}", [P, HEAD, D]) for q in range(2)]
            product = [ps(f"a_product{q}", [P, HEAD, D]) for q in range(2)]
            own_gathered = sem("a_own_gathered")
            v_did = sem("a_v_did")
            rows_loaded = [sem(f"a_rows_loaded{q}") for q in range(2)]
            gathered = [sem(f"a_gathered{g}") for g in range(GROUPS[0])]
            pick_row_loaded = sem("a_pick_row_loaded")
            compared = sem("a_compared")
            choice_stored = sem("a_choice_stored")
            group_used = sem("a_group_used")
            logit_made = sem("a_logit_made")
            mask_made = sem("a_mask_made")
            emb_made = [sem(f"a_emb_made{q}") for q in range(2)]
            emb_turned = [sem(f"a_emb_turned{q}") for q in range(2)]
            emb_copied = [sem(f"a_emb_copied{q}") for q in range(2)]
            product_made = [sem(f"a_product_made{q}") for q in range(2)]
            product_used = [sem(f"a_product_used{q}") for q in range(2)]
            var_made = sem("a_var_made")
            std_made = sem("a_std_made")
            centred = sem("a_centred")
            h_made = sem("a_h_made")
            stored = sem("a_stored")
            block = ctx.enter_context(nc.Block())
            own_a, own_h, own_x = (slice(c * D, (c + 1) * D) for c in range(3))

            @block.sync
            def _(sp):
                bodies = bodies_of(sp, 0)
                load_slots(sp, 0, 0, bodies, slot_rows, slot_tiles, rows_loaded, group_used)

            @block.gpsimd
            def _(pool):
                for t in range(TILES):
                    pool.indirect_dma_start(own_rows[:, t, :], None, own0,
                                            bass.IndirectOffsetOnAxis(row_info[0][:, t, 2:3], 0)
                                            ).then_inc(own_gathered, 16)
                bodies = bodies_of(pool, 0)
                gather(pool, 0, 0, bodies, table0, rows, slot_rows, rows_loaded, group_used, gathered)
                pool.wait_ge(h_made, 1)
                for t in range(TILES):
                    node_of = bass.IndirectOffsetOnAxis(row_info[0][:, t, 2:3], 0)
                    pool.indirect_dma_start(own1, node_of, own_rows[:, t, own_x], None).then_inc(stored, 16)
                    pool.indirect_dma_start(table1, node_of, own_rows[:, t, own_h], None).then_inc(stored, 16)
                pool.wait_ge(stored, 2 * TILES * 16)

            @block.scalar
            def _(act):
                act.dma_start(w2[:, :], bc(w2_in.rearrange("k o -> o k"), [P, D])).then_inc(w_loaded, 16)
                act.dma_start(b2[:, :], bc(b2_in.rearrange("(o n) -> o n", o=1), [P, 1])).then_inc(w_loaded, 16)
                act.dma_start(wl[:, :], wl_in).then_inc(w_loaded, 16)
                act.dma_start(bl[:, :], bl_in.rearrange("(o n) -> o n", o=1)).then_inc(w_loaded, 16)
                act.wait_ge(w_loaded, (3 + 4) * 16)
                bodies = bodies_of(act, 0)

                def masks(j):
                    for g in range(GROUPS[0]):
                        act.wait_ge(logit_made, j * GROUPS[0] + g + 1)
                        act.activation(mask[g][:, :], logit[g][:, :], ACT.Sigmoid,
                                       bias=b2[:, :]).then_inc(mask_made, 1)
                act.sem_inc(compared, 1)
                act.sem_inc(choice_stored, 1)
                with act.Fori(0, TILES) as s:
                    act.wait_ge(compared, s + 1)
                    act.dma_start(pick_row[:, :], bc(picks[bass.ds(s, 1), :], [P, NODES_PAD])
                                  ).then_inc(pick_row_loaded, 16)
                    masks(s)
                    act.wait_ge(compared, s + 2)
                    act.dma_start(chosen[bass.ds(s, 1), :, :].squeeze(0),
                                  is_pick[:, :].bitcast(U8)).then_inc(choice_stored, 16)
                with act.If(bodies > TILES):
                    with act.Fori(TILES, bodies) as j:
                        masks(j)
                act.wait_ge(choice_stored, TILES * 16 + 1)
                with act.Fori(0, PASSES) as i:
                    for q, _, n in halves(0):
                        act.wait_ge(emb_turned[q], i + 1)
                        act.wait_ge(product_made[q], i)
                        act.copy(emb_t[q][:, 0:n, :], turned[q][:, 0:n, :]).then_inc(emb_copied[q], 1)
                act.wait_ge(var_made, 1)
                act.sqrt(rstd[:, :], rstd[:, :]).then_inc(std_made, 1)
                act.wait_ge(centred, 1)
                h1 = own_rows[:, 0:TILES, own_h]
                act.activation(h1, h1, ACT.Relu).then_inc(h_made, 1)

            @block.tensor
            def _(pe):
                pe.wait_ge(w_loaded, (3 + 4) * 16)
                with pe.Fori(0, PASSES) as i:
                    for q, t, n in halves(i * PASS):
                        pe.wait_ge(emb_made[q], i + 1)
                        pe.wait_ge(emb_copied[q], i)
                        for c in range(n):
                            last = pe.transpose(turned[q][:, c, :], emb[q][:, c, :], ident[:, :])
                        last.then_inc(emb_turned[q], 1)
                    for q, t, n in halves(i * PASS):
                        pe.wait_ge(emb_copied[q], i + 1)
                        pe.wait_ge(product_used[q], i)
                        for c in range(n):
                            pe.matmul(product[q][:, c, :], emb_t[q][:, c, :], wl[:, :], start=True, stop=False)
                            last = pe.matmul(product[q][:, c, :], ones[0:1, :], bl[0:1, :], start=False,
                                             stop=True)
                        last.then_inc(product_made[q], 1)

            @block.vector
            def _(dve):
                own = Count(dve, v_did)
                own.did(dve.memset(acc[:, :, :], 0.0))
                own.did(dve.memset(own_rows[:, TILES, :], 0.0))
                own.wait()
                dve.sem_inc(group_used, GROUPS[0])
                dve.wait_ge(w_loaded, (3 + 4) * 16)
                dve.wait_ge(own_gathered, TILES * 16)
                bodies = bodies_of(dve, 0)

                def body(j):
                    tiles = []
                    for g in range(GROUPS[0] + 1):
                        if g < GROUPS[0]:
                            q, place = share_of(0, g)
                            if place == 0:
                                dve.wait_ge(rows_loaded[q], j * 32 + 32)
                                turn(dve, turns)
                            tiles.append(dve.value_load(slot_tiles[q][0:1, place:place + 1],
                                                        min_val=0, max_val=TILES))
                            dve.wait_ge(gathered[g], j * (GROUP * 16) + GROUP * 16)
                            a = own_rows[:, bass.ds(tiles[g], 1), own_a]
                            own.did(dve.tensor_tensor(hidden[g % 2][:, :, :], rows[g][:, :, 0:D],
                                                      bc(a, [P, GROUP, D]), ALU.add))
                            own.wait()
                            for s in range(GROUP):
                                last = dve.scalar_tensor_tensor(
                                    weighed[:, s, :], hidden[g % 2][:, s, :], 0.0, w2[:, :], ALU.max, ALU.mult,
                                    accum_out=logit[g][:, s:s + 1])
                            last.then_inc(logit_made, 1)
                        if g > 0:
                            f = g - 1
                            dve.wait_ge(mask_made, j * GROUPS[0] + f + 1)
                            sums = acc[:, bass.ds(tiles[f], 1), 0:D + 1].squeeze(1)
                            for s in range(GROUP):
                                own.wait()
                                own.did(dve.scalar_tensor_tensor(
                                    sums, rows[f][:, s, D:2 * D + 1], mask[f][:, s:s + 1], sums,
                                    ALU.mult, ALU.add))
                            own.wait()
                            dve.sem_inc(group_used, 1)

                with dve.Fori(0, TILES) as s:
                    own.enter(s, GROUPS[0] * (1 + GROUP))
                    body(s)
                    dve.wait_ge(pick_row_loaded, s * 16 + 16)
                    dve.wait_ge(choice_stored, s * 16 + 1)
                    turn(dve, turns)
                    dve.tensor_scalar(is_pick[:, :], pick_row[:, :], one_up[:, :], None, ALU.is_equal,
                                      saturate=False).then_inc(compared, 1)
                    own.leave(TILES)
                with dve.If(bodies > TILES):
                    with dve.Fori(TILES, bodies) as j:
                        own.enter(j - TILES, GROUPS[0] * (1 + GROUP))
                        body(j)
                        own.leave(bodies - TILES)
                own.wait()
                own.did(dve.tensor_scalar(per_mask[:, :], acc[:, 0:TILES, D], 1e-9, None, ALU.add))
                own.did(dve.tensor_scalar(has_half[:, :], row_info[0][:, 0:TILES, 1], 0.0, 0.5,
                                          ALU.is_gt, ALU.mult))
                own.wait()
                own.did(dve.reciprocal(per_mask[:, :], per_mask[:, :]))
                own.wait()
                turn(dve, turns)
                with dve.Fori(0, PASSES) as i:
                    own.enter(i, 3 * PASS)
                    for q, t, n in halves(i * PASS):
                        dve.wait_ge(emb_turned[q], i)
                        for c in range(n):
                            col = bass.ds(t + c, 1)
                            h_of = own_rows[:, col, own_h].squeeze(1)
                            own.did(dve.scalar_tensor_tensor(
                                emb[q][:, c, :], acc[:, col, 0:D].squeeze(1), per_mask[:, col], h_of,
                                ALU.mult, ALU.subtract))
                            own.wait()
                            own.did(dve.scalar_tensor_tensor(
                                emb[q][:, c, :], emb[q][:, c, :], has_half[:, col], h_of, ALU.mult, ALU.add))
                        own.wait()
                        dve.sem_inc(emb_made[q], 1)
                    for q, t, n in halves(i * PASS):
                        dve.wait_ge(product_made[q], i + 1)
                        x_of = own_rows[:, bass.ds(t, n), own_x]
                        dve.scalar_tensor_tensor(x_of, product[q][:, 0:n, :], 0.0, x_of, ALU.max,
                                                 ALU.add).then_inc(product_used[q], 1)
                        dve.wait_ge(product_used[q], i + 1)
                        for c in range(n):
                            own.did(dve.bn_stats(stats[:, bass.ds(t + c, 1), :].squeeze(1),
                                                 own_rows[:, bass.ds(t + c, 1), own_x].squeeze(1)))
                    own.leave(PASSES)
                rstd_steps(dve, own, stats, mean, spread, rstd)
                dve.sem_inc(var_made, 1)
                dve.wait_ge(std_made, 1)
                own.did(dve.reciprocal(rstd[:, :], rstd[:, :]))
                h1 = own_rows[:, 0:TILES, own_h]
                own.did(dve.tensor_tensor(h1, own_rows[:, 0:TILES, own_x],
                                          bc(mean[:, :].unsqueeze(2), [P, TILES, D]), ALU.subtract))
                own.wait()
                dve.tensor_tensor(h1, h1, bc(rstd[:, :].unsqueeze(2), [P, TILES, D]),
                                  ALU.mult).then_inc(centred, 1)

        LAYERS = 4
        with ExitStack() as ctx:
            sb, ps, sem = tensors(ctx)
            own_x1 = sb("c_own_x1", [P, TILES, D])
            new = sb("c_new", [P, TILES, D])
            acc = sb("c_acc", [P, TILES + 1, D])
            acc_t = sb("c_acc_t", [P, NODES_PAD])
            h_t = sb("c_h_t", [P, NODES_PAD])
            rows = [sb(f"c_rows{g}", [P, GROUP, D]) for g in range(GROUPS[1])]
            pairs = sb("c_pairs", [P, 2, D])
            best = sb("c_best", [P, D])
            slot_rows = [sb(f"c_slot_rows{q}", [P, n * GROUP], I32) for q, _, n in shares(1)]
            slot_tiles = [sb(f"c_slot_tiles{q}", [1, n], I32) for q, _, n in shares(1)]
            source = [sb(f"c_source{p}", [P, D]) for p in range(2)]
            rest = [sb(f"c_rest{m}", [P, D]) for m in range(2)]
            parts = [sb(f"c_parts{p}", [P, 3, D], BF16) for p in range(2)]
            choice = [sb(f"c_choice{p}", [P, NODES_PAD], F8) for p in range(2)]
            w = [sb(f"c_w{m}", [P, D]) for m in range(2)]
            r = [sb(f"c_r{m}", [P, D]) for m in range(2)]
            b = [sb(f"c_b{m}", [P, 1]) for m in range(2)]
            w_now = sb("c_w_now", [P, D])
            r_now = sb("c_r_now", [P, D])
            b_now = sb("c_b_now", [P, 1])
            stage = [sb(f"c_stage{q}", [P, HEAD, D]) for q in range(2)]
            new_t = [sb(f"c_new_t{q}", [P, HEAD, D]) for q in range(2)]
            wide = [ps(f"c_wide{q}", [P, 2 * BANK]) for q in range(WIDE)]
            product = [wide[q][:, 0:BANK].rearrange("p (c m) -> p c m", m=D) for q in range(2)]
            back = [wide[q][:, BANK:2 * BANK].rearrange("p (c m) -> p c m", m=D) for q in range(2)]
            turned = [wide[2 + q][:, 0:BANK].rearrange("p (c m) -> p c m", m=D) for q in range(2)]
            own_gathered = sem("c_own_gathered")
            v_did = sem("c_v_did")
            weights_set = sem("c_weights_set")
            rows_loaded = [sem(f"c_rows_loaded{q}") for q in range(2)]
            gathered = [sem(f"c_gathered{g}") for g in range(GROUPS[1])]
            group_used = sem("c_group_used")
            choice_loaded = [sem(f"c_choice_loaded{p}") for p in range(2)]
            rest_made = sem("c_rest_made")
            parts_made = sem("c_parts_made")
            part_selected = sem("c_part_selected")
            part_used = sem("c_part_used")
            source_loaded = [sem(f"c_source_loaded{p}") for p in range(2)]
            tile_done = sem("c_tile_done")
            maxima_done = sem("c_maxima_done")
            staged = [sem(f"c_staged{q}") for q in range(2)]
            tile_turned = [sem(f"c_tile_turned{q}") for q in range(2)]
            tile_copied = [sem(f"c_tile_copied{q}") for q in range(2)]
            product_made = [sem(f"c_product_made{q}") for q in range(2)]
            new_made = [sem(f"c_new_made{q}") for q in range(2)]
            new_turned = [sem(f"c_new_turned{q}") for q in range(2)]
            new_out = [sem(f"c_new_out{q}") for q in range(2)]
            table_stored = sem("c_table_stored")
            table_ready = sem("c_table_ready")
            out_stored = sem("c_out_stored")
            block = ctx.enter_context(nc.Block())
            STEPS = TILES * PARTS
            PAIRS = TILES // 2
            EVENS, ODDS = PAIRS + 1, PAIRS

            def uses(layer, s_pair, p, first):
                return layer * EVENS if first else layer * ODDS + s_pair if p else layer * EVENS + s_pair + 1

            def over_sources(eng, layer, body):
                body(0, uses(layer, 0, 0, True), 0)
                with eng.Fori(0, PAIRS) as i:
                    for p in (1, 0):
                        body(i * 2 + 2 - p, uses(layer, i, p, False), p)

            @block.sync
            def _(sp):
                for m, (wi, ri, bi) in enumerate(((gw1_in, gr1_in, gb1_in), (gw2_in, gr2_in, gb2_in))):
                    sp.dma_start(w[m][:, :], wi).then_inc(w_loaded, 16)
                    sp.dma_start(r[m][:, :], ri).then_inc(w_loaded, 16)
                    sp.dma_start(b[m][:, :], bi.rearrange("(k o) -> k o", o=1)).then_inc(w_loaded, 16)
                bodies = bodies_of(sp, 1)
                with sp.Fori(0, LAYERS) as layer:
                    load_slots(sp, 1, layer * bodies, bodies, slot_rows, slot_tiles, rows_loaded, group_used)

            @block.gpsimd
            def _(pool):
                for t in range(TILES):
                    node_of = bass.IndirectOffsetOnAxis(row_info[1][:, t, 2:3], 0)
                    pool.indirect_dma_start(own_x1[:, t, :], None, own1, node_of).then_inc(own_gathered, 16)
                    pool.indirect_dma_start(new[:, t, :], None, table1, node_of).then_inc(own_gathered, 16)
                bodies = bodies_of(pool, 1)
                pool.sem_inc(table_ready, 1)
                with pool.Fori(0, LAYERS) as layer:
                    pool.wait_ge(table_ready, layer + 1)
                    turn(pool, turns)
                    gather(pool, 1, layer * bodies, bodies, table1, rows, slot_rows, rows_loaded, group_used,
                           gathered)
                    pool.wait_ge(maxima_done, layer + 1)
                    turn(pool, turns)
                    with pool.If(layer < LAYERS - 1):
                        for t in range(TILES):
                            q = int(t % PASS >= HEAD)
                            if t % PASS in (0, HEAD):
                                pool.wait_ge(new_out[q], layer * PASSES + t // PASS + 2)
                                turn(pool, turns)
                            pool.indirect_dma_start(table1, bass.IndirectOffsetOnAxis(row_info[1][:, t, 2:3], 0),
                                                    new[:, t, :], None).then_inc(table_stored, 16)
                        pool.wait_ge(table_stored, layer * (TILES * 16) + TILES * 16)
                        pool.sem_inc(table_ready, 1)
                    with pool.Else():
                        for t in range(TILES):
                            q = int(t % PASS >= HEAD)
                            if t % PASS in (0, HEAD):
                                pool.wait_ge(new_out[q], (LAYERS - 1) * PASSES + t // PASS + 2)
                            pool.indirect_dma_start(out, bass.IndirectOffsetOnAxis(row_info[1][:, t, 2:3], 0),
                                                    new[:, t, :], None, bounds_check=NODES - 1,
                                                    oob_is_err=False).then_inc(out_stored, 16)
                pool.wait_ge(out_stored, TILES * 16)

            @block.scalar
            def _(act):
                for q in range(2):
                    act.sem_inc(new_made[q], 1)
                act.sem_inc(parts_made, 1)
                with act.Fori(0, PASSES) as i:
                    for q, t, n in halves(i * PASS):
                        act.wait_ge(tile_turned[q], i + 2)
                        act.copy(h_t[:, bass.ds(t * P, n * P)],
                                 turned[q][:, 0:n, :].rearrange("p c m -> p (c m)")).then_inc(tile_copied[q], 1)

                with act.Fori(0, LAYERS) as layer:
                    act.wait_ge(table_ready, layer + 1)
                    turn(act, turns)

                    def split(s, used, p):
                        done = layer * STEPS + s * PARTS
                        act.wait_ge(tile_done, layer * TILES + s + 1)
                        turn(act, turns)
                        act.dma_start(choice[p][:, :].bitcast(U8),
                                      chosen[bass.ds(s, 1), :, :].squeeze(0)).then_inc(choice_loaded[p], 16)
                        act.dma_start(source[p][:, :], table1[bass.ds(s * P, P), :]).then_inc(source_loaded[p], 16)
                        return done

                    def convert(s, used, p):
                        act.wait_ge(source_loaded[p], used * 16 + 16)
                        n = layer * TILES + s
                        act.copy(parts[p][:, 0, :], source[p][:, :]).then_inc(parts_made, 1)
                        act.wait_ge(rest_made, n * 2 + 1)
                        act.copy(parts[p][:, 1, :], rest[0][:, :]).then_inc(parts_made, 1)
                        act.wait_ge(rest_made, n * 2 + 2)
                        act.copy(parts[p][:, 2, :], rest[1][:, :]).then_inc(parts_made, 1)

                    def body(s, used, p):
                        split(s, used, p)
                        convert(s, used, p)
                    over_sources(act, layer, body)
                    with act.Fori(0, PASSES) as i:
                        n_pass = layer * PASSES + i
                        for q, t, n in halves(i * PASS):
                            act.wait_ge(tile_turned[q], n_pass + PASSES + 1)
                            act.wait_ge(maxima_done, layer + 1)
                            act.copy(stage[q][:, 0:n, :], acc[:, bass.ds(t, n), :]).then_inc(staged[q], 1)
                        for q, t, n in halves(i * PASS):
                            cols = bass.ds(t * P, n * P)
                            act.wait_ge(product_made[q], n_pass + 1)
                            act.wait_ge(new_turned[q], n_pass + 1)
                            act.activation(new_t[q][:, 0:n, :], product[q][:, 0:n, :], ACT.Relu, bias=b_now[:, :])
                            act.activation(h_t[:, cols], product[q][:, 0:n, :].rearrange("p c m -> p (c m)"),
                                           ACT.Relu, bias=b_now[:, :]).then_inc(new_made[q], 1)

            @block.tensor
            def _(pe):
                for q in range(2):
                    pe.sem_inc(tile_turned[q], 1)
                    pe.sem_inc(new_turned[q], 1)
                pe.sem_inc(tile_done, 2)

                def turn_tiles(n_pass, q, n):
                    pe.wait_ge(staged[q], n_pass + 1)
                    pe.wait_ge(tile_copied[q], n_pass + 1)
                    for c in range(n):
                        last = pe.transpose(turned[q][:, c, :], stage[q][:, c, :], ident[:, :])
                    last.then_inc(tile_turned[q], 1)

                with pe.Fori(0, PASSES) as i:
                    for q, t, n in halves(i * PASS):
                        turn_tiles(i, q, n)
                with pe.Fori(0, LAYERS) as layer:
                    def select(s, used, p):
                        n = layer * TILES + s
                        pe.wait_ge(parts_made, n * 3 + 4)
                        pe.wait_ge(choice_loaded[p], used * 16 + 16)
                        for c in range(PARTS):
                            q = c % WIDE
                            pe.wait_ge(part_used, layer * STEPS + s * PARTS + c + 1)
                            turn(pe, turns)
                            for m in range(3):
                                for lo_c, hi_c in ((0, BANK), (BANK, PART)):
                                    last = pe.matmul(wide[q][:, lo_c:hi_c], parts[p][:, m, :],
                                                     choice[p][:, c * PART + lo_c:c * PART + hi_c],
                                                     start=(m == 0), stop=(m == 2))
                            last.then_inc(part_selected, 1)
                        pe.wait_ge(part_selected, layer * STEPS + s * PARTS + PARTS)
                        pe.sem_inc(tile_done, 1)
                    over_sources(pe, layer, select)
                    pe.wait_ge(part_used, layer * STEPS + STEPS + WIDE)
                    pe.wait_ge(weights_set, layer * 3 + 3)
                    turn(pe, turns)
                    with pe.Fori(0, PASSES) as i:
                        n_pass = layer * PASSES + i
                        for q, t, n in halves(i * PASS):
                            turn_tiles(n_pass + PASSES, q, n)
                        for q, t, n in halves(i * PASS):
                            cols = bass.ds(t * P, n * P)
                            pe.wait_ge(tile_copied[q], n_pass + PASSES + 2)
                            pe.wait_ge(new_made[q], n_pass + 1)
                            whole_q = wide[q][:, 0:n * P]
                            pe.matmul(whole_q, w_now[:, :], acc_t[:, cols], start=True, stop=False)
                            pe.matmul(whole_q, r_now[:, :], h_t[:, cols], start=False,
                                      stop=True).then_inc(product_made[q], 1)
                        for q, t, n in halves(i * PASS):
                            pe.wait_ge(new_made[q], n_pass + 2)
                            pe.wait_ge(new_out[q], n_pass + 1)
                            for c in range(n):
                                last = pe.transpose(back[q][:, c, :], new_t[q][:, c, :], ident[:, :])
                            last.then_inc(new_turned[q], 1)

            @block.vector
            def _(dve):
                dve.memset(acc[:, :, :], 0.0).then_inc(v_did, 1)
                dve.wait_ge(v_did, 1)
                dve.sem_inc(group_used, GROUPS[1])
                dve.sem_inc(part_used, WIDE)
                for q in range(2):
                    dve.sem_inc(tile_copied[q], 1)
                    dve.sem_inc(new_out[q], 1)
                dve.wait_ge(w_loaded, (3 + 4 + 6) * 16)
                dve.tensor_copy(w_now[:, :], w[0][:, :]).then_inc(weights_set, 1)
                dve.tensor_copy(r_now[:, :], r[0][:, :]).then_inc(weights_set, 1)
                dve.tensor_copy(b_now[:, :], b[0][:, :]).then_inc(weights_set, 1)
                dve.wait_ge(own_gathered, 2 * TILES * 16)
                with dve.Fori(0, PASSES) as i:
                    for q, t, n in halves(i * PASS):
                        dve.wait_ge(tile_turned[q], i + 1)
                        dve.tensor_copy(stage[q][:, 0:n, :], new[:, bass.ds(t, n), :]).then_inc(staged[q], 1)
                bodies = bodies_of(dve, 1)
                with dve.Fori(0, LAYERS) as layer:
                    base = layer * (bodies * (3 * GROUPS[1]) + 1) + 1

                    class Groups:

                        def __init__(self, j):
                            self.j, self.m, self.best_of = j, 0, {}

                        def did(self, back=0):
                            if self.m or not back:
                                dve.wait_ge(v_did, base + self.j * (3 * GROUPS[1]) + (self.m - back))

                        def pair(self, g):
                            n = layer * bodies + self.j
                            q, place = share_of(1, g)
                            if place == 0:
                                dve.wait_ge(rows_loaded[q], n * 32 + 32)
                                turn(dve, turns)
                            tile = dve.value_load(slot_tiles[q][0:1, place:place + 1], min_val=0, max_val=TILES)
                            self.best_of[g] = acc[:, bass.ds(tile, 1), :].squeeze(1)
                            dve.wait_ge(gathered[g], n * (GROUP * 16) + GROUP * 16)
                            self.did(back=1)
                            dve.tensor_tensor(pairs[:, :, :], rows[g][:, 0:2, :], rows[g][:, 2:4, :],
                                              ALU.max).then_inc(v_did, 1)
                            self.m += 1

                        def join(self, g):
                            self.did()
                            dve.sem_inc(group_used, 1)
                            dve.tensor_tensor(best[:, :], pairs[:, 0, :], pairs[:, 1, :], ALU.max
                                              ).then_inc(v_did, 1)
                            self.m += 1

                        def keep(self, g):
                            self.did()
                            dve.tensor_tensor(self.best_of[g], self.best_of[g], best[:, :], ALU.max
                                              ).then_inc(v_did, 1)
                            self.m += 1

                    def take_parts(s, c, first):
                        n = layer * STEPS + s * PARTS + c
                        part = acc_t[:, c * PART:(c + 1) * PART]
                        dve.wait_ge(part_selected, n + 1)
                        if first:
                            dve.tensor_copy(part, wide[c % WIDE][:, 0:PART]).then_inc(part_used, 1)
                        else:
                            dve.wait_ge(part_used, n - PARTS + WIDE + 1)
                            dve.tensor_tensor(part, part, wide[c % WIDE][:, 0:PART], ALU.max).then_inc(part_used, 1)

                    def split(s, p):
                        n = layer * TILES + s
                        dve.wait_ge(parts_made, n * 3 + 2)
                        dve.tensor_tensor(rest[0][:, :], source[p][:, :], parts[p][:, 0, :],
                                          ALU.subtract).then_inc(rest_made, 1)
                        dve.wait_ge(parts_made, n * 3 + 3)
                        dve.tensor_tensor(rest[1][:, :], rest[0][:, :], parts[p][:, 1, :],
                                          ALU.subtract).then_inc(rest_made, 1)

                    def body(s, next_p, groups=None, first_parts=()):
                        for c in range(PARTS):
                            take_parts(s, c, first=groups is None)
                            if c == 0 and next_p is not None:
                                split(s + 1, next_p)
                            for g, at in first_parts:
                                if c == at + 2:
                                    groups.keep(g)
                            for g, at in first_parts:
                                if c == at + 1:
                                    groups.join(g)
                                if c == at:
                                    groups.pair(g)

                    AT = (((0, 1), (1, 3), (2, 5)), ((3, 1), (4, 4)))
                    assert GROUPS[1] == len(AT[0]) + len(AT[1])

                    def pair_of_tiles(s, j, next_p):
                        groups = Groups(j)
                        body(s, 0, groups, AT[0])
                        body(s + 1, next_p, groups, AT[1])
                    split(0, 0)
                    body(0, 1)
                    with dve.Fori(0, PAIRS - 1) as i:
                        pair_of_tiles(i * 2 + 1, i, 1)
                    pair_of_tiles(TILES - 2, PAIRS - 1, None)
                    with dve.If(bodies > PAIRS):
                        with dve.Fori(PAIRS, bodies) as j:
                            groups = Groups(j)
                            for g in range(GROUPS[1]):
                                groups.pair(g)
                                groups.join(g)
                                groups.keep(g)
                    dve.wait_ge(v_did, base + bodies * (3 * GROUPS[1]))
                    dve.wait_ge(part_used, layer * STEPS + STEPS + WIDE)
                    dve.wait_ge(table_ready, layer + 1)
                    dve.sem_inc(maxima_done, 1)
                    with dve.Fori(0, PASSES) as i:
                        n_pass = layer * PASSES + i
                        for q, t, n in halves(i * PASS):
                            cols = bass.ds(t * P, n * P)
                            dve.wait_ge(tile_turned[q], n_pass + PASSES + 2)
                            dve.tensor_tensor(acc_t[:, cols], acc_t[:, cols],
                                              turned[q][:, 0:n, :].rearrange("p c m -> p (c m)"),
                                              ALU.max).then_inc(tile_copied[q], 1)
                        for q, t, n in halves(i * PASS):
                            dve.wait_ge(new_turned[q], n_pass + 2)
                            turn(dve, turns)
                            with dve.If(layer < LAYERS - 1):
                                dve.tensor_copy(new[:, bass.ds(t, n), :], back[q][:, 0:n, :]
                                                ).then_inc(new_out[q], 1)
                            with dve.Else():
                                dve.tensor_tensor(new[:, bass.ds(t, n), :], back[q][:, 0:n, :],
                                                  own_x1[:, bass.ds(t, n), :], ALU.add).then_inc(new_out[q], 1)
                    for q in range(2):
                        dve.wait_ge(staged[q], layer * PASSES + 2 * PASSES)
                        dve.wait_ge(new_made[q], layer * PASSES + PASSES + 1)
                    dve.memset(acc[:, :, :], 0.0).then_inc(v_did, 1)
                    dve.tensor_copy(w_now[:, :], w[1][:, :]).then_inc(weights_set, 1)
                    dve.tensor_copy(r_now[:, :], r[1][:, :]).then_inc(weights_set, 1)
                    dve.tensor_copy(b_now[:, :], b[1][:, :]).then_inc(weights_set, 1)


_INS = ["x", "src", "dst", "L0_gnn_W1", "L0_gnn_b1", "L0_gnn_W2", "L0_gnn_b2", "L0_gnn_Wl", "L0_gnn_bl",
        "L1_gnn_W1", "L1_gnn_b1", "L1_gnn_R1", "L1_gnn_W2", "L1_gnn_b2", "L1_gnn_R2"]


def kernel(**inputs):
    import concourse.bacc as bacc
    from concourse.bass_utils import run_bass_kernel_spmd

    nc = bacc.Bacc("TRN2", target_bir_lowering=False, num_devices=1)
    arrays, args = {}, []
    for name in _INS:
        a = np.ascontiguousarray(inputs[name])
        arrays[f"in_{name}"] = a
        args.append(nc.dram_tensor(f"in_{name}", a.shape, mybir.dt.from_np(a.dtype), kind="ExternalInput").ap())
    args.append(nc.dram_tensor("out_x", (NODES, D), F32, kind="ExternalOutput").ap())
    gnn(nc, *args)
    return run_bass_kernel_spmd(nc, [arrays], core_ids=[0]).results[0]["out_x"]
```
